# Optimizing a Trainium2 kernel written in Bass

```python
import numpy as np
import jax
import jax.numpy as jnp

def _softmax(x, axis=-1):
    return jax.nn.softmax(x, axis=axis)

def _gelu(x):
    return jax.nn.gelu(x, approximate=True)

def _silu(x):
    return jax.nn.silu(x)

def _sigmoid(x):
    return jax.nn.sigmoid(x)

def _layernorm(x, axis=-1, eps=1e-05):
    m = jnp.mean(x, axis=axis, keepdims=True)
    v = jnp.var(x, axis=axis, keepdims=True)
    return (x - m) / jnp.sqrt(v + eps)

def _scatter_add(tgt, idx, src, axis=0):
    return tgt.at[idx].add(src)

def _segment_sum(src, seg, n):
    return jax.ops.segment_sum(src, seg, n)
kernel_name = 'mk_decoder_postln_d2_seqx_r4_11b72b'

def setup_inputs(seed: int=0):
    np.random.seed(seed)
    _w = jnp.asarray

    def _rec_inputs():
        import jax
        import jax.numpy as jnp
        _rk = jax.random.key(seed)
        x = -0.0002928 + 1 * jax.random.normal(jax.random.fold_in(_rk, 1), (2, 1024, 256), jnp.float32)
        _lenS = 1024 - jax.random.randint(jax.random.fold_in(_rk, 7), (2,), 0, max(1, 1024 // 4) + 1, jnp.int32)
        _lenS2 = 77 - jax.random.randint(jax.random.fold_in(_rk, 8), (2,), 0, max(1, 77 // 4) + 1, jnp.int32)
        _ctx_1024P = jax.random.normal(jax.random.fold_in(_rk, 11), (2, 16, 256), jnp.float32)
        _ctx_1024c = jax.random.dirichlet(jax.random.fold_in(_rk, 511), 0.3 * jnp.ones((16,), jnp.float32), (2, 77))
        _ctx_1024t = jnp.einsum('bsk,bkd->bsd', _ctx_1024c, _ctx_1024P)
        _ctx_1024t = _ctx_1024t * jax.lax.rsqrt(jnp.mean(jnp.square(_ctx_1024t)) + 1e-12) * 0.953939
        ctx_1024 = -1.39393e-06 + 0.999914 * (_ctx_1024t + 0.3 * jax.random.normal(jax.random.fold_in(_rk, 611), (2, 77, 256), jnp.float32))
        return (x, ctx_1024)
    x, ctx_1024 = _rec_inputs()

    def _L0_attn_setup():
        import jax, jax.numpy as jnp
        import numpy as np
        D_MODEL = 256
        H = 16
        DH = 64
        EPS = 1e-05

        def _layernorm(x, g, b):
            mu = jnp.mean(x, axis=-1, keepdims=True)
            var = jnp.var(x, axis=-1, keepdims=True)
            return (x - mu) * jax.lax.rsqrt(var + EPS) * g + b
        key = jax.random.key(seed)
        ks = jax.random.split(key, 16)
        B, L = (4, 1024)
        s = 0.02
        inp = {'x': jax.random.normal(ks[0], (B, L, D_MODEL), jnp.float32), 'ln1_g': jnp.ones((D_MODEL,), jnp.float32), 'ln1_b': jnp.zeros((D_MODEL,), jnp.float32), 'Wq': jax.random.normal(ks[1], (D_MODEL, H * DH), jnp.float32) * s, 'bq': jnp.zeros((H * DH,), jnp.float32), 'Wk': jax.random.normal(ks[2], (D_MODEL, H * DH), jnp.float32) * s, 'bk': jnp.zeros((H * DH,), jnp.float32), 'Wv': jax.random.normal(ks[3], (D_MODEL, H * DH), jnp.float32) * s, 'bv': jnp.zeros((H * DH,), jnp.float32), 'Wg': jax.random.normal(ks[4], (D_MODEL, H * DH), jnp.float32) * s, 'bg': jnp.zeros((H * DH,), jnp.float32), 'decay_logit': jnp.zeros((H,), jnp.float32), 'Wo': jax.random.normal(ks[5], (H * DH, D_MODEL), jnp.float32) * s, 'bo': jnp.zeros((D_MODEL,), jnp.float32), 'ln2_g': jnp.ones((D_MODEL,), jnp.float32), 'ln2_b': jnp.zeros((D_MODEL,), jnp.float32), 'W1': jax.random.normal(ks[6], (D_MODEL, 4 * D_MODEL), jnp.float32) * s, 'b1': jnp.zeros((4 * D_MODEL,), jnp.float32), 'W2': jax.random.normal(ks[7], (4 * D_MODEL, D_MODEL), jnp.float32) * s, 'b2': jnp.zeros((D_MODEL,), jnp.float32)}
        return inp
    _L0_attn_all = _L0_attn_setup()
    _L0_attn_in = {k: v for k, v in _L0_attn_all.items() if k in ('ln1_g', 'ln1_b', 'Wq', 'bq', 'Wk', 'bk', 'Wv', 'bv', 'Wg', 'bg', 'decay_logit', 'Wo', 'bo', 'ln2_g', 'ln2_b', 'W1', 'b1', 'W2', 'b2')}
    del _L0_attn_all

    def _L0_xattn_setup():
        import jax, jax.numpy as jnp
        import numpy as np
        EMBED_DIM = 256
        NUM_HEADS = 16
        DIM_K = EMBED_DIM // NUM_HEADS
        B, S = (2, 512)
        key = jax.random.key(seed)
        ks = jax.random.split(key, 7)
        scale = 1.0 / np.sqrt(EMBED_DIM)
        return {'query': jax.random.normal(ks[0], (B, S, EMBED_DIM), dtype=jnp.float32), 'key': jax.random.normal(ks[1], (B, S, EMBED_DIM), dtype=jnp.float32), 'value': jax.random.normal(ks[2], (B, S, EMBED_DIM), dtype=jnp.float32), 'Wq': jax.random.normal(ks[3], (EMBED_DIM, EMBED_DIM), dtype=jnp.float32) * scale, 'Wk': jax.random.normal(ks[4], (EMBED_DIM, EMBED_DIM), dtype=jnp.float32) * scale, 'Wv': jax.random.normal(ks[5], (EMBED_DIM, EMBED_DIM), dtype=jnp.float32) * scale, 'Wo': jax.random.normal(ks[6], (EMBED_DIM, EMBED_DIM), dtype=jnp.float32) * scale}
    _L0_xattn_all = _L0_xattn_setup()
    _L0_xattn_in = {k: v for k, v in _L0_xattn_all.items() if k in ('Wq', 'Wk', 'Wv', 'Wo')}
    del _L0_xattn_all

    def _L0_ffn_setup():
        import jax, jax.numpy as jnp
        import numpy as np
        B, S, H, I, E = (2, 1024, 256, 128, 8)
        key = jax.random.key(seed)
        ks = jax.random.split(key, 5)
        scale_h = 1.0 / np.sqrt(H)
        scale_i = 1.0 / np.sqrt(I)
        return {'hidden_states': jax.random.normal(ks[0], (B, S, H), dtype=jnp.float32), 'gate_w': jax.random.normal(ks[1], (E, H), dtype=jnp.float32) * scale_h, 'w_gate': jax.random.normal(ks[2], (E, I, H), dtype=jnp.float32) * scale_h, 'w_up': jax.random.normal(ks[3], (E, I, H), dtype=jnp.float32) * scale_h, 'w_down': jax.random.normal(ks[4], (E, H, I), dtype=jnp.float32) * scale_i}
    _L0_ffn_all = _L0_ffn_setup()
    _L0_ffn_in = {k: v for k, v in _L0_ffn_all.items() if k in ('gate_w', 'w_gate', 'w_up', 'w_down')}
    del _L0_ffn_all

    def _L1_attn_setup():
        import jax, jax.numpy as jnp
        import numpy as np
        import math
        D_MODEL = 256
        D_STATE = 16
        D_CONV = 4
        EXPAND = 2
        D_INNER = EXPAND * D_MODEL
        DT_RANK = max(1, D_MODEL // 16)

        def _selective_scan(u, delta, A, B_ssm, C_ssm, D_param):

            def step(h, inp):
                u_t, d_t, b_t, c_t = inp
                dA = jnp.exp(d_t[..., None] * A)
                h = dA * h + (d_t * u_t)[..., None] * b_t[:, None, :]
                y = jnp.einsum('bdn,bn->bd', h, c_t)
                return (h, y)
            Bsz = u.shape[0]
            h0 = jnp.zeros((Bsz, u.shape[2], A.shape[1]), dtype=u.dtype)
            xs = (jnp.swapaxes(u, 0, 1), jnp.swapaxes(delta, 0, 1), jnp.swapaxes(B_ssm, 0, 1), jnp.swapaxes(C_ssm, 0, 1))
            _, ys = jax.lax.scan(step, h0, xs)
            y = jnp.swapaxes(ys, 0, 1)
            return y + u * D_param
        key = jax.random.key(seed)
        ks = jax.random.split(key, 10)
        B, L = (4, 512)
        x = jax.random.normal(ks[0], (B, L, D_MODEL), dtype=jnp.float32)
        in_proj_w = jax.random.normal(ks[1], (2 * D_INNER, D_MODEL), dtype=jnp.float32) * (1.0 / math.sqrt(D_MODEL))
        conv_w = jax.random.normal(ks[2], (D_INNER, 1, D_CONV), dtype=jnp.float32) * (1.0 / math.sqrt(D_CONV))
        conv_b = jax.random.normal(ks[3], (D_INNER,), dtype=jnp.float32) * 0.1
        x_proj_w = jax.random.normal(ks[4], (DT_RANK + 2 * D_STATE, D_INNER), dtype=jnp.float32) * (1.0 / math.sqrt(D_INNER))
        dt_proj_w = jax.random.normal(ks[5], (D_INNER, DT_RANK), dtype=jnp.float32) * (1.0 / math.sqrt(DT_RANK))
        dt = jnp.exp(jax.random.uniform(ks[6], (D_INNER,)) * (math.log(0.1) - math.log(0.001)) + math.log(0.001))
        dt = jnp.clip(dt, 0.0001, None)
        dt_proj_b = dt + jnp.log(-jnp.expm1(-dt))
        A_log = jnp.log(jnp.broadcast_to(jnp.arange(1, D_STATE + 1, dtype=jnp.float32)[None, :], (D_INNER, D_STATE)))
        D_param = jnp.ones((D_INNER,), dtype=jnp.float32)
        out_proj_w = jax.random.normal(ks[7], (D_MODEL, D_INNER), dtype=jnp.float32) * (1.0 / math.sqrt(D_INNER))
        return {'x': x, 'in_proj_w': in_proj_w, 'conv_w': conv_w, 'conv_b': conv_b, 'x_proj_w': x_proj_w, 'dt_proj_w': dt_proj_w, 'dt_proj_b': dt_proj_b, 'A_log': A_log, 'D_param': D_param, 'out_proj_w': out_proj_w}
    _L1_attn_all = _L1_attn_setup()
    _L1_attn_in = {k: v for k, v in _L1_attn_all.items() if k in ('in_proj_w', 'conv_w', 'conv_b', 'x_proj_w', 'dt_proj_w', 'dt_proj_b', 'A_log', 'D_param', 'out_proj_w')}
    del _L1_attn_all

    def _L1_xattn_setup():
        import jax, jax.numpy as jnp
        import numpy as np
        DIM = 256
        HEADS = 16
        HEAD_DIM = DIM // HEADS
        SCALE = HEAD_DIM ** (-0.5)
        B, N, S = (2, 512, 512)

        def _slice_head(x, W_qkv, b_qkv, idx):
            b, l, _ = x.shape
            qkv = (x @ W_qkv + b_qkv).reshape(b, l, 3, HEADS, HEAD_DIM)
            return jnp.transpose(qkv[:, :, idx], (0, 2, 1, 3))
        key = jax.random.key(seed)
        ks = jax.random.split(key, 5)
        return {'query': jax.random.normal(ks[0], (B, N, DIM), dtype=jnp.float32), 'key': jax.random.normal(ks[1], (B, S, DIM), dtype=jnp.float32), 'value': jax.random.normal(ks[2], (B, S, DIM), dtype=jnp.float32), 'W_qkv': jax.random.normal(ks[3], (DIM, 3 * DIM), dtype=jnp.float32) * DIM ** (-0.5), 'b_qkv': jnp.zeros((3 * DIM,), dtype=jnp.float32), 'W_out': jax.random.normal(ks[4], (DIM, DIM), dtype=jnp.float32) * DIM ** (-0.5), 'b_out': jnp.zeros((DIM,), dtype=jnp.float32)}
    _L1_xattn_all = _L1_xattn_setup()
    _L1_xattn_in = {k: v for k, v in _L1_xattn_all.items() if k in ('W_qkv', 'b_qkv', 'W_out', 'b_out')}
    del _L1_xattn_all

    def _L1_ffn_setup():
        import jax, jax.numpy as jnp
        import numpy as np
        D_IN, D_HID = (256, 1024)

        def _ternary(key, shape):
            return jax.random.randint(key, shape, -1, 2).astype(jnp.float32)

        def _tlin(x, w, s):
            return jnp.einsum('bsi,oi->bso', x, w) * s
        key = jax.random.key(seed)
        ks = jax.random.split(key, 12)
        inv = lambda fan: 1.0 / np.sqrt(fan).astype(np.float32)
        return {'x': jax.random.normal(ks[0], (4, 512, D_IN), dtype=jnp.float32), 'w1_w': _ternary(ks[1], (D_HID, D_IN)), 'w1_s': jax.random.uniform(ks[2], (D_HID,), dtype=jnp.float32) * inv(D_IN), 'w2_w': _ternary(ks[3], (D_HID, D_IN)), 'w2_s': jax.random.uniform(ks[4], (D_HID,), dtype=jnp.float32) * inv(D_IN), 'h1_w': _ternary(ks[5], (D_HID, D_HID)), 'h1_s': jax.random.uniform(ks[6], (D_HID,), dtype=jnp.float32) * inv(D_HID), 'h2_w': _ternary(ks[7], (D_HID, D_HID)), 'h2_s': jax.random.uniform(ks[8], (D_HID,), dtype=jnp.float32) * inv(D_HID), 'w3_w': _ternary(ks[9], (D_IN, D_HID)), 'w3_s': jax.random.uniform(ks[10], (D_IN,), dtype=jnp.float32) * inv(D_HID)}
    _L1_ffn_all = _L1_ffn_setup()
    _L1_ffn_in = {k: v for k, v in _L1_ffn_all.items() if k in ('w1_w', 'w1_s', 'w2_w', 'w2_s', 'h1_w', 'h1_s', 'h2_w', 'h2_s', 'w3_w', 'w3_s')}
    del _L1_ffn_all
    return {'x': x, 'ctx_1024': ctx_1024, 'L0_attn_ln1_g': _L0_attn_in['ln1_g'], 'L0_attn_ln1_b': _L0_attn_in['ln1_b'], 'L0_attn_Wq': _L0_attn_in['Wq'], 'L0_attn_bq': _L0_attn_in['bq'], 'L0_attn_Wk': _L0_attn_in['Wk'], 'L0_attn_bk': _L0_attn_in['bk'], 'L0_attn_Wv': _L0_attn_in['Wv'], 'L0_attn_bv': _L0_attn_in['bv'], 'L0_attn_Wg': _L0_attn_in['Wg'], 'L0_attn_bg': _L0_attn_in['bg'], 'L0_attn_decay_logit': _L0_attn_in['decay_logit'], 'L0_attn_Wo': _L0_attn_in['Wo'], 'L0_attn_bo': _L0_attn_in['bo'], 'L0_attn_ln2_g': _L0_attn_in['ln2_g'], 'L0_attn_ln2_b': _L0_attn_in['ln2_b'], 'L0_attn_W1': _L0_attn_in['W1'], 'L0_attn_b1': _L0_attn_in['b1'], 'L0_attn_W2': _L0_attn_in['W2'], 'L0_attn_b2': _L0_attn_in['b2'], 'L0_xattn_Wq': _L0_xattn_in['Wq'], 'L0_xattn_Wk': _L0_xattn_in['Wk'], 'L0_xattn_Wv': _L0_xattn_in['Wv'], 'L0_xattn_Wo': _L0_xattn_in['Wo'], 'L0_ffn_gate_w': _L0_ffn_in['gate_w'], 'L0_ffn_w_gate': _L0_ffn_in['w_gate'], 'L0_ffn_w_up': _L0_ffn_in['w_up'], 'L0_ffn_w_down': _L0_ffn_in['w_down'], 'L1_attn_in_proj_w': _L1_attn_in['in_proj_w'], 'L1_attn_conv_w': _L1_attn_in['conv_w'], 'L1_attn_conv_b': _L1_attn_in['conv_b'], 'L1_attn_x_proj_w': _L1_attn_in['x_proj_w'], 'L1_attn_dt_proj_w': _L1_attn_in['dt_proj_w'], 'L1_attn_dt_proj_b': _L1_attn_in['dt_proj_b'], 'L1_attn_A_log': _L1_attn_in['A_log'], 'L1_attn_D_param': _L1_attn_in['D_param'], 'L1_attn_out_proj_w': _L1_attn_in['out_proj_w'], 'L1_xattn_W_qkv': _L1_xattn_in['W_qkv'], 'L1_xattn_b_qkv': _L1_xattn_in['b_qkv'], 'L1_xattn_W_out': _L1_xattn_in['W_out'], 'L1_xattn_b_out': _L1_xattn_in['b_out'], 'L1_ffn_w1_w': _L1_ffn_in['w1_w'], 'L1_ffn_w1_s': _L1_ffn_in['w1_s'], 'L1_ffn_w2_w': _L1_ffn_in['w2_w'], 'L1_ffn_w2_s': _L1_ffn_in['w2_s'], 'L1_ffn_h1_w': _L1_ffn_in['h1_w'], 'L1_ffn_h1_s': _L1_ffn_in['h1_s'], 'L1_ffn_h2_w': _L1_ffn_in['h2_w'], 'L1_ffn_h2_s': _L1_ffn_in['h2_s'], 'L1_ffn_w3_w': _L1_ffn_in['w3_w'], 'L1_ffn_w3_s': _L1_ffn_in['w3_s']}

def reference(x, ctx_1024, L0_attn_ln1_g, L0_attn_ln1_b, L0_attn_Wq, L0_attn_bq, L0_attn_Wk, L0_attn_bk, L0_attn_Wv, L0_attn_bv, L0_attn_Wg, L0_attn_bg, L0_attn_decay_logit, L0_attn_Wo, L0_attn_bo, L0_attn_ln2_g, L0_attn_ln2_b, L0_attn_W1, L0_attn_b1, L0_attn_W2, L0_attn_b2, L0_xattn_Wq, L0_xattn_Wk, L0_xattn_Wv, L0_xattn_Wo, L0_ffn_gate_w, L0_ffn_w_gate, L0_ffn_w_up, L0_ffn_w_down, L1_attn_in_proj_w, L1_attn_conv_w, L1_attn_conv_b, L1_attn_x_proj_w, L1_attn_dt_proj_w, L1_attn_dt_proj_b, L1_attn_A_log, L1_attn_D_param, L1_attn_out_proj_w, L1_xattn_W_qkv, L1_xattn_b_qkv, L1_xattn_W_out, L1_xattn_b_out, L1_ffn_w1_w, L1_ffn_w1_s, L1_ffn_w2_w, L1_ffn_w2_s, L1_ffn_h1_w, L1_ffn_h1_s, L1_ffn_h2_w, L1_ffn_h2_s, L1_ffn_w3_w, L1_ffn_w3_s):
    import jax
    import jax.numpy as jnp

    def _L0_attn_ref(x, ln1_g, ln1_b, Wq, bq, Wk, bk, Wv, bv, Wg, bg, decay_logit, Wo, bo, ln2_g, ln2_b, W1, b1, W2, b2):
        import jax, jax.numpy as jnp
        import numpy as np
        D_MODEL = 256
        H = 16
        DH = 64
        EPS = 1e-05

        def _layernorm(x, g, b):
            mu = jnp.mean(x, axis=-1, keepdims=True)
            var = jnp.var(x, axis=-1, keepdims=True)
            return (x - mu) * jax.lax.rsqrt(var + EPS) * g + b
        B, L, _ = x.shape
        y = _layernorm(x, ln1_g, ln1_b)

        def proj(W, b):
            return (y @ W + b).reshape(B, L, H, DH).transpose(1, 0, 2, 3)
        q = proj(Wq, bq)
        k = proj(Wk, bk)
        v = proj(Wv, bv)
        g = jax.nn.sigmoid(y @ Wg + bg).reshape(B, L, H, DH).transpose(1, 0, 2, 3)
        decay = jax.nn.sigmoid(decay_logit)[None, :, None]
        scale = DH ** (-0.5)

        def step(state, qkvg):
            q_t, k_t, v_t, g_t = qkvg
            state = decay * state + k_t * v_t
            out_t = g_t * q_t * state * scale
            return (state, out_t)
        state0 = jnp.zeros((B, H, DH), x.dtype)
        _, outs = jax.lax.scan(step, state0, (q, k, v, g))
        o = outs.transpose(1, 0, 2, 3).reshape(B, L, H * DH) @ Wo + bo
        x2 = x + o
        h = _layernorm(x2, ln2_g, ln2_b)
        ff = jax.nn.gelu(h @ W1 + b1, approximate=False) @ W2 + b2
        return x2 + ff

    def _L0_xattn_ref(query, key, value, Wq, Wk, Wv, Wo):
        import jax, jax.numpy as jnp
        import numpy as np
        EMBED_DIM = 256
        NUM_HEADS = 16
        DIM_K = EMBED_DIM // NUM_HEADS
        B, S = (2, 512)
        b, s, e = query.shape

        def proj(x, W):
            y = x @ W.T
            return y.reshape(b, -1, NUM_HEADS, DIM_K).transpose(0, 2, 1, 3)
        q = proj(query, Wq)
        k = proj(key, Wk)
        v = proj(value, Wv)
        scores = jnp.einsum('bhqd,bhkd->bhqk', q, k) / jnp.sqrt(jnp.float32(DIM_K))
        attn = jax.nn.softmax(scores, axis=-1)
        x = jnp.einsum('bhqk,bhkd->bhqd', attn, v)
        x = x.transpose(0, 2, 1, 3).reshape(b, -1, e)
        return x @ Wo.T

    def _L0_ffn_ref(hidden_states, gate_w, w_gate, w_up, w_down):
        import jax, jax.numpy as jnp
        import numpy as np
        B, S, H, I, E = (2, 1024, 256, 128, 8)
        b, s, h = hidden_states.shape
        x = hidden_states.reshape(-1, h)
        logits = x @ gate_w.T
        top_v = jnp.max(logits, axis=-1)
        sel = jnp.argmax(logits, axis=-1)
        rw = jax.nn.sigmoid(top_v)
        out = jnp.zeros_like(x)
        n_exp = gate_w.shape[0]
        for e in range(n_exp):
            mask = (sel == e).astype(x.dtype)
            xs = x * (rw * mask)[:, None]
            g = xs @ w_gate[e].T
            u = xs @ w_up[e].T
            out = out + u * jax.nn.silu(g) @ w_down[e].T
        return out.reshape(b, s, h)

    def _L1_attn_ref(x, in_proj_w, conv_w, conv_b, x_proj_w, dt_proj_w, dt_proj_b, A_log, D_param, out_proj_w):
        import jax, jax.numpy as jnp
        import numpy as np
        import math
        D_MODEL = 256
        D_STATE = 16
        D_CONV = 4
        EXPAND = 2
        D_INNER = EXPAND * D_MODEL
        DT_RANK = max(1, D_MODEL // 16)

        def _selective_scan(u, delta, A, B_ssm, C_ssm, D_param):

            def step(h, inp):
                u_t, d_t, b_t, c_t = inp
                dA = jnp.exp(d_t[..., None] * A)
                h = dA * h + (d_t * u_t)[..., None] * b_t[:, None, :]
                y = jnp.einsum('bdn,bn->bd', h, c_t)
                return (h, y)
            Bsz = u.shape[0]
            h0 = jnp.zeros((Bsz, u.shape[2], A.shape[1]), dtype=u.dtype)
            xs = (jnp.swapaxes(u, 0, 1), jnp.swapaxes(delta, 0, 1), jnp.swapaxes(B_ssm, 0, 1), jnp.swapaxes(C_ssm, 0, 1))
            _, ys = jax.lax.scan(step, h0, xs)
            y = jnp.swapaxes(ys, 0, 1)
            return y + u * D_param
        B, L, _ = x.shape
        xz = x @ in_proj_w.T
        x_branch, z_branch = jnp.split(xz, 2, axis=-1)
        xc = jnp.swapaxes(x_branch, 1, 2)
        xc = jax.lax.conv_general_dilated(xc, conv_w, window_strides=(1,), padding=[(D_CONV - 1, 0)], dimension_numbers=('NCH', 'OIH', 'NCH'), feature_group_count=D_INNER)
        xc = xc + conv_b[None, :, None]
        x_conv = jax.nn.silu(jnp.swapaxes(xc, 1, 2))
        x_dbl = x_conv @ x_proj_w.T
        dt_lr, B_ssm, C_ssm = jnp.split(x_dbl, [DT_RANK, DT_RANK + D_STATE], axis=-1)
        dt = jax.nn.softplus(dt_lr @ dt_proj_w.T + dt_proj_b)
        A = -jnp.exp(A_log)
        y = _selective_scan(x_conv, dt, A, B_ssm, C_ssm, D_param)
        y = y * jax.nn.silu(z_branch)
        return y @ out_proj_w.T

    def _L1_xattn_ref(query, key, value, W_qkv, b_qkv, W_out, b_out):
        import jax, jax.numpy as jnp
        import numpy as np
        DIM = 256
        HEADS = 16
        HEAD_DIM = DIM // HEADS
        SCALE = HEAD_DIM ** (-0.5)
        B, N, S = (2, 512, 512)

        def _slice_head(x, W_qkv, b_qkv, idx):
            b, l, _ = x.shape
            qkv = (x @ W_qkv + b_qkv).reshape(b, l, 3, HEADS, HEAD_DIM)
            return jnp.transpose(qkv[:, :, idx], (0, 2, 1, 3))
        q = _slice_head(query, W_qkv, b_qkv, 0)
        k = _slice_head(key, W_qkv, b_qkv, 1)
        v = _slice_head(value, W_qkv, b_qkv, 2)
        attn = jnp.einsum('bhnd,bhsd->bhns', q, k) * SCALE
        attn = jax.nn.softmax(attn, axis=-1)
        out = jnp.einsum('bhns,bhsd->bhnd', attn, v)
        out = jnp.transpose(out, (0, 2, 1, 3)).reshape(query.shape[0], query.shape[1], DIM)
        return out @ W_out + b_out

    def _L1_ffn_ref(x, w1_w, w1_s, w2_w, w2_s, h1_w, h1_s, h2_w, h2_s, w3_w, w3_s):
        import jax, jax.numpy as jnp
        import numpy as np
        D_IN, D_HID = (256, 1024)

        def _ternary(key, shape):
            return jax.random.randint(key, shape, -1, 2).astype(jnp.float32)

        def _tlin(x, w, s):
            return jnp.einsum('bsi,oi->bso', x, w) * s
        h = jax.nn.silu(_tlin(x, w1_w, w1_s)) * _tlin(x, w2_w, w2_s)
        h = jax.nn.gelu(_tlin(h, h1_w, h1_s), approximate=False)
        h = jax.nn.gelu(_tlin(h, h2_w, h2_s), approximate=False)
        return _tlin(h, w3_w, w3_s)
    x = _layernorm(x + _L0_attn_ref(x, L0_attn_ln1_g, L0_attn_ln1_b, L0_attn_Wq, L0_attn_bq, L0_attn_Wk, L0_attn_bk, L0_attn_Wv, L0_attn_bv, L0_attn_Wg, L0_attn_bg, L0_attn_decay_logit, L0_attn_Wo, L0_attn_bo, L0_attn_ln2_g, L0_attn_ln2_b, L0_attn_W1, L0_attn_b1, L0_attn_W2, L0_attn_b2), axis=-1)
    x = _layernorm(x + _L0_xattn_ref(x, ctx_1024, ctx_1024, L0_xattn_Wq, L0_xattn_Wk, L0_xattn_Wv, L0_xattn_Wo), axis=-1)
    x = _layernorm(x + _L0_ffn_ref(x, L0_ffn_gate_w, L0_ffn_w_gate, L0_ffn_w_up, L0_ffn_w_down), axis=-1)
    x = _layernorm(x + _L1_attn_ref(x, L1_attn_in_proj_w, L1_attn_conv_w, L1_attn_conv_b, L1_attn_x_proj_w, L1_attn_dt_proj_w, L1_attn_dt_proj_b, L1_attn_A_log, L1_attn_D_param, L1_attn_out_proj_w), axis=-1)
    x = _layernorm(x + _L1_xattn_ref(x, ctx_1024, ctx_1024, L1_xattn_W_qkv, L1_xattn_b_qkv, L1_xattn_W_out, L1_xattn_b_out), axis=-1)
    x = _layernorm(x + _L1_ffn_ref(x, L1_ffn_w1_w, L1_ffn_w1_s, L1_ffn_w2_w, L1_ffn_w2_s, L1_ffn_h1_w, L1_ffn_h1_s, L1_ffn_h2_w, L1_ffn_h2_s, L1_ffn_w3_w, L1_ffn_w3_s), axis=-1)
    return x

_drawn_inputs = setup_inputs


def setup_inputs(seed=0):
    import zlib

    import numpy as np

    out = dict(_drawn_inputs(seed))
    spreads = {'L0_attn_ln1_g': (1.0, 0.6),
     'L0_attn_ln1_b': (0.0, 0.8),
     'L0_attn_bq': (0.0, 0.8),
     'L0_attn_bk': (0.0, 0.8),
     'L0_attn_bv': (0.0, 0.8),
     'L0_attn_bg': (0.0, 0.8),
     'L0_attn_decay_logit': (0.0, 0.8),
     'L0_attn_bo': (0.0, 0.1),
     'L0_attn_ln2_g': (1.0, 0.6),
     'L0_attn_ln2_b': (0.0, 1.535),
     'L0_attn_b1': (0.0, 0.499),
     'L0_attn_b2': (0.0, 0.1),
     'L1_attn_D_param': (1.0, 0.2),
     'L1_xattn_b_qkv': (0.0, 0.1),
     'L1_xattn_b_out': (0.0, 0.1)}
    factors = {'L0_attn_Wq': 5.615,
     'L0_attn_Wk': 7.298,
     'L0_attn_Wv': 6.887,
     'L0_attn_Wg': 8.0,
     'L0_attn_Wo': 4.842,
     'L1_ffn_w1_w': 8.0,
     'L1_ffn_w1_s': 8.0,
     'L1_ffn_w2_w': 8.0,
     'L1_ffn_w2_s': 8.0,
     'L1_ffn_h1_w': 8.0,
     'L1_ffn_h1_s': 8.0,
     'L1_ffn_h2_w': 8.0,
     'L1_ffn_h2_s': 8.0,
     'L1_ffn_w3_w': 8.0,
     'L1_ffn_w3_s': 8.0}
    for name, (base, spread) in spreads.items():
        noise = np.random.default_rng([zlib.crc32(name.encode()), seed]).standard_normal(out[name].shape)
        drawn = base * np.exp(spread * noise) if base else spread * noise
        out[name] = jnp.asarray(drawn.astype(out[name].dtype))
    for name, factor in factors.items():
        out[name] = (out[name] * factor).astype(out[name].dtype)
    return out
```

```python
from contextlib import ExitStack

import concourse.bass as bass
from concourse import mybir

F32 = mybir.dt.float32
F32R = mybir.dt.float32r
ACT = mybir.ActivationFunctionType
ALU = mybir.AluOpType
AX = mybir.AxisListType.X

P = 128
D = 256
KD = D // P
BATCH, SEQ = 2, 1024
TOK = BATCH * SEQ
CH = 512
NCH = TOK // CH
CPB = SEQ // CH
TT = CH // P
HID = 1024
KH = HID // P
NE = 8
KEYS = 77
HEADS, DH = 16, 16
HPT = P // DH
ROWS = HPT * KEYS
BLK = [P, P, P, P, ROWS - 4 * P]
HPB = 4
INNER, NST, DTR, TAPS = 512, 16, 16, 4
KI = INNER // P
XDB = DTR + 2 * NST
LO = 64
EPS = 1e-5
ENGINES = 5


class Signal:

    def __init__(self, sem, per):
        self.sem, self.per, self.seen = sem, per, 0

    def by(self, instruction):
        self.seen += 1
        instruction.then_inc(self.sem, 1)

    def wait(self, eng, it, k):
        assert 1 <= k <= self.per, (self.sem, k)
        eng.wait_ge(self.sem, it * self.per + k)


class Ring:

    def __init__(self, plan, psum, full, freed):
        self.psum, self.full, self.freed = psum, full, freed
        self.slots, self.where = [], {}
        for name, reader, n in plan:
            self.where[name] = len(self.slots)
            self.slots += [reader] * n
        self.given = {"act": 0, "dve": 0}
        full.per = sum(r is not None for r in self.slots)
        for r in freed:
            freed[r].per = self.slots.count(r)

    def bank(self, name, n=1):
        b = self.where[name] % 8
        return self.psum[:, b, :] if n == 1 else self.psum[:, b:b + n, :]

    def acquire(self, pe, it, name, n=1):
        for r in ("act", "dve"):
            old = [s - 8 for s in range(self.where[name], self.where[name] + n) if s >= 8 and self.slots[s - 8] == r]
            if old:
                self.freed[r].wait(pe, it, self.slots[:old[-1] + 1].count(r))
        return self.bank(name, n)

    def filled(self, eng, it, name, n=1):
        s = self.where[name] + n - 1
        self.full.wait(eng, it, sum(r is not None for r in self.slots[:s + 1]))
        return self.bank(name, n)

    def free(self, instruction, name, last=0):
        s = self.where[name] + last
        r = self.slots[s]
        assert self.slots[:s].count(r) == self.given[r], (name, self.given)
        self.given[r] += 1
        self.freed[r].by(instruction)


def decoder(nc, t, mid, kz_dram, vz_dram, out):
    top = ExitStack()
    with top:
        def alloc(stack, name, shape, dt=F32):
            return stack.enter_context(nc.sbuf_tensor(name, shape, dt))

        def sem(name):
            return top.enter_context(nc.semaphore(name))

        def sig(name, per):
            return Signal(sem(name), per)

        ident = alloc(top, "ident", [P, P])
        head_mask = alloc(top, "head_mask", [P, HPT])
        row_mask = alloc(top, "row_mask", [P, 5, P])
        first_key = alloc(top, "first_key", [P, NE])
        half_neg = alloc(top, "half_neg", [P, TT])
        sel_bc = alloc(top, "sel_bc", [P, 2 * NST], F32R)
        keep = alloc(top, "keep", [P, NCH])
        x_in = alloc(top, "x_in", [P, TT, D])
        x_a = alloc(top, "x_a", [P, TT, D])
        x_b = alloc(top, "x_b", [P, TT, D])
        x_r = alloc(top, "x_r", [P, TT, D])
        xT = alloc(top, "xT", [P, KD, CH])
        kz = alloc(top, "kz", [P, KD, HPT, KEYS])
        vz = alloc(top, "vz", [P, KD, 5, P])
        qT = alloc(top, "qT", [P, KD, CH])
        oaT = alloc(top, "oaT", [P, KD, CH])
        mx = alloc(top, "mx", [P, 2, HEADS])
        rs = alloc(top, "rs", [P, 2, HEADS])
        stats = alloc(top, "stats", [P, TT, 6])
        mv = alloc(top, "mv", [P, TT, 2])
        ve = alloc(top, "ve", [P, TT])
        rstd = alloc(top, "rstd", [P, TT])
        psum = top.enter_context(nc.psum_tensor("psum", [P, 8, CH], F32))

        s_const = sem("constants_made")
        s_setup = sem("setup_on_dve")

        def load(eng, dst, src, s):
            eng.dma_start(dst, src).then_inc(s, 16)

        class Pass:

            def __init__(self, tag, plan, per, scr_p, scr_pt):
                self.tag = tag
                self.s = {n: sig(f"{tag}_{n}", k) for n, k in per.items()}
                full = sig(f"{tag}_banks_full", 0)
                freed = {"act": sig(f"{tag}_act_freed", 0), "dve": sig(f"{tag}_dve_freed", 0)}
                self.ring = Ring(plan, psum, full, freed)
                self.end = sem(f"{tag}_iteration_done")
                self.chunk_in = sem(f"{tag}_chunk_loaded")
                self.stored = sem(f"{tag}_chunk_stored")
                self.p, self.pt = scr_p, scr_pt

            def iteration_end(self, eng, it):
                eng.drain().then_inc(self.end, 1)
                eng.wait_ge(self.end, it * ENGINES + ENGINES + 1)

            def check(self):
                bad = [(n, s.seen, s.per) for n, s in [*self.s.items(), ("full", self.ring.full), *self.ring.freed.items()]
                       if s.seen != s.per]
                assert not bad, bad

            def ln_dve(self, dve, it, k, src, dst):
                for i in range(TT):
                    dve.bn_stats(stats[:, i, :], src[:, i, :])
                dve.drain()
                for i in range(TT):
                    dve.bn_aggr(mv[:, i, :], stats[:, i, :])
                dve.drain()
                self.s["var"].by(dve.tensor_scalar(ve[:, :], mv[:, :, 1], EPS, None, op0=ALU.add))
                self.s["rstd"].wait(dve, it, k)
                for i in range(TT):
                    self.s["xn"].by(dve.tensor_scalar(dst[:, i, :], src[:, i, :], mv[:, i, 0:1], rstd[:, i:i + 1],
                                                      op0=ALU.subtract, op1=ALU.mult))

            def ln_pool(self, pool, it, k):
                self.s["var"].wait(pool, it, k)
                self.s["rstd"].by(pool.tensor_tensor(out=rstd[:, :], in0=ve[:, :], in1=half_neg[:, :], op=ALU.pow))

            def residual_ln(self, dve, it, name, resid, k, dst):
                for h in range(2):
                    ps = self.ring.filled(dve, it, f"{name}{h}")
                    self.ring.free(dve.tensor_tensor(x_r[:, 2 * h:2 * h + 2, :], ps.rearrange("p (t d) -> p t d", t=2),
                                                     resid[:, 2 * h:2 * h + 2, :], ALU.add), f"{name}{h}")
                dve.drain()
                self.ln_dve(dve, it, k, x_r, dst)

            def transpose_pe(self, pe, it, name, src, k):
                if k:
                    self.s["xn"].wait(pe, it, TT * k)
                for kd in range(KD):
                    ps = self.ring.acquire(pe, it, f"{name}{kd}")
                    for i in range(TT):
                        last = pe.transpose(ps[:, i * P:(i + 1) * P], src[:, i, kd * P:(kd + 1) * P], ident[:, :])
                    self.ring.full.by(last)

            def transpose_act(self, act, it, name, gain=None, bias=None):
                for kd in range(KD):
                    ps = self.ring.filled(act, it, f"{name}{kd}")
                    if gain is None:
                        ins = act.activation(xT[:, kd, :], ps, ACT.Identity)
                    else:
                        ins = act.activation(xT[:, kd, :], ps, ACT.Identity, bias=bias[:, kd:kd + 1],
                                             scale=gain[:, kd:kd + 1])
                    self.ring.free(ins, f"{name}{kd}")
                self.s["xT"].by(act.drain())

            def product(self, pe, it, name, w, m, rhs, kt, width=P):
                ps = self.ring.acquire(pe, it, name)
                for k in range(kt):
                    last = pe.matmul(ps[0:width, :], w[:, k, m * P:m * P + width], rhs[:, k, :],
                                     start=k == 0, stop=k == kt - 1)
                self.ring.full.by(last)

            def product_tok(self, pe, it, name, actT, w, kt):
                for h in range(2):
                    ps = self.ring.acquire(pe, it, f"{name}{h}")
                    for i in range(2):
                        tok = slice((2 * h + i) * P, (2 * h + i + 1) * P)
                        for k in range(kt):
                            last = pe.matmul(ps[:, i * D:(i + 1) * D], actT[:, k, tok], w[:, k, :],
                                             start=k == 0, stop=k == kt - 1)
                    self.ring.full.by(last)

            def attn_pe(self, pe, it, wo, xt_k):
                s, ring = self.s, self.ring

                def scores(i):
                    ps = ring.acquire(pe, it, f"s{i}", 4)
                    for b in range(4):
                        kd, h0 = b // 2, (b % 2) * HPB
                        ring.full.by(pe.matmul(ps[:, b, 0:HPB * KEYS], qT[:, kd, i * P:(i + 1) * P],
                                               kz[:, kd, h0:h0 + HPB, :].rearrange("p h k -> p (h k)"),
                                               start=True, stop=True))

                def turn(i):
                    s["probs"].wait(pe, it, i + 1)
                    for g in range(3):
                        ps = ring.acquire(pe, it, f"pT{i}_{g}")
                        for pos in range(4 if g < 2 else 2):
                            kd, blk = (g, pos) if g < 2 else (pos, 4)
                            c0, n = kd * ROWS + blk * P, BLK[blk]
                            last = pe.transpose(ps[0:n, pos * P:(pos + 1) * P], self.p[:, i % 2, c0:c0 + n], ident[:, :])
                        ring.full.by(last)
                    s["probsT"].wait(pe, it, i + 1)
                    ps = ring.acquire(pe, it, f"pv{i}")
                    for kd in range(KD):
                        for blk, n in enumerate(BLK):
                            g, pos = (kd, blk) if blk < 4 else (2, kd)
                            last = pe.matmul(ps[:, kd * P:(kd + 1) * P], vz[0:n, kd, blk, :],
                                             self.pt[0:n, i % 2, g, pos * P:(pos + 1) * P],
                                             start=blk == 0, stop=blk == 4)
                    ring.full.by(last)

                s["qT"].wait(pe, it, 1)
                scores(0)
                for i in range(TT):
                    if i + 1 < TT:
                        scores(i + 1)
                    turn(i)
                s["oaT"].wait(pe, it, 1)
                self.product_tok(pe, it, "ao_x", oaT, wo, KD)

            def attn_act(self, act, it, q_bias=None, v_bias=None):
                s, ring = self.s, self.ring
                for kd in range(KD):
                    ps = ring.filled(act, it, f"xq{kd}")
                    b = 0.0 if q_bias is None else q_bias[:, kd:kd + 1]
                    ring.free(act.activation(qT[:, kd, :], ps, ACT.Identity, bias=b), f"xq{kd}")
                s["qT"].by(act.drain())

                def exps(i):
                    s["centred"].wait(act, it, i + 1)
                    s["exps"].by(act.activation(self.p[:, i % 2, :], self.p[:, i % 2, :], ACT.Exp, scale=DH ** -0.5))

                def move(i):
                    for g in range(3):
                        n, w = (P, CH) if g < 2 else (BLK[4], 2 * P)
                        ps = ring.filled(act, it, f"pT{i}_{g}")
                        ring.free(act.activation(self.pt[0:n, i % 2, g, 0:w], ps[0:n, 0:w], ACT.Copy), f"pT{i}_{g}")
                    s["probsT"].by(act.drain())
                    ps = ring.filled(act, it, f"pv{i}")
                    for kd in range(KD):
                        b = 0.0 if v_bias is None else v_bias[:, kd:kd + 1]
                        ins = act.activation(oaT[:, kd, i * P:(i + 1) * P], ps[:, kd * P:(kd + 1) * P], ACT.Identity, bias=b)
                    ring.free(ins, f"pv{i}")

                exps(0)
                for i in range(TT):
                    if i + 1 < TT:
                        exps(i + 1)
                    move(i)
                s["oaT"].by(act.drain())

            def attn_dve(self, dve, it):
                s, ring = self.s, self.ring

                def centre(i):
                    ps = ring.filled(dve, it, f"s{i}", 4)[:, :, 0:HPB * KEYS].rearrange("p b (h k) -> p b h k", h=HPB)
                    m = mx[:, i % 2, :].rearrange("p (b h) -> p b h", b=4)
                    dve.tensor_reduce(m, ps, axis=AX, op=ALU.max)
                    dve.drain()
                    if i >= 2:
                        ring.filled(dve, it, f"pT{i - 2}_2")
                    for b in range(4):
                        ins = dve.tensor_tensor(
                            self.p[:, i % 2, b * HPB * KEYS:(b + 1) * HPB * KEYS].rearrange("p (h k) -> p h k", h=HPB),
                            ps[:, b], m[:, b, :].unsqueeze(2).to_broadcast([P, HPB, KEYS]), ALU.subtract)
                        ring.free(ins, f"s{i}", b)
                    s["centred"].by(dve.drain())

                centre(0)
                for i in range(TT):
                    if i + 1 < TT:
                        centre(i + 1)
                    s["exps"].wait(dve, it, i + 1)
                    r = rs[:, i % 2, :]
                    dve.tensor_reduce(r, self.p[:, i % 2, :].rearrange("p (h k) -> p h k", h=HEADS), axis=AX, op=ALU.add)
                    dve.drain()
                    s["inv_sums"].by(dve.reciprocal(r, r))

            def attn_pool(self, pool, it):
                s = self.s
                for i in range(TT):
                    s["inv_sums"].wait(pool, it, i + 1)
                    v = self.p[:, i % 2, :].rearrange("p (h k) -> p h k", h=HEADS)
                    s["probs"].by(pool.tensor_tensor(out=v, in0=v, in1=rs[:, i % 2, :].unsqueeze(2).to_broadcast([P, HEADS, KEYS]),
                                                     op=ALU.mult))

        ATTN_SIGNALS = dict(qT=1, centred=TT, exps=TT, inv_sums=TT, probs=TT, probsT=TT, oaT=1)
        ATTN_PLAN = [("xq0", "act", 1), ("xq1", "act", 1), ("s0", "dve", 4)]
        for i in range(TT):
            if i + 1 < TT:
                ATTN_PLAN += [(f"s{i + 1}", "dve", 4)]
            ATTN_PLAN += [(f"pT{i}_{g}", "act", 1) for g in range(3)] + [(f"pv{i}", "act", 1)]
        ATTN_PLAN += [("ao_x0", "dve", 1), ("ao_x1", "dve", 1)]

        def attn_plan(before):
            pad = -(before + 2) % 4
            return ([("pad", None, pad)] if pad else []) + ATTN_PLAN

        def kv_setup(tag, stack, w_k, w_v, k_bias, loaded):
            ctx_sb = alloc(stack, f"{tag}ctx_sb", [P, KD, BATCH, KEYS])
            ctx_rep = alloc(stack, f"{tag}ctx_rep", [P, KD, BATCH, HPT, KEYS])
            k_sb = alloc(stack, f"{tag}k_sb", [P, KD, BATCH, KEYS])
            kz_sb = alloc(stack, f"{tag}kz_sb", [P, BATCH, KD, HPT, KEYS])
            vz_sb = alloc(stack, f"{tag}vz_sb", [P, BATCH, KD, 5, P])
            s_ctx, s_rep, s_kp, s_ks = (sem(f"{tag}_{n}") for n in ("ctx", "ctx_rep", "k_psum", "k_sb"))
            s_vp, s_vf, s_made, s_st = (sem(f"{tag}_{n}") for n in ("v_psum", "v_freed", "kzvz_made", "kzvz_stored"))

            def on_sync(sp):
                load(sp, ctx_sb[:].rearrange("p k b s -> p (k b s)"), t["ctxT"], s_ctx)

            def on_pe(pe):
                pe.wait_ge(s_ctx, 16)
                for s_loaded in loaded:
                    pe.wait_ge(s_loaded, 16)
                for m in range(KD):
                    for k in range(KD):
                        last = pe.matmul(psum[:, m, 0:BATCH * KEYS], w_k[:, k, m * P:(m + 1) * P],
                                         ctx_sb[:, k].rearrange("p b s -> p (b s)"), start=k == 0, stop=k == KD - 1)
                    last.then_inc(s_kp, 1)
                pe.wait_ge(s_rep, 1)
                for n in range(BATCH * 5):
                    b, blk = n // 5, n % 5
                    if n >= 4:
                        pe.wait_ge(s_vf, n - 3)
                    for k in range(KD):
                        rows = ctx_rep[:, k, b].rearrange("p h s -> p (h s)")[:, blk * P:blk * P + BLK[blk]]
                        last = pe.matmul(psum[0:BLK[blk], 2 + n % 4, 0:D], rows, w_v[:, k, 0:D], start=k == 0, stop=k == KD - 1)
                    last.then_inc(s_vp, 1)

            def on_act(act):
                for m in range(KD):
                    act.wait_ge(s_kp, m + 1)
                    b = 0.0 if k_bias is None else k_bias[:, m:m + 1]
                    act.activation(k_sb[:, m].rearrange("p b s -> p (b s)"), psum[:, m, 0:BATCH * KEYS],
                                   ACT.Identity, bias=b).then_inc(s_ks, 1)

            def on_dve(dve):
                dve.wait_ge(s_ctx, 16)
                for k in range(KD):
                    for b in range(BATCH):
                        dve.tensor_copy(ctx_rep[:, k, b], ctx_sb[:, k, b].unsqueeze(1).to_broadcast([P, HPT, KEYS]))
                dve.drain().then_inc(s_rep, 1)
                dve.wait_ge(s_ks, KD)
                dve.wait_ge(s_const, 1)
                for b in range(BATCH):
                    for m in range(KD):
                        dve.tensor_tensor(kz_sb[:, b, m], k_sb[:, m, b].unsqueeze(1).to_broadcast([P, HPT, KEYS]),
                                          head_mask[:, :].unsqueeze(2).to_broadcast([P, HPT, KEYS]), ALU.mult)
                dve.memset(vz_sb[:, :, :, 4, :], 0.0)
                dve.drain()
                for n in range(BATCH * 5):
                    b, blk = n // 5, n % 5
                    r = BLK[blk]
                    dve.wait_ge(s_vp, n + 1)
                    dve.tensor_tensor(vz_sb[0:r, b, :, blk, :], psum[0:r, 2 + n % 4, 0:D].rearrange("p (k c) -> p k c", k=KD),
                                      row_mask[0:r, blk, :].unsqueeze(1).to_broadcast([r, KD, P]), ALU.mult).then_inc(s_vf, 1)
                dve.drain().then_inc(s_made, 1)

            def store(sp):
                sp.wait_ge(s_made, 1)
                sp.dma_start(kz_dram.rearrange("b p n -> p b n"), kz_sb[:].rearrange("p b m h s -> p b (m h s)")).then_inc(s_st, 16)
                sp.dma_start(vz_dram.rearrange("b p n -> p b n"), vz_sb[:].rearrange("p b m k c -> p b (m k c)")).then_inc(s_st, 16)
                sp.wait_ge(s_st, 32)

            return on_sync, on_pe, on_act, on_dve, store

        def chunk_loads(sp, ps, it, src):
            b = sp.snap(it // CPB)
            tile0 = sp.snap(it * TT)
            sp.wait_ge(ps.end, it * ENGINES + 1)
            sp.dma_start(x_in[:], src[bass.ds(tile0, TT), :, :].rearrange("t p d -> p t d")).then_inc(ps.chunk_in, 16)
            sp.dma_start(kz[:].rearrange("p m h s -> p (m h s)"),
                         kz_dram[bass.ds(b, 1), :, :].rearrange("b p n -> p (b n)")).then_inc(ps.chunk_in, 16)
            sp.dma_start(vz[:].rearrange("p m k c -> p (m k c)"),
                         vz_dram[bass.ds(b, 1), :, :].rearrange("b p n -> p (b n)")).then_inc(ps.chunk_in, 16)
            return tile0

        x_dram = t["x"].rearrange("b (t p) d -> (b t) p d", p=P)
        mid_v = mid.rearrange("(t p) d -> t p d", p=P)
        out_v = out.rearrange("b (t p) d -> (b t) p d", p=P)

        la = ExitStack()
        with la:
            def w(name, k, n):
                return alloc(la, "sb_" + name, [P, k, n])
            WA = {"a_Wq": (KD, HID), "a_Wk": (KD, HID), "a_Wv": (KD, HID), "a_Wg": (KD, HID), "a_Wo": (KH, D),
                  "a_W1": (KD, HID), "a_W2": (KH, D), "x0_Wq": (KD, D), "x0_Wk": (KD, D), "x0_Wv": (KD, D),
                  "x0_Wo": (KD, D), "e_gate": (KD, NE), "e_Wg": (KD, HID), "e_Wu": (KD, HID), "e_Wd": (NE, D)}
            ORDER_A = ["x0_Wk", "x0_Wv", "a_Wk", "a_Wg", "a_Wv", "a_Wq", "a_Wo", "a_W1", "a_W2", "x0_Wq", "x0_Wo",
                       "e_gate", "e_Wg", "e_Wu", "e_Wd"]
            VA = {"v_ln1_g": KD, "v_ln1_b": KD, "v_bq": KH, "v_bk": KH, "v_bv": KH, "v_bg": KH, "v_decay": KH,
                  "v_ln2_g": KD, "v_ln2_b": KD, "v_b1": KH}
            s_vec_a = sem("a_vectors_loaded")
            s_decay = sem("decay_made")
            s_w = {n: sem("loaded_" + n) for n in WA}
            wa = {n: w(n, *WA[n]) for n in WA}
            va = {n: alloc(la, "sb_" + n, [P, k]) for n, k in VA.items()}
            n_vec_a = 16 * (len(VA) + 2)
            bo_row = alloc(la, "bo_row", [P, D])
            b2_row = alloc(la, "b2_row", [P, D])
            decay = alloc(la, "decay", [P, KH])
            carry = alloc(la, "carry", [P, KH])
            with ExitStack() as setup_stack:
                kv0 = kv_setup("kv0", setup_stack, wa["x0_Wk"], wa["x0_Wv"], None, (s_w["x0_Wk"], s_w["x0_Wv"]))
            hT = alloc(la, "hT", [P, KH, CH])
            rB = alloc(la, "rB", [P, NE, CH])
            scr = alloc(la, "scr", [P, 2, HEADS * KEYS])
            scr_t = alloc(la, "scr_t", [P, 2, 3, CH])
            g_sb = alloc(la, "g_sb", [P, 2, CH])
            with ExitStack() as stack:
                k_sb = alloc(stack, "k_sb", [P, 2, CH])
                kv = alloc(stack, "kv", [P, CH])
                st = alloc(stack, "st", [P, CH])
                qg = alloc(stack, "qg", [P, CH])
            XM = 2
            xm = alloc(la, "xm", [P, XM, KD, CH])
            lg = alloc(la, "lg", [P, TT, NE])
            eq = alloc(la, "eq", [P, TT, NE])
            top1 = alloc(la, "top1", [P, TT])
            sgm = alloc(la, "sgm", [P, TT])
            fk = alloc(la, "fk", [P, TT])
            rT = alloc(la, "rT", [NE, CH])

            plan = [("xT1_0", "act", 1), ("xT1_1", "act", 1)]
            for m in range(KH):
                plan += [(f"k{m}", "act", 1), (f"g{m}", "act", 1), (f"v{m}", "dve", 1), (f"q{m}", "dve", 1)]
            plan += [("ao0", "dve", 1), ("ao1", "dve", 1), ("xT2_0", "act", 1), ("xT2_1", "act", 1)]
            plan += [(f"f{m}", "act", 1) for m in range(KH)]
            plan += [("fo0", "dve", 1), ("fo1", "dve", 1), ("xT3_0", "act", 1), ("xT3_1", "act", 1)]
            plan += attn_plan(len(plan) and sum(n for _, _, n in plan))
            plan += [("xT4_0", "act", 1), ("xT4_1", "act", 1), ("lg", "dve", 1), ("rT", "act", 1)]
            plan += [(f"rb{e}", "act", 1) for e in range(NE)]
            plan += [("eg", "act", 1), ("eu", "dve", 1), ("ed0", "dve", 1), ("ed1", "dve", 1)]
            A = Pass("A", plan, dict(var=5, rstd=5, xn=5 * TT, xT=4, kg=KH, kvd=KH, oT=KH, resid=3, gelu=1,
                                     top=1, sig=1, route=1, rT=1, rb=NE, xm=NE, xmu=NE - 1, silu=1, he=NE,
                                     **ATTN_SIGNALS), scr, scr_t)
            S, ring = A.s, A.ring
            he = hT
            sg, hu = g_sb[:, 0, :], g_sb[:, 1, :]

            blockA = ExitStack()
            with blockA:
                block = blockA.enter_context(nc.Block())

                @block.sync
                def _(sp):
                    kv0[0](sp)
                    for n in ORDER_A[:2]:
                        load(sp, wa[n][:].rearrange("p k n -> p (k n)"), t[n], s_w[n])
                    sp.wait_ge(s_w["x0_Wk"], 16)
                    for n in VA:
                        load(sp, va[n][:], t[n], s_vec_a)
                    for dst, n in ((bo_row, "r_bo"), (b2_row, "r_b2")):
                        load(sp, dst[:], t[n].unsqueeze(0).to_broadcast([P, D]), s_vec_a)
                    for n in ORDER_A[2:]:
                        load(sp, wa[n][:].rearrange("p k n -> p (k n)"), t[n], s_w[n])
                    kv0[4](sp)
                    sp.sem_inc(A.end, 1)
                    with sp.Fori(0, NCH) as it:
                        tile0 = chunk_loads(sp, A, it, x_dram)
                        S["xn"].wait(sp, it, 5 * TT)
                        sp.dma_start(mid_v[bass.ds(tile0, TT), :, :].rearrange("t p d -> p t d"), x_b[:]).then_inc(A.stored, 16)
                        sp.wait_ge(A.stored, it * 16 + 16)
                        sp.sem_inc(A.end, 1)

                @block.gpsimd
                def _(pool):
                    pool.memset(ident[:], 0.0)
                    pool.memset(head_mask[:], 1.0)
                    pool.memset(row_mask[:], 1.0)
                    pool.memset(half_neg[:], -0.5)
                    for e in range(NE):
                        pool.memset(first_key[:, e:e + 1], float(NE - e))
                    for c in range(NCH):
                        pool.memset(keep[:, c:c + 1], float(c % CPB != CPB - 1))
                    pool.drain()
                    pool.affine_select(out=ident[:], in_=ident[:], compare_op=ALU.not_equal, fill=1.0, base=0,
                                       pattern=[[-1, P]], channel_multiplier=1)
                    pool.affine_select(out=head_mask[:], in_=head_mask[:], compare_op=ALU.is_ge, fill=0.0, base=0,
                                       pattern=[[-DH, HPT]], channel_multiplier=1)
                    v = row_mask[:].rearrange("p k (h c) -> p k h c", c=DH)
                    pool.affine_select(out=v, in_=v, compare_op=ALU.is_ge, fill=0.0, base=0,
                                       pattern=[[P, 5], [-KEYS, HPT], [0, DH]], channel_multiplier=1)
                    pool.drain()
                    pool.affine_select(out=head_mask[:], in_=head_mask[:], compare_op=ALU.is_ge, fill=0.0, base=DH - 1,
                                       pattern=[[DH, HPT]], channel_multiplier=-1)
                    pool.affine_select(out=v, in_=v, compare_op=ALU.is_ge, fill=0.0, base=KEYS - 1,
                                       pattern=[[-P, 5], [KEYS, HPT], [0, DH]], channel_multiplier=-1)
                    pool.drain().then_inc(s_const, 1)
                    pool.wait_ge(s_vec_a, n_vec_a)
                    with pool.Fori(0, NCH) as it:
                        A.ln_pool(pool, it, 1)
                        bc = bo_row[:].unsqueeze(1).to_broadcast([P, TT, D])
                        pool.wait_ge(A.chunk_in, it * 48 + 48)
                        S["resid"].by(pool.tensor_tensor(out=x_a[:], in0=x_in[:], in1=bc, op=ALU.add))
                        A.ln_pool(pool, it, 2)
                        bc = b2_row[:].unsqueeze(1).to_broadcast([P, TT, D])
                        S["resid"].by(pool.tensor_tensor(out=x_in[:], in0=x_in[:], in1=bc, op=ALU.add))
                        pool.drain()
                        S["xn"].wait(pool, it, 2 * TT)
                        S["resid"].by(pool.tensor_tensor(out=x_a[:], in0=x_in[:], in1=x_r[:], op=ALU.add))
                        A.ln_pool(pool, it, 3)
                        A.attn_pool(pool, it)
                        A.ln_pool(pool, it, 4)
                        A.ln_pool(pool, it, 5)
                        A.iteration_end(pool, it)

                @block.vector
                def _(dve):
                    kv0[3](dve)
                    dve.memset(carry[:], 0.0)
                    dve.tensor_tensor(sel_bc[:], ident[:, DTR:XDB], ident[:, LO + DTR:LO + XDB], ALU.add)
                    dve.drain().then_inc(s_setup, 1)
                    dve.wait_ge(s_vec_a, n_vec_a)
                    dve.wait_ge(s_decay, 1)
                    with dve.Fori(0, NCH) as it:
                        dve.wait_ge(A.chunk_in, it * 48 + 48)
                        A.ln_dve(dve, it, 1, x_in, x_b)
                        for m in range(KH):
                            S["kg"].wait(dve, it, m + 1)
                            ps = ring.filled(dve, it, f"v{m}")
                            ins = dve.scalar_tensor_tensor(kv[:], ps, va["v_bv"][:, m:m + 1], k_sb[:, m % 2, :],
                                                           op0=ALU.add, op1=ALU.mult)
                            ring.free(ins, f"v{m}")
                            dve.drain()
                            dve.tensor_tensor_scan(st[:], decay[:, m:m + 1].to_broadcast([P, CH]), kv[:],
                                                   carry[:, m:m + 1], ALU.mult, ALU.add)
                            ps = ring.filled(dve, it, f"q{m}")
                            ins = dve.scalar_tensor_tensor(qg[:], ps, va["v_bq"][:, m:m + 1], g_sb[:, m % 2, :],
                                                           op0=ALU.add, op1=ALU.mult)
                            ring.free(ins, f"q{m}")
                            S["kvd"].by(dve.drain())
                            dve.tensor_scalar(carry[:, m:m + 1], st[:, CH - 1:CH], keep[:, bass.ds(it, 1)], None, op0=ALU.mult)
                            S["oT"].by(dve.scalar_tensor_tensor(hT[:, m, :], st[:], 64 ** -0.5, qg[:],
                                                                op0=ALU.mult, op1=ALU.mult))
                        S["resid"].wait(dve, it, 1)
                        A.residual_ln(dve, it, "ao", x_a, 2, x_b)
                        S["resid"].wait(dve, it, 3)
                        A.residual_ln(dve, it, "fo", x_a, 3, x_b)
                        A.attn_dve(dve, it)
                        A.residual_ln(dve, it, "ao_x", x_b, 4, x_a)
                        ps = ring.filled(dve, it, "lg")
                        ring.free(dve.tensor_copy(lg[:], ps[:, 0:TT * NE].rearrange("p (t e) -> p t e", t=TT)), "lg")
                        dve.drain()
                        S["top"].by(dve.tensor_reduce(top1[:], lg[:], axis=AX, op=ALU.max))
                        dve.drain()
                        dve.tensor_tensor(eq[:], lg[:], top1[:].unsqueeze(2).to_broadcast([P, TT, NE]), ALU.is_equal)
                        dve.drain()
                        dve.tensor_tensor(eq[:], eq[:], first_key[:].unsqueeze(1).to_broadcast([P, TT, NE]), ALU.mult)
                        dve.drain()
                        dve.tensor_reduce(fk[:], eq[:], axis=AX, op=ALU.max)
                        dve.drain()
                        dve.tensor_tensor(eq[:], eq[:], fk[:].unsqueeze(2).to_broadcast([P, TT, NE]), ALU.is_equal)
                        dve.drain()
                        S["sig"].wait(dve, it, 1)
                        S["route"].by(dve.tensor_tensor(lg[:], eq[:], sgm[:].unsqueeze(2).to_broadcast([P, TT, NE]), ALU.mult))
                        for e in range(NE):
                            S["rb"].wait(dve, it, e + 1)
                            if e >= XM:
                                S["xmu"].wait(dve, it, e - XM + 1)
                            S["xm"].by(dve.tensor_tensor(xm[:, e % XM], xT[:], rB[:, e, :].unsqueeze(1).to_broadcast([P, KD, CH]),
                                                         ALU.mult))
                        S["silu"].wait(dve, it, 1)
                        ps = ring.filled(dve, it, "eu")
                        ring.free(dve.tensor_tensor(hu, ps, sg, ALU.mult), "eu")
                        dve.drain()
                        for e in range(NE):
                            S["he"].by(dve.scalar_tensor_tensor(he[:, e, :], rB[:, e, :], 0.0, hu, op0=ALU.is_gt, op1=ALU.mult))
                        A.residual_ln(dve, it, "ed", x_a, 5, x_b)
                        A.iteration_end(dve, it)

                @block.scalar
                def _(act):
                    kv0[2](act)
                    act.wait_ge(s_vec_a, n_vec_a)
                    act.activation(decay[:], va["v_decay"][:], ACT.Sigmoid).then_inc(s_decay, 1)
                    with act.Fori(0, NCH) as it:
                        A.transpose_act(act, it, "xT1_", va["v_ln1_g"], va["v_ln1_b"])
                        for m in range(KH):
                            if m >= 2:
                                S["kvd"].wait(act, it, m - 1)
                            ps = ring.filled(act, it, f"k{m}")
                            ring.free(act.activation(k_sb[:, m % 2, :], ps, ACT.Identity, bias=va["v_bk"][:, m:m + 1]), f"k{m}")
                            ps = ring.filled(act, it, f"g{m}")
                            ring.free(act.activation(g_sb[:, m % 2, :], ps, ACT.Sigmoid, bias=va["v_bg"][:, m:m + 1]), f"g{m}")
                            S["kg"].by(act.drain())
                        A.transpose_act(act, it, "xT2_", va["v_ln2_g"], va["v_ln2_b"])
                        ring.filled(act, it, "ao1")
                        for m in range(KH):
                            ps = ring.filled(act, it, f"f{m}")
                            ring.free(act.activation(hT[:, m, :], ps, ACT.Gelu, bias=va["v_b1"][:, m:m + 1]), f"f{m}")
                        S["gelu"].by(act.drain())
                        A.transpose_act(act, it, "xT3_")
                        A.attn_act(act, it)
                        A.transpose_act(act, it, "xT4_")
                        S["top"].wait(act, it, 1)
                        S["sig"].by(act.activation(sgm[:], top1[:], ACT.Sigmoid))
                        ps = ring.filled(act, it, "rT")
                        ring.free(act.activation(rT[:], ps[0:NE, :], ACT.Copy), "rT")
                        S["rT"].by(act.drain())
                        for e in range(NE):
                            ps = ring.filled(act, it, f"rb{e}")
                            ring.free(act.activation(rB[:, e, :], ps, ACT.Copy), f"rb{e}")
                            S["rb"].by(act.drain())
                        ps = ring.filled(act, it, "eg")
                        ring.free(act.activation(sg, ps, ACT.Silu), "eg")
                        S["silu"].by(act.drain())
                        A.iteration_end(act, it)

                @block.tensor
                def _(pe):
                    pe.wait_ge(s_const, 1)
                    kv0[1](pe)
                    pe.wait_ge(s_setup, 1)
                    for n in ORDER_A[2:]:
                        pe.wait_ge(s_w[n], 16)
                    with pe.Fori(0, NCH) as it:
                        A.transpose_pe(pe, it, "xT1_", x_b, 1)
                        S["xT"].wait(pe, it, 1)
                        for m in range(KH):
                            for n in "kgvq":
                                A.product(pe, it, f"{n}{m}", wa["a_W" + n], m, xT, KD)
                        S["oT"].wait(pe, it, KH)
                        A.product_tok(pe, it, "ao", hT, wa["a_Wo"], KH)
                        A.transpose_pe(pe, it, "xT2_", x_b, 2)
                        S["xT"].wait(pe, it, 2)
                        for m in range(KH):
                            A.product(pe, it, f"f{m}", wa["a_W1"], m, xT, KD)
                        S["gelu"].wait(pe, it, 1)
                        A.product_tok(pe, it, "fo", hT, wa["a_W2"], KH)
                        A.transpose_pe(pe, it, "xT3_", x_b, 3)
                        S["xT"].wait(pe, it, 3)
                        pe.wait_ge(A.chunk_in, it * 48 + 48)
                        for m in range(KD):
                            A.product(pe, it, f"xq{m}", wa["x0_Wq"], m, xT, KD)
                        A.attn_pe(pe, it, wa["x0_Wo"], 3)
                        A.transpose_pe(pe, it, "xT4_", x_a, 4)
                        S["xT"].wait(pe, it, 4)
                        ps = ring.acquire(pe, it, "lg")
                        for i in range(TT):
                            for k in range(KD):
                                last = pe.matmul(ps[:, i * NE:(i + 1) * NE], xT[:, k, i * P:(i + 1) * P], wa["e_gate"][:, k, :],
                                                 start=k == 0, stop=k == KD - 1)
                        ring.full.by(last)
                        S["route"].wait(pe, it, 1)
                        ps = ring.acquire(pe, it, "rT")
                        for i in range(TT):
                            last = pe.transpose(ps[0:NE, i * P:(i + 1) * P], lg[:, i, :], ident[:])
                        ring.full.by(last)
                        S["rT"].wait(pe, it, 1)
                        for e in range(NE):
                            ps = ring.acquire(pe, it, f"rb{e}")
                            ring.full.by(pe.matmul(ps, ident[0:NE, e:e + 1].to_broadcast([NE, P]), rT[:], start=True, stop=True))
                        pg, pu = ring.acquire(pe, it, "eg"), ring.acquire(pe, it, "eu")
                        for e in range(NE):
                            S["xm"].wait(pe, it, e + 1)
                            for ps, wt in ((pg, wa["e_Wg"]), (pu, wa["e_Wu"])):
                                for k in range(KD):
                                    last = pe.matmul(ps, wt[:, k, e * P:(e + 1) * P], xm[:, e % XM, k, :],
                                                     start=e == 0 and k == 0, stop=e == NE - 1 and k == KD - 1)
                                    if e == NE - 1 and k == KD - 1:
                                        ring.full.by(last)
                            if e < NE - 1:
                                S["xmu"].by(last)
                        S["he"].wait(pe, it, NE)
                        A.product_tok(pe, it, "ed", he, wa["e_Wd"], NE)
                        A.iteration_end(pe, it)
            A.check()

        lb = ExitStack()
        with lb:
            WB = {"m_in": (KD, 2 * INNER), "m_xp": (KI, LO + XDB), "m_out": (KI, D), "x1_Wqkv": (KD, 3 * D),
                  "x1_Wo": (KD, D), "f_w1": (KD, HID), "f_w2": (KD, HID), "f_h1": (KH, HID), "f_h2": (KH, HID),
                  "f_w3": (KH, D)}
            ORDER_B = ["x1_Wqkv", "m_in", "m_xp", "m_out", "x1_Wo", "f_w1", "f_w2", "f_h1", "f_h2", "f_w3"]
            VB = {"v_convw": KI * TAPS, "v_convb": KI, "v_dtb": KI, "v_alog": KI * NST, "v_D": KI, "v_bqkv": 3 * KD,
                  "v_s1": KH, "v_s2": KH, "v_s3": KH, "v_s4": KH}
            n_vec_b = 16 * (len(VB) + 3)
            s_vec_b = sem("b_vectors_loaded")
            s_wb = {n: sem("loaded_" + n) for n in WB}
            s_setup_b, s_exp_a = sem("b_setup_on_dve"), sem("exp_a_log")
            wb = {n: alloc(lb, "sb_" + n, [P, *WB[n]]) for n in WB}
            vb = {n: alloc(lb, "sb_" + n, [P, k]) for n, k in VB.items()}
            dtw = alloc(lb, "dtw", [DTR, INNER])
            bout_row = alloc(lb, "bout_row", [P, D])
            s5_row = alloc(lb, "s5_row", [P, D])
            halo = alloc(lb, "halo", [P, KI, TAPS - 1])
            h_carry = alloc(lb, "h_carry", [P, KI, NST])
            xd_r = alloc(lb, "xd_r", [LO + XDB, CH], F32R)
            xd_hi = x_r[0:LO + XDB, 0:2, :].rearrange("p t d -> p (t d)").bitcast(F32R)
            dtr = x_r[0:DTR, 2:4, :].rearrange("p t d -> p (t d)")
            with ExitStack() as stack:
                kv1 = kv_setup("kv1", stack, wb["x1_Wqkv"][:, :, D:2 * D], wb["x1_Wqkv"][:, :, 2 * D:3 * D],
                               vb["v_bqkv"][:, KD:2 * KD], (s_vec_b, s_wb["x1_Wqkv"]))
            with ExitStack() as stack:
                xbuf = alloc(stack, "xbuf", [P, KI, TAPS - 1 + CH])
                u = alloc(stack, "u", [P, KI, CH])
                wdt = alloc(stack, "wdt", [P, KI, CH])
                dt = alloc(stack, "dt", [P, KI, CH])
                dA = alloc(stack, "dA", [P, KI, CH])
                hb = alloc(stack, "hb", [P, KI, CH])
            y = xbuf[:, :, 0:CH]
            with ExitStack() as stack:
                scr = alloc(stack, "scr_b", [P, 2, HEADS * KEYS])
                scr_t = alloc(stack, "scr_t_b", [P, 2, 3, CH])
            with ExitStack() as stack:
                h0 = alloc(stack, "h0", [P, KH, CH])
                h1 = alloc(stack, "h1", [P, KH, CH])
                gate = alloc(stack, "gate", [P, 2, CH])

            plan = [("xT1_0", "act", 1), ("xT1_1", "act", 1)]
            plan += [(f"x{m}", "act", 1) for m in range(KI)] + [("xd", "dve", 1)] + [(f"dt{m}", "act", 1) for m in range(KI)]
            for n in range(NST):
                plan += [(f"B{n}", "dve", 1), (f"C{n}", "dve", 1)]
            plan += [(f"z{m}", "act", 1) for m in range(KI)] + [("mo0", "dve", 1), ("mo1", "dve", 1)]
            plan += [("xT2_0", "act", 1), ("xT2_1", "act", 1)]
            plan += attn_plan(sum(n for _, _, n in plan))
            plan += [("xT3_0", "act", 1), ("xT3_1", "act", 1)]
            for m in range(KH):
                plan += [(f"a{m}", "act", 1), (f"b{m}", "dve", 1)]
            plan += [(f"c{m}", "act", 1) for m in range(KH)] + [(f"d{m}", "act", 1) for m in range(KH)]
            plan += [("fo0", "dve", 1), ("fo1", "dve", 1)]
            B = Pass("B", plan, dict(var=3, rstd=3, xn=3 * TT, xT=3, xb=KI, conv=1, u=1, xd=1, soft=1, dt=1, y0=1,
                                     dA=NST * KI, scan=NST * KI, ch=NST, yn=NST, zs=KI, yz=1, resid=1, silu=KH, h0=1,
                                     gelu=2, **ATTN_SIGNALS), scr, scr_t)
            S, ring = B.s, B.ring

            blockB = ExitStack()
            with blockB:
                block = blockB.enter_context(nc.Block())

                @block.sync
                def _(sp):
                    for n in VB:
                        load(sp, vb[n][:], t[n], s_vec_b)
                    load(sp, dtw[:], t["m_dtw"], s_vec_b)
                    for dst, n in ((bout_row, "r_bout"), (s5_row, "r_s5")):
                        load(sp, dst[:], t[n].unsqueeze(0).to_broadcast([P, D]), s_vec_b)
                    kv1[0](sp)
                    for n in ORDER_B:
                        load(sp, wb[n][:].rearrange("p k n -> p (k n)"), t[n], s_wb[n])
                    kv1[4](sp)
                    sp.sem_inc(B.end, 1)
                    with sp.Fori(0, NCH) as it:
                        tile0 = chunk_loads(sp, B, it, mid_v)
                        S["xn"].wait(sp, it, 3 * TT)
                        sp.dma_start(out_v[bass.ds(tile0, TT), :, :].rearrange("t p d -> p t d"), x_a[:]).then_inc(B.stored, 16)
                        sp.wait_ge(B.stored, it * 16 + 16)
                        sp.sem_inc(B.end, 1)

                @block.gpsimd
                def _(pool):
                    pool.wait_ge(s_vec_b, n_vec_b)
                    with pool.Fori(0, NCH) as it:
                        S["u"].wait(pool, it, 1)
                        S["y0"].by(pool.tensor_tensor(out=y, in0=u[:], in1=vb["v_D"][:].unsqueeze(2).to_broadcast([P, KI, CH]),
                                                      op=ALU.mult))
                        for n in range(NST):
                            S["ch"].wait(pool, it, n + 1)
                            S["yn"].by(pool.tensor_tensor(out=y, in0=y, in1=u[:], op=ALU.add))
                            S["yn"].wait(pool, it, n + 1)
                        B.ln_pool(pool, it, 1)
                        S["xn"].wait(pool, it, TT)
                        S["resid"].by(pool.tensor_tensor(out=x_in[:], in0=x_a[:], in1=bout_row[:].unsqueeze(1).to_broadcast([P, TT, D]),
                                                         op=ALU.add))
                        B.attn_pool(pool, it)
                        B.ln_pool(pool, it, 2)
                        B.ln_pool(pool, it, 3)
                        B.iteration_end(pool, it)

                @block.vector
                def _(dve):
                    dve.wait_ge(s_vec_b, n_vec_b)
                    kv1[3](dve)
                    dve.memset(halo[:], 0.0)
                    dve.memset(h_carry[:], 0.0)
                    dve.memset(xd_r[:].bitcast(F32), 0.0)
                    dve.wait_ge(s_exp_a, 1)
                    dve.tensor_scalar(vb["v_alog"][:], vb["v_alog"][:], -1.0, None, op0=ALU.mult)
                    dve.drain().then_inc(s_setup_b, 1)
                    with dve.Fori(0, NCH) as it:
                        dve.wait_ge(B.chunk_in, it * 48 + 48)
                        dve.tensor_copy(xbuf[:, :, 0:TAPS - 1], halo[:])
                        dve.drain()
                        S["xb"].wait(dve, it, KI)
                        for m in range(KI):
                            dve.tensor_scalar(wdt[:, m, :], xbuf[:, m, 0:CH], vb["v_convw"][:, m * TAPS:m * TAPS + 1],
                                              vb["v_convb"][:, m:m + 1], op0=ALU.mult, op1=ALU.add)
                        for tap in range(1, TAPS):
                            dve.drain()
                            for m in range(KI):
                                dve.scalar_tensor_tensor(wdt[:, m, :], xbuf[:, m, tap:tap + CH],
                                                         vb["v_convw"][:, m * TAPS + tap:m * TAPS + tap + 1], wdt[:, m, :],
                                                         op0=ALU.mult, op1=ALU.add)
                        S["conv"].by(dve.drain())
                        dve.tensor_scalar(halo[:], xbuf[:, :, CH:CH + TAPS - 1], keep[:, bass.ds(it, 1)], None, op0=ALU.mult)
                        dve.drain()
                        ps = ring.filled(dve, it, "xd")
                        dve.tensor_copy(dtr, ps[0:DTR, :])
                        dve.tensor_copy(xd_r[0:XDB, :], ps[0:XDB, :])
                        dve.tensor_copy(xd_hi[LO:LO + XDB, :], ps[LO:LO + XDB, :])
                        dve.drain()
                        ring.free(dve.tensor_tensor(xd_r[LO:LO + XDB, :], ps[LO:LO + XDB, :], xd_hi[LO:LO + XDB, :].bitcast(F32),
                                                    ALU.subtract), "xd")
                        S["xd"].by(dve.drain())
                        S["soft"].wait(dve, it, 1)
                        S["dt"].by(dve.scalar_tensor_tensor(dt[:], dt[:], 0.0, hb[:], op0=ALU.max, op1=ALU.add))
                        dve.drain()
                        dve.tensor_tensor(wdt[:], dt[:], u[:], ALU.mult)
                        dve.drain()
                        S["y0"].wait(dve, it, 1)
                        for n in range(NST):
                            ps = ring.filled(dve, it, f"B{n}")
                            ring.free(dve.tensor_tensor(hb[:], wdt[:], ps.unsqueeze(1).to_broadcast([P, KI, CH]), ALU.mult), f"B{n}")
                            dve.drain()
                            for j in range(KI):
                                S["dA"].wait(dve, it, n * KI + j + 1)
                                S["scan"].by(dve.tensor_tensor_scan(hb[:, j, :], dA[:, j, :], hb[:, j, :],
                                                                    h_carry[:, j, n:n + 1], ALU.mult, ALU.add))
                            dve.drain()
                            dve.tensor_scalar(h_carry[:, :, n], hb[:, :, CH - 1], keep[:, bass.ds(it, 1)], None, op0=ALU.mult)
                            if n:
                                S["yn"].wait(dve, it, n)
                            ps = ring.filled(dve, it, f"C{n}")
                            ring.free(dve.tensor_tensor(u[:], hb[:], ps.unsqueeze(1).to_broadcast([P, KI, CH]), ALU.mult), f"C{n}")
                            S["ch"].by(dve.drain())
                        S["yn"].wait(dve, it, NST)
                        S["zs"].wait(dve, it, KI)
                        S["yz"].by(dve.tensor_tensor(wdt[:], y, dA[:], ALU.mult))
                        B.residual_ln(dve, it, "mo", x_in, 1, x_a)
                        B.attn_dve(dve, it)
                        S["resid"].wait(dve, it, 1)
                        B.residual_ln(dve, it, "ao_x", x_in, 2, x_b)
                        for m in range(KH):
                            S["silu"].wait(dve, it, m + 1)
                            ps = ring.filled(dve, it, f"b{m}")
                            ring.free(dve.scalar_tensor_tensor(h0[:, m, :], ps, vb["v_s2"][:, m:m + 1], gate[:, m % 2, :],
                                                               op0=ALU.mult, op1=ALU.mult), f"b{m}")
                        S["h0"].by(dve.drain())
                        for h in range(2):
                            ps = ring.filled(dve, it, f"fo{h}")
                            ring.free(dve.tensor_tensor(x_r[:, 2 * h:2 * h + 2, :], ps.rearrange("p (t d) -> p t d", t=2),
                                                        s5_row[:].unsqueeze(1).to_broadcast([P, 2, D]), ALU.mult), f"fo{h}")
                        dve.drain()
                        dve.tensor_tensor(x_r[:], x_r[:], x_b[:], ALU.add)
                        dve.drain()
                        B.ln_dve(dve, it, 3, x_r, x_a)
                        B.iteration_end(dve, it)

                @block.scalar
                def _(act):
                    act.wait_ge(s_vec_b, n_vec_b)
                    act.activation(vb["v_alog"][:], vb["v_alog"][:], ACT.Exp).then_inc(s_exp_a, 1)
                    kv1[2](act)
                    act.wait_ge(s_setup_b, 1)
                    with act.Fori(0, NCH) as it:
                        B.transpose_act(act, it, "xT1_")
                        for m in range(KI):
                            ps = ring.filled(act, it, f"x{m}")
                            ring.free(act.activation(xbuf[:, m, TAPS - 1:], ps, ACT.Copy), f"x{m}")
                            S["xb"].by(act.drain())
                        S["conv"].wait(act, it, 1)
                        act.activation(u[:], wdt[:], ACT.Silu)
                        S["u"].by(act.drain())
                        for m in range(KI):
                            ps = ring.filled(act, it, f"dt{m}")
                            ring.free(act.activation(dt[:, m, :], ps, ACT.Identity, bias=vb["v_dtb"][:, m:m + 1]), f"dt{m}")
                        act.drain()
                        act.activation(hb[:], dt[:], ACT.Abs)
                        act.drain()
                        act.activation(hb[:], hb[:], ACT.Exp, scale=-1.0)
                        act.drain()
                        S["soft"].by(act.activation(hb[:], hb[:], ACT.Ln, bias=1.0))
                        S["dt"].wait(act, it, 1)
                        for n in range(NST):
                            for j in range(KI):
                                if n:
                                    S["scan"].wait(act, it, (n - 1) * KI + j + 1)
                                S["dA"].by(act.activation(dA[:, j, :], dt[:, j, :], ACT.Exp,
                                                          scale=vb["v_alog"][:, j * NST + n:j * NST + n + 1]))
                        for m in range(KI):
                            S["scan"].wait(act, it, (NST - 1) * KI + m + 1)
                            ps = ring.filled(act, it, f"z{m}")
                            ring.free(act.activation(dA[:, m, :], ps, ACT.Silu), f"z{m}")
                            S["zs"].by(act.drain())
                        B.transpose_act(act, it, "xT2_")
                        B.attn_act(act, it, vb["v_bqkv"][:, 0:KD], vb["v_bqkv"][:, 2 * KD:3 * KD])
                        B.transpose_act(act, it, "xT3_")
                        for m in range(KH):
                            if m >= 2:
                                ring.freed["dve"].wait(act, it, ring.slots[:ring.where[f"b{m - 2}"] + 1].count("dve"))
                            ps = ring.filled(act, it, f"a{m}")
                            ring.free(act.activation(gate[:, m % 2, :], ps, ACT.Silu, scale=vb["v_s1"][:, m:m + 1]), f"a{m}")
                            S["silu"].by(act.drain())
                        for m in range(KH):
                            ps = ring.filled(act, it, f"c{m}")
                            ring.free(act.activation(h1[:, m, :], ps, ACT.Gelu, scale=vb["v_s3"][:, m:m + 1]), f"c{m}")
                        S["gelu"].by(act.drain())
                        for m in range(KH):
                            ps = ring.filled(act, it, f"d{m}")
                            ring.free(act.activation(h0[:, m, :], ps, ACT.Gelu, scale=vb["v_s4"][:, m:m + 1]), f"d{m}")
                        S["gelu"].by(act.drain())
                        B.iteration_end(act, it)

                @block.tensor
                def _(pe):
                    kv1[1](pe)
                    pe.wait_ge(s_setup_b, 1)
                    for n in ORDER_B[1:5]:
                        pe.wait_ge(s_wb[n], 16)
                    with pe.Fori(0, NCH) as it:
                        pe.wait_ge(B.chunk_in, it * 48 + 48)
                        B.transpose_pe(pe, it, "xT1_", x_in, 0)
                        S["xT"].wait(pe, it, 1)
                        for m in range(KI):
                            B.product(pe, it, f"x{m}", wb["m_in"], m, xT, KD)
                        S["u"].wait(pe, it, 1)
                        B.product(pe, it, "xd", wb["m_xp"], 0, u, KI, LO + XDB)
                        S["xd"].wait(pe, it, 1)
                        for m in range(KI):
                            ps = ring.acquire(pe, it, f"dt{m}")
                            ring.full.by(pe.matmul(ps, dtw[:, m * P:(m + 1) * P], dtr, start=True, stop=True))
                        for n in range(NST):
                            for c, nm in ((n, f"B{n}"), (NST + n, f"C{n}")):
                                ps = ring.acquire(pe, it, nm)
                                ring.full.by(pe.matmul(ps, sel_bc[0:LO + XDB, c:c + 1].to_broadcast([LO + XDB, P]), xd_r[:],
                                                       start=True, stop=True))
                        for m in range(KI):
                            B.product(pe, it, f"z{m}", wb["m_in"], KI + m, xT, KD)
                        S["yz"].wait(pe, it, 1)
                        B.product_tok(pe, it, "mo", wdt, wb["m_out"], KI)
                        B.transpose_pe(pe, it, "xT2_", x_a, 1)
                        S["xT"].wait(pe, it, 2)
                        for m in range(KD):
                            B.product(pe, it, f"xq{m}", wb["x1_Wqkv"], m, xT, KD)
                        B.attn_pe(pe, it, wb["x1_Wo"], 2)
                        B.transpose_pe(pe, it, "xT3_", x_b, 2)
                        S["xT"].wait(pe, it, 3)
                        for n in ORDER_B[5:]:
                            pe.wait_ge(s_wb[n], 16)
                        for m in range(KH):
                            B.product(pe, it, f"a{m}", wb["f_w1"], m, xT, KD)
                            B.product(pe, it, f"b{m}", wb["f_w2"], m, xT, KD)
                        S["h0"].wait(pe, it, 1)
                        for m in range(KH):
                            B.product(pe, it, f"c{m}", wb["f_h1"], m, h0, KH)
                        S["gelu"].wait(pe, it, 1)
                        for m in range(KH):
                            B.product(pe, it, f"d{m}", wb["f_h2"], m, h1, KH)
                        S["gelu"].wait(pe, it, 2)
                        B.product_tok(pe, it, "fo", h0, wb["f_w3"], KH)
                        B.iteration_end(pe, it)
            B.check()


def kernel(x, ctx_1024, L0_attn_ln1_g, L0_attn_ln1_b, L0_attn_Wq, L0_attn_bq, L0_attn_Wk, L0_attn_bk, L0_attn_Wv,
           L0_attn_bv, L0_attn_Wg, L0_attn_bg, L0_attn_decay_logit, L0_attn_Wo, L0_attn_bo, L0_attn_ln2_g,
           L0_attn_ln2_b, L0_attn_W1, L0_attn_b1, L0_attn_W2, L0_attn_b2, L0_xattn_Wq, L0_xattn_Wk, L0_xattn_Wv,
           L0_xattn_Wo, L0_ffn_gate_w, L0_ffn_w_gate, L0_ffn_w_up, L0_ffn_w_down, L1_attn_in_proj_w, L1_attn_conv_w,
           L1_attn_conv_b, L1_attn_x_proj_w, L1_attn_dt_proj_w, L1_attn_dt_proj_b, L1_attn_A_log, L1_attn_D_param,
           L1_attn_out_proj_w, L1_xattn_W_qkv, L1_xattn_b_qkv, L1_xattn_W_out, L1_xattn_b_out, L1_ffn_w1_w, L1_ffn_w1_s,
           L1_ffn_w2_w, L1_ffn_w2_s, L1_ffn_h1_w, L1_ffn_h1_s, L1_ffn_h2_w, L1_ffn_h2_s, L1_ffn_w3_w, L1_ffn_w3_s):
    import numpy as np
    from concourse import bacc
    from concourse.bass_utils import run_bass_kernel_spmd

    def rows(w):
        w = np.asarray(w)
        return np.ascontiguousarray(w.reshape(-1, P, w.shape[1]).transpose(1, 0, 2).reshape(P, -1))

    def vec(v):
        return np.ascontiguousarray(np.asarray(v).reshape(-1, P).T)

    def flat(w):
        w = np.asarray(w)
        return w.reshape(-1, w.shape[2])

    xp = np.asarray(L1_attn_x_proj_w)
    gap = np.zeros((LO - XDB, INNER), np.float32)
    a = {
        "x": np.asarray(x),
        "ctxT": np.ascontiguousarray(np.asarray(ctx_1024).reshape(BATCH, KEYS, KD, P).transpose(3, 2, 0, 1).reshape(P, -1)),
        "a_Wq": rows(L0_attn_Wq), "a_Wk": rows(L0_attn_Wk), "a_Wv": rows(L0_attn_Wv), "a_Wg": rows(L0_attn_Wg),
        "a_Wo": rows(L0_attn_Wo), "a_W1": rows(L0_attn_W1), "a_W2": rows(L0_attn_W2),
        "x0_Wq": rows(np.asarray(L0_xattn_Wq).T), "x0_Wk": rows(np.asarray(L0_xattn_Wk).T),
        "x0_Wv": rows(np.asarray(L0_xattn_Wv).T), "x0_Wo": rows(np.asarray(L0_xattn_Wo).T),
        "e_gate": rows(np.asarray(L0_ffn_gate_w).T), "e_Wg": rows(flat(L0_ffn_w_gate).T),
        "e_Wu": rows(flat(L0_ffn_w_up).T), "e_Wd": rows(flat(np.asarray(L0_ffn_w_down).transpose(0, 2, 1))),
        "v_ln1_g": vec(L0_attn_ln1_g), "v_ln1_b": vec(L0_attn_ln1_b), "v_bq": vec(L0_attn_bq), "v_bk": vec(L0_attn_bk),
        "v_bv": vec(L0_attn_bv), "v_bg": vec(L0_attn_bg),
        "v_decay": vec(np.repeat(np.asarray(L0_attn_decay_logit), HID // HEADS)),
        "v_ln2_g": vec(L0_attn_ln2_g), "v_ln2_b": vec(L0_attn_ln2_b), "v_b1": vec(L0_attn_b1),
        "r_bo": np.asarray(L0_attn_bo), "r_b2": np.asarray(L0_attn_b2),
        "m_in": rows(np.asarray(L1_attn_in_proj_w).T), "m_xp": rows(np.concatenate([xp, gap, xp]).T),
        "m_dtw": np.ascontiguousarray(np.asarray(L1_attn_dt_proj_w).T), "m_out": rows(np.asarray(L1_attn_out_proj_w).T),
        "v_convw": rows(np.asarray(L1_attn_conv_w)[:, 0, :]), "v_convb": vec(L1_attn_conv_b), "v_dtb": vec(L1_attn_dt_proj_b),
        "v_alog": rows(L1_attn_A_log), "v_D": vec(L1_attn_D_param),
        "x1_Wqkv": rows(L1_xattn_W_qkv), "v_bqkv": vec(L1_xattn_b_qkv), "x1_Wo": rows(L1_xattn_W_out),
        "r_bout": np.asarray(L1_xattn_b_out),
        "f_w1": rows(np.asarray(L1_ffn_w1_w).T), "f_w2": rows(np.asarray(L1_ffn_w2_w).T), "f_h1": rows(np.asarray(L1_ffn_h1_w).T),
        "f_h2": rows(np.asarray(L1_ffn_h2_w).T), "f_w3": rows(np.asarray(L1_ffn_w3_w).T),
        "v_s1": vec(L1_ffn_w1_s), "v_s2": vec(L1_ffn_w2_s), "v_s3": vec(L1_ffn_h1_s), "v_s4": vec(L1_ffn_h2_s),
        "r_s5": np.asarray(L1_ffn_w3_s),
    }
    nc = bacc.Bacc("TRN2", target_bir_lowering=False, num_devices=1)
    t = {n: nc.dram_tensor("in_" + n, v.shape, F32, kind="ExternalInput").ap() for n, v in a.items()}
    mid = nc.dram_tensor("mid", (TOK, D), F32, kind="Internal").ap()
    kz_dram = nc.dram_tensor("kz_dram", (BATCH, P, KD * ROWS), F32, kind="Internal").ap()
    vz_dram = nc.dram_tensor("vz_dram", (BATCH, P, KD * 5 * P), F32, kind="Internal").ap()
    out = nc.dram_tensor("out", (BATCH, SEQ, D), F32, kind="ExternalOutput").ap()
    decoder(nc, t, mid, kz_dram, vz_dram, out)
    r = run_bass_kernel_spmd(nc, [{"in_" + n: v for n, v in a.items()}], core_ids=[0])
    return r.results[0]["out"]
```

```python
from contextlib import ExitStack

import concourse.bass as bass
from concourse import mybir

F32 = mybir.dt.float32
BF16 = mybir.dt.bfloat16
ACT = mybir.ActivationFunctionType
ALU = mybir.AluOpType
AX = mybir.AxisListType.X

P = 128
D = 256
KD = D // P
BATCH, SEQ = 2, 1024
TOK = BATCH * SEQ
CH = 256
NCH = TOK // CH
CPB = SEQ // CH
TT = CH // P
BANK = 512
MPB = BANK // CH
RING = 4
HID = 1024
KH = HID // P
NE = 8
KEYS = 77
HEADS, DH = 16, 16
HPT = P // DH
ROWS = HPT * KEYS
BLK = [P, P, P, P, ROWS - 4 * P]
HPB = 4
INNER, NST, DTR, TAPS = 512, 16, 16, 4
KI = INNER // P
BC = 2 * NST
PARTS = 3
EPS = 1e-5


class Signal:

    def __init__(self, sem, per):
        self.sem, self.per, self.seen = sem, per, 0

    def by(self, instruction):
        self.seen += 1
        instruction.then_inc(self.sem, 1)

    def wait(self, eng, c, k):
        assert k >= 1, (self.sem, k)
        eng.wait_ge(self.sem, c * self.per + k)


class Ring:

    def __init__(self, plan, psum, first, full, freed):
        self.psum, self.first, self.full, self.freed = psum, first, full, freed
        self.slots, self.where = [], {}
        for name, reader, n in plan:
            self.where[name] = len(self.slots)
            self.slots += [reader] * n
        self.given = {"act": 0, "dve": 0}
        full.per = sum(r is not None for r in self.slots)
        for r in freed:
            freed[r].per = self.slots.count(r)

    def bank(self, name, n=1):
        b = self.first + self.where[name] % RING
        return self.psum[:, b, :] if n == 1 else self.psum[:, b:b + n, :]

    def acquire(self, pe, c, name, n=1):
        own = range(self.where[name], self.where[name] + n)
        for r in ("act", "dve"):
            old = [s - RING for s in own if s >= RING and self.slots[s - RING] == r]
            last = [max(o for o in range(len(self.slots)) if o % RING == s % RING and self.slots[o]) for s in own if s < RING]
            last = [s for s in last if self.slots[s] == r]
            if old:
                self.freed[r].wait(pe, c, self.freed[r].per + self.slots[:old[-1] + 1].count(r))
            elif last:
                self.freed[r].wait(pe, c, self.slots[:max(last) + 1].count(r))
        return self.bank(name, n)

    def start(self, pe):
        for r in self.freed.values():
            pe.sem_inc(r.sem, r.per)

    def filled(self, eng, c, name, n=1):
        s = self.where[name] + n - 1
        self.full.wait(eng, c, sum(r is not None for r in self.slots[:s + 1]))
        return self.bank(name, n)

    def free(self, instruction, name, last=0):
        s = self.where[name] + last
        r = self.slots[s]
        assert self.slots[:s].count(r) == self.given[r] % self.freed[r].per, (name, self.given)
        self.given[r] += 1
        self.freed[r].by(instruction)


def two(ap):
    return ap.rearrange("p (k n) -> p k n", k=2)


def decoder(nc, t, mid, kz_dram, vz_dram, out):
    top = ExitStack()
    with top:
        def alloc(stack, name, shape, dt=F32):
            return stack.enter_context(nc.sbuf_tensor(name, shape, dt))

        def sem(name):
            return top.enter_context(nc.semaphore(name))

        ident = alloc(top, "ident", [P, P])
        head_mask = alloc(top, "head_mask", [P, HPT])
        row_mask = alloc(top, "row_mask", [P, 5, P])
        first_key = alloc(top, "first_key", [P, NE])
        half_neg = alloc(top, "half_neg", [P, TT])
        sel8 = alloc(top, "sel8", [P, NE], BF16)
        sel_bc = alloc(top, "sel_bc", [P, BC], BF16)
        keep = alloc(top, "keep", [P, NCH + 1])
        kz = alloc(top, "kz", [P, KD, HPT, KEYS])
        vz = alloc(top, "vz", [P, KD, 5, P])
        psum = top.enter_context(nc.psum_tensor("psum", [P, 8, BANK], F32))

        s_const = sem("constants_made")
        s_setup = sem("setup_on_dve")

        def load(eng, dst, src, s):
            eng.dma_start(dst, src).then_inc(s, 16)

        class Stage:

            def __init__(self, tag, plan, first_bank, per, stack):
                self.s = {n: Signal(sem(f"{tag}_{n}"), k) for n, k in per.items()}
                full = Signal(sem(f"{tag}_banks_full"), 0)
                freed = {"act": Signal(sem(f"{tag}_act_freed"), 0), "dve": Signal(sem(f"{tag}_dve_freed"), 0)}
                self.ring = Ring(plan, psum, first_bank, full, freed)
                self.r = alloc(stack, f"{tag}_r", [P, TT, D])
                self.xT = alloc(stack, f"{tag}_xT", [P, KD, CH])
                self.norm = {}
                for lane in ("", "in_")[:1 + ("in_var" in per)]:
                    self.norm[lane] = [alloc(stack, f"{tag}_{lane}{n}", [P, TT, *k])
                                       for n, k in (("stats", [6]), ("mv", [2]), ("ve", []), ("rstd", []))]

            def check(self, **ahead):
                bad = [(n, s.seen, s.per) for n, s in [*self.s.items(), ("full", self.ring.full), *self.ring.freed.items()]
                       if s.seen != 2 * s.per + ahead.get(n, 0)]
                assert not bad, bad

            def ln_dve(self, dve, c, k, src, dst, lane=""):
                stats, mv, ve, rstd = self.norm[lane]
                for i in range(TT):
                    dve.bn_stats(stats[:, i, :], src[:, i, :])
                dve.drain()
                for i in range(TT):
                    dve.bn_aggr(mv[:, i, :], stats[:, i, :])
                dve.drain()
                self.s[lane + "var"].by(dve.tensor_scalar(ve[:, :], mv[:, :, 1], EPS, None, op0=ALU.add))
                self.s[lane + "rstd"].wait(dve, c, k)
                for i in range(TT):
                    ins = dve.tensor_scalar(dst[:, i, :], src[:, i, :], mv[:, i, 0:1], rstd[:, i:i + 1],
                                            op0=ALU.subtract, op1=ALU.mult)
                self.s[lane + "xn"].by(ins)

            def ln_pool(self, pool, c, k, lane=""):
                _, _, ve, rstd = self.norm[lane]
                self.s[lane + "var"].wait(pool, c, k)
                self.s[lane + "rstd"].by(pool.tensor_tensor(out=rstd[:, :], in0=ve[:, :], in1=half_neg[:, :], op=ALU.pow))

            def residual_ln(self, dve, c, name, resid, k, dst):
                ps = self.ring.filled(dve, c, name)
                self.ring.free(dve.tensor_tensor(self.r[:], two(ps), resid[:], ALU.add), name)
                dve.drain()
                self.ln_dve(dve, c, k, self.r, dst)

            def transpose_pe(self, pe, c, name, src):
                ps = self.ring.acquire(pe, c, name)
                for kd in range(KD):
                    for i in range(TT):
                        last = pe.transpose(ps[:, kd * CH + i * P:kd * CH + (i + 1) * P], src[:, i, kd * P:(kd + 1) * P], ident[:])
                self.ring.full.by(last)

            def transpose_act(self, act, c, name, gain=None, bias=None):
                ps = self.ring.filled(act, c, name)
                if gain is None:
                    self.ring.free(act.activation(self.xT[:], two(ps), ACT.Copy), name)
                else:
                    for kd in range(KD):
                        ins = act.activation(self.xT[:, kd, :], two(ps)[:, kd, :], ACT.Identity, bias=bias[:, kd:kd + 1],
                                             scale=gain[:, kd:kd + 1])
                    self.ring.free(ins, name)
                self.s["xT"].by(act.drain())

            def product(self, pe, c, name, w, pair, rhs, kt):
                ps = self.ring.acquire(pe, c, name)
                for j in range(MPB):
                    m = pair * MPB + j
                    for k in range(kt):
                        last = pe.matmul(ps[:, j * CH:(j + 1) * CH], w[:, k, m * P:(m + 1) * P], rhs[:, k, :],
                                         start=k == 0, stop=k == kt - 1)
                self.ring.full.by(last)

            def product_tok(self, pe, c, name, actT, w, kt, late=None):
                ps = self.ring.acquire(pe, c, name)
                for i in range(TT):
                    for k in range(kt):
                        if late and (i, k) == (0, late[0]):
                            late[1]()
                        last = pe.matmul(ps[:, i * D:(i + 1) * D], actT[:, k, i * P:(i + 1) * P], w[:, k, :],
                                         start=k == 0, stop=k == kt - 1)
                self.ring.full.by(last)

        class Attention(Stage):

            SIGNALS = dict(qT=1, centred=TT, exps=TT, inv_sums=TT, probs=TT, probsT=TT, oaT=1)
            PLAN = [("xTq", "act", 1), ("xq", "act", 1)]
            PLAN += [(f"s{i}_{h}", "dve", 2) for i in range(TT) for h in range(2)]
            for i in range(TT):
                PLAN += [(f"pT{i}_0", "act", 1), (f"pT{i}_1", "act", 1), (f"pT{i}_2", "act", 1), (f"pv{i}", "act", 1)]
            PLAN += [("ao", "dve", 1)]

            def __init__(self, tag, plan, first_bank, per, stack, scratch):
                super().__init__(tag, self.PLAN + plan, first_bank, dict(self.SIGNALS, **per), stack)
                self.qT = alloc(stack, f"{tag}_qT", [P, KD, CH])
                self.oaT = alloc(stack, f"{tag}_oaT", [P, KD, CH])
                self.mx = alloc(stack, f"{tag}_mx", [P, 2, HEADS])
                self.rs = alloc(stack, f"{tag}_rs", [P, 2, HEADS])
                self.p = alloc(scratch, f"{tag}_p", [P, 2, HEADS * KEYS])
                self.pt = alloc(scratch, f"{tag}_pt", [P, 3, BANK])

            def scores_pe(self, pe, c, i):
                for h in range(2):
                    ps = self.ring.acquire(pe, c, f"s{i}_{h}", 2)
                    for b in range(2):
                        self.ring.full.by(pe.matmul(ps[:, b, 0:HPB * KEYS], self.qT[:, h, i * P:(i + 1) * P],
                                                    kz[:, h, b * HPB:(b + 1) * HPB, :].rearrange("p h k -> p (h k)"),
                                                    start=True, stop=True))

            def turn_pe(self, pe, c, i):
                self.s["probs"].wait(pe, c, i + 1)
                for g in range(3):
                    ps = self.ring.acquire(pe, c, f"pT{i}_{g}")
                    for pos in range(4 if g < 2 else 2):
                        kd, blk = (g, pos) if g < 2 else (pos, 4)
                        c0, n = kd * ROWS + blk * P, BLK[blk]
                        last = pe.transpose(ps[0:n, pos * P:(pos + 1) * P], self.p[:, i % 2, c0:c0 + n], ident[:])
                    self.ring.full.by(last)

            def mix_pe(self, pe, c, i):
                self.s["probsT"].wait(pe, c, i + 1)
                ps = self.ring.acquire(pe, c, f"pv{i}")
                for kd in range(KD):
                    for blk, n in enumerate(BLK):
                        g, pos = (kd, blk) if blk < 4 else (2, kd)
                        last = pe.matmul(ps[:, kd * P:(kd + 1) * P], vz[0:n, kd, blk, :],
                                         self.pt[0:n, g, pos * P:(pos + 1) * P], start=blk == 0, stop=blk == 4)
                self.ring.full.by(last)

            def query_act(self, act, c, bias=None):
                ps = self.ring.filled(act, c, "xq")
                for kd in range(KD):
                    b = 0.0 if bias is None else bias[:, kd:kd + 1]
                    ins = act.activation(self.qT[:, kd, :], two(ps)[:, kd, :], ACT.Identity, bias=b)
                self.ring.free(ins, "xq")
                self.s["qT"].by(act.drain())

            def exp_act(self, act, c, i):
                self.s["centred"].wait(act, c, i + 1)
                self.s["exps"].by(act.activation(self.p[:, i % 2, :], self.p[:, i % 2, :], ACT.Exp, scale=DH ** -0.5))

            def move_act(self, act, c, i):
                for g in range(3):
                    n, w = (P, BANK) if g < 2 else (BLK[4], 2 * P)
                    ps = self.ring.filled(act, c, f"pT{i}_{g}")
                    self.ring.free(act.activation(self.pt[0:n, g, 0:w], ps[0:n, 0:w], ACT.Copy), f"pT{i}_{g}")
                self.s["probsT"].by(act.drain())

            def mixed_act(self, act, c, i, bias=None):
                ps = self.ring.filled(act, c, f"pv{i}")
                for kd in range(KD):
                    b = 0.0 if bias is None else bias[:, kd:kd + 1]
                    ins = act.activation(self.oaT[:, kd, i * P:(i + 1) * P], ps[:, kd * P:(kd + 1) * P], ACT.Identity, bias=b)
                self.ring.free(ins, f"pv{i}")
                if i == TT - 1:
                    self.s["oaT"].by(act.drain())

            def centre_dve(self, dve, c, i):
                for h in range(2):
                    ps = self.ring.filled(dve, c, f"s{i}_{h}", 2)[:, :, 0:HPB * KEYS].rearrange("p b (h k) -> p b h k", h=HPB)
                    m = self.mx[:, i % 2, h * HPT:(h + 1) * HPT].rearrange("p (b h) -> p b h", b=2)
                    dve.tensor_reduce(m, ps, axis=AX, op=ALU.max)
                    dve.drain()
                    for b in range(2):
                        c0 = h * ROWS + b * HPB * KEYS
                        ins = dve.tensor_tensor(self.p[:, i % 2, c0:c0 + HPB * KEYS].rearrange("p (h k) -> p h k", h=HPB),
                                                ps[:, b], m[:, b, :].unsqueeze(2).to_broadcast([P, HPB, KEYS]), ALU.subtract)
                        self.ring.free(ins, f"s{i}_{h}", b)
                self.s["centred"].by(dve.drain())

            def sums_dve(self, dve, c, i):
                self.s["exps"].wait(dve, c, i + 1)
                r = self.rs[:, i % 2, :]
                dve.tensor_reduce(r, self.p[:, i % 2, :].rearrange("p (h k) -> p h k", h=HEADS), axis=AX, op=ALU.add)
                dve.drain()
                self.s["inv_sums"].by(dve.reciprocal(r, r))

            def scale_pool(self, pool, c, i):
                self.s["inv_sums"].wait(pool, c, i + 1)
                v = self.p[:, i % 2, :].rearrange("p (h k) -> p h k", h=HEADS)
                self.s["probs"].by(pool.tensor_tensor(out=v, in0=v, in1=self.rs[:, i % 2, :].unsqueeze(2).to_broadcast([P, HEADS, KEYS]),
                                                      op=ALU.mult))

        def kv_setup(tag, stack, w_k, w_v, k_bias, loaded):
            ctx_sb = alloc(stack, f"{tag}ctx_sb", [P, KD, BATCH, KEYS])
            ctx_rep = alloc(stack, f"{tag}ctx_rep", [P, KD, BATCH, HPT, KEYS])
            k_sb = alloc(stack, f"{tag}k_sb", [P, KD, BATCH, KEYS])
            kz_sb = alloc(stack, f"{tag}kz_sb", [P, BATCH, KD, HPT, KEYS])
            vz_sb = alloc(stack, f"{tag}vz_sb", [P, BATCH, KD, 5, P])
            s_ctx, s_rep, s_kp, s_ks = (sem(f"{tag}_{n}") for n in ("ctx", "ctx_rep", "k_psum", "k_sb"))
            s_vp, s_vf, s_made, s_st = (sem(f"{tag}_{n}") for n in ("v_psum", "v_freed", "kzvz_made", "kzvz_stored"))

            def on_sync(sp):
                load(sp, ctx_sb[:].rearrange("p k b s -> p (k b s)"), t["ctxT"], s_ctx)

            def on_pe(pe):
                pe.wait_ge(s_ctx, 16)
                for s_loaded in loaded:
                    pe.wait_ge(s_loaded, 16)
                for m in range(KD):
                    for k in range(KD):
                        last = pe.matmul(psum[:, m, 0:BATCH * KEYS], w_k[:, k, m * P:(m + 1) * P],
                                         ctx_sb[:, k].rearrange("p b s -> p (b s)"), start=k == 0, stop=k == KD - 1)
                    last.then_inc(s_kp, 1)
                pe.wait_ge(s_rep, 1)
                for n in range(BATCH * 5):
                    b, blk = n // 5, n % 5
                    if n >= 4:
                        pe.wait_ge(s_vf, n - 3)
                    for k in range(KD):
                        rows = ctx_rep[:, k, b].rearrange("p h s -> p (h s)")[:, blk * P:blk * P + BLK[blk]]
                        last = pe.matmul(psum[0:BLK[blk], 2 + n % 4, 0:D], rows, w_v[:, k, 0:D], start=k == 0, stop=k == KD - 1)
                    last.then_inc(s_vp, 1)

            def on_act(act):
                for m in range(KD):
                    act.wait_ge(s_kp, m + 1)
                    b = 0.0 if k_bias is None else k_bias[:, m:m + 1]
                    act.activation(k_sb[:, m].rearrange("p b s -> p (b s)"), psum[:, m, 0:BATCH * KEYS],
                                   ACT.Identity, bias=b).then_inc(s_ks, 1)

            def on_dve(dve):
                dve.wait_ge(s_ctx, 16)
                for k in range(KD):
                    for b in range(BATCH):
                        dve.tensor_copy(ctx_rep[:, k, b], ctx_sb[:, k, b].unsqueeze(1).to_broadcast([P, HPT, KEYS]))
                dve.drain().then_inc(s_rep, 1)
                dve.wait_ge(s_ks, KD)
                dve.wait_ge(s_const, 1)
                for b in range(BATCH):
                    for m in range(KD):
                        dve.tensor_tensor(kz_sb[:, b, m], k_sb[:, m, b].unsqueeze(1).to_broadcast([P, HPT, KEYS]),
                                          head_mask[:, :].unsqueeze(2).to_broadcast([P, HPT, KEYS]), ALU.mult)
                dve.memset(vz_sb[:, :, :, 4, :], 0.0)
                dve.drain()
                for n in range(BATCH * 5):
                    b, blk = n // 5, n % 5
                    r = BLK[blk]
                    dve.wait_ge(s_vp, n + 1)
                    dve.tensor_tensor(vz_sb[0:r, b, :, blk, :], psum[0:r, 2 + n % 4, 0:D].rearrange("p (k c) -> p k c", k=KD),
                                      row_mask[0:r, blk, :].unsqueeze(1).to_broadcast([r, KD, P]), ALU.mult).then_inc(s_vf, 1)
                dve.drain().then_inc(s_made, 1)

            def store(sp):
                sp.wait_ge(s_made, 1)
                sp.dma_start(kz_dram.rearrange("b p n -> p b n"), kz_sb[:].rearrange("p b m h s -> p b (m h s)")).then_inc(s_st, 16)
                sp.dma_start(vz_dram.rearrange("b p n -> p b n"), vz_sb[:].rearrange("p b m k c -> p b (m k c)")).then_inc(s_st, 16)
                sp.wait_ge(s_st, 32)

            return on_sync, on_pe, on_act, on_dve, store

        def load_kv(sp, b, s):
            sp.dma_start(kz[:].rearrange("p m h s -> p (m h s)"), kz_dram[bass.ds(b, 1), :, :].rearrange("b p n -> p (b n)")).then_inc(s, 16)
            sp.dma_start(vz[:].rearrange("p m k c -> p (m k c)"), vz_dram[bass.ds(b, 1), :, :].rearrange("b p n -> p (b n)")).then_inc(s, 16)

        x_dram = t["x"].rearrange("b (t p) d -> (b t) p d", p=P)
        mid_v = mid.rearrange("(t p) d -> t p d", p=P)
        out_v = out.rearrange("b (t p) d -> (b t) p d", p=P)

        def sync_loop(sp, first, second, src, x_in, x_out, dst, n_ln, s_x, s_kv, s_stored, s_turns):
            def chunk_in(it, tile):
                first.s["x_in_free"].wait(sp, it, first.s["x_in_free"].per)
                sp.dma_start(x_in[:], src[bass.ds(tile, TT), :, :].rearrange("t p d -> p t d")).then_inc(s_x, 16)

            def chunk_out(c, tile):
                second.s["xn"].wait(sp, c, n_ln)
                sp.dma_start(dst[bass.ds(tile, TT), :, :].rearrange("t p d -> p t d"), x_out[:]).then_inc(s_stored, 16)

            sp.dma_start(x_in[:], src[0:TT, :, :].rearrange("t p d -> p t d")).then_inc(s_x, 16)
            load_kv(sp, 0, s_kv)
            sp.sem_inc(s_stored, 16)
            chunk_in(0, TT)
            with sp.Fori(1, NCH) as it:
                tile_next, tile_out, c = sp.snap((it + 1) % NCH * TT), sp.snap((it - 1) * TT), sp.snap(it - 1)
                b = sp.snap(it // CPB)
                chunk_in(it, tile_next)
                second.s["oaT"].wait(sp, c, 1)
                load_kv(sp, b, s_kv)
                chunk_out(c, tile_out)
                sp.sem_inc(s_turns, 1)
            chunk_out(NCH - 1, (NCH - 1) * TT)
            sp.wait_ge(s_stored, 16 * (NCH + 1))
            sp.wait_ge(s_x, 16 * (NCH + 1))

        la = ExitStack()
        with la:
            WA = {"a_Wq": (KD, HID), "a_Wk": (KD, HID), "a_Wv": (KD, HID), "a_Wg": (KD, HID), "a_Wo": (KH, D),
                  "a_W1": (KD, HID), "a_W2": (KH, D), "x0_Wq": (KD, D), "x0_Wk": (KD, D), "x0_Wv": (KD, D),
                  "x0_Wo": (KD, D), "e_gate": (KD, NE), "e_Wg": (KD, HID), "e_Wu": (KD, HID), "e_Wd": (NE, D)}
            ORDER_A = ["x0_Wk", "x0_Wv", "a_Wk", "a_Wg", "a_Wv", "a_Wq", "a_Wo", "a_W1", "a_W2", "x0_Wq", "x0_Wo",
                       "e_gate", "e_Wg", "e_Wu", "e_Wd"]
            VA = {"v_ln1_g": KD, "v_ln1_b": KD, "v_bq": KH, "v_bk": KH, "v_bv": KH, "v_bg": KH, "v_decay": KH,
                  "v_ln2_g": KD, "v_ln2_b": KD, "v_b1": KH}
            s_vec_a, s_decay = sem("a_vectors_loaded"), sem("decay_made")
            s_w = {n: sem("loaded_" + n) for n in WA}
            n_vec_a = 16 * (len(VA) + 2)
            wa = {n: alloc(la, "sb_" + n, [P, *WA[n]]) for n in WA}
            va = {n: alloc(la, "sb_" + n, [P, k]) for n, k in VA.items()}
            bo_row = alloc(la, "bo_row", [P, D])
            b2_row = alloc(la, "b2_row", [P, D])
            decay = alloc(la, "decay", [P, KH])
            carry = alloc(la, "carry", [P, KH])
            x_in = alloc(la, "x_in", [P, TT, D])
            x_n = alloc(la, "x_n", [P, TT, D])
            x_n2 = alloc(la, "x_n2", [P, TT, D])
            x_bo = alloc(la, "x_bo", [P, TT, D])
            x_b2 = alloc(la, "x_b2", [P, TT, D])
            x_1 = alloc(la, "x_1", [P, TT, D])
            x_2 = alloc(la, "x_2", [P, TT, D])
            x_3 = alloc(la, "x_3", [P, TT, D])
            with ExitStack() as stack:
                kv0 = kv_setup("kv0", stack, wa["x0_Wk"], wa["x0_Wv"], None, (s_w["x0_Wk"], s_w["x0_Wv"]))
            hT = alloc(la, "hT", [P, KH, CH])
            k_sb = alloc(la, "k_sb", [P, 2, MPB, CH])
            g_sb = alloc(la, "g_sb", [P, 2, MPB, CH])
            kv = alloc(la, "kv", [P, MPB, CH])
            st = alloc(la, "st", [P, MPB, CH])
            qg = alloc(la, "qg", [P, MPB, CH])
            rB = alloc(la, "rB", [P, NE, CH])
            he = alloc(la, "he", [P, NE, CH])
            XM = 3
            xm = alloc(la, "xm", [P, XM, KD, CH])
            sg = alloc(la, "sg", [P, CH])
            hu = alloc(la, "hu", [P, CH])
            lg = alloc(la, "lg", [P, TT, NE])
            eq = alloc(la, "eq", [P, TT, NE])
            rw = alloc(la, "rw", [P, TT, 32 * PARTS])
            r_hi = alloc(la, "r_hi", [P, 2, TT, NE], BF16)
            top1 = alloc(la, "top1", [P, TT])
            sgm = alloc(la, "sgm", [P, TT])
            fk = alloc(la, "fk", [P, TT])
            rT = alloc(la, "rT", [32 * PARTS, CH], BF16)
            NP = KH // MPB
            plan = [("xT1", "act", 1)]
            for j in range(NP):
                plan += [(f"k{j}", "act", 1), (f"g{j}", "act", 1), (f"v{j}", "dve", 1), (f"q{j}", "dve", 1)]
            plan += [("ao", "dve", 1), ("xT2", "act", 1)] + [(f"f{j}", "act", 1) for j in range(NP)] + [("fo", "dve", 1)]
            F = Stage("attnffn", plan, 0, dict(in_var=1, in_rstd=1, in_xn=1, var=2, rstd=2, xn=2, xT=2, x_in_free=2, kg=NP, kvd=NP, oT=NP, resid=3, gelu=1), la)
            plan = [("xTe", "act", 1), ("lg", "dve", 1), ("rT", "act", 1)] + [(f"rb{j}", "act", 1) for j in range(NE // 2)]
            plan += [("gu", "dve", 1), ("ed", "dve", 1)]
            X = Attention("xmoe", plan, 4, dict(var=2, rstd=2, xn=2, xT=2, top=1, sig=1, route=1, rT=1, rb=NE // 2, xm=NE,
                                                xmu=NE - 1, silu=1, he=NE), la, la)
            s_x, s_kv, s_stored, s_turns = sem("A_x_in"), sem("A_kv_in"), sem("A_stored"), sem("A_sync_turns")

            with nc.Block() as block:
                @block.sync
                def _(sp):
                    kv0[0](sp)
                    for n in ORDER_A[:2]:
                        load(sp, wa[n][:].rearrange("p k n -> p (k n)"), t[n], s_w[n])
                    for n in VA:
                        load(sp, va[n][:], t[n], s_vec_a)
                    for dst, n in ((bo_row, "r_bo"), (b2_row, "r_b2")):
                        load(sp, dst[:], t[n].unsqueeze(0).to_broadcast([P, D]), s_vec_a)
                    for n in ORDER_A[2:]:
                        load(sp, wa[n][:].rearrange("p k n -> p (k n)"), t[n], s_w[n])
                    kv0[4](sp)
                    sync_loop(sp, F, X, x_dram, x_in, x_3, mid_v, 2, s_x, s_kv, s_stored, s_turns)

                @block.gpsimd
                def _(pool):
                    pool.memset(ident[:], 0.0)
                    pool.memset(head_mask[:], 1.0)
                    pool.memset(row_mask[:], 1.0)
                    pool.memset(half_neg[:], -0.5)
                    pool.memset(rw[:], 0.0)
                    for e in range(NE):
                        pool.memset(first_key[:, e:e + 1], float(NE - e))
                    for c in range(NCH + 1):
                        pool.memset(keep[:, c:c + 1], float(c % CPB != CPB - 1))
                    pool.drain()
                    pool.affine_select(out=ident[:], in_=ident[:], compare_op=ALU.not_equal, fill=1.0, base=0,
                                       pattern=[[-1, P]], channel_multiplier=1)
                    pool.affine_select(out=head_mask[:], in_=head_mask[:], compare_op=ALU.is_ge, fill=0.0, base=0,
                                       pattern=[[-DH, HPT]], channel_multiplier=1)
                    v = row_mask[:].rearrange("p k (h c) -> p k h c", c=DH)
                    pool.affine_select(out=v, in_=v, compare_op=ALU.is_ge, fill=0.0, base=0,
                                       pattern=[[P, 5], [-KEYS, HPT], [0, DH]], channel_multiplier=1)
                    pool.drain()
                    pool.affine_select(out=head_mask[:], in_=head_mask[:], compare_op=ALU.is_ge, fill=0.0, base=DH - 1,
                                       pattern=[[DH, HPT]], channel_multiplier=-1)
                    pool.affine_select(out=v, in_=v, compare_op=ALU.is_ge, fill=0.0, base=KEYS - 1,
                                       pattern=[[-P, 5], [KEYS, HPT], [0, DH]], channel_multiplier=-1)
                    pool.drain().then_inc(s_const, 1)
                    pool.wait_ge(s_vec_a, n_vec_a)

                    def attn_residuals(c):
                        bc = bo_row[:].unsqueeze(1).to_broadcast([P, TT, D])
                        pool.wait_ge(s_x, c * 16 + 16)
                        S = F.s["resid"]
                        S.by(pool.tensor_tensor(out=x_bo[:], in0=x_in[:], in1=bc, op=ALU.add))
                        bc = b2_row[:].unsqueeze(1).to_broadcast([P, TT, D])
                        S.by(pool.tensor_tensor(out=x_b2[:], in0=x_in[:], in1=bc, op=ALU.add))
                        F.s["x_in_free"].by(pool.drain())

                    def ffn_residual(c):
                        F.s["xn"].wait(pool, c, 1)
                        F.s["resid"].by(pool.tensor_tensor(out=x_b2[:], in0=x_b2[:], in1=F.r[:], op=ALU.add))

                    F.ln_pool(pool, 0, 1, "in_")
                    attn_residuals(0)
                    F.ln_pool(pool, 0, 1)
                    ffn_residual(0)
                    F.ln_pool(pool, 1, 1, "in_")
                    F.ln_pool(pool, 0, 2)
                    with pool.Fori(1, NCH) as it:
                        c = it - 1
                        attn_residuals(it)
                        X.scale_pool(pool, c, 0)
                        X.scale_pool(pool, c, 1)
                        X.ln_pool(pool, c, 1)
                        F.ln_pool(pool, it, 1)
                        ffn_residual(it)
                        F.ln_pool(pool, it + 1, 1, "in_")
                        F.ln_pool(pool, it, 2)
                        X.ln_pool(pool, c, 2)
                    for i in range(TT):
                        X.scale_pool(pool, NCH - 1, i)
                    X.ln_pool(pool, NCH - 1, 1)
                    X.ln_pool(pool, NCH - 1, 2)

                @block.vector
                def _(dve):
                    kv0[3](dve)
                    dve.memset(carry[:], 0.0)
                    for sel, n, at in ((sel8, NE, 0), (sel_bc, BC, 32)):
                        dve.tensor_tensor(sel[:], ident[:, at:at + n], ident[:, at + 32:at + 32 + n], ALU.add)
                        dve.drain()
                        dve.tensor_tensor(sel[:], sel[:], ident[:, at + 64:at + 64 + n], ALU.add)
                    dve.drain().then_inc(s_setup, 1)
                    dve.wait_ge(s_vec_a, n_vec_a)
                    dve.wait_ge(s_decay, 1)
                    S, ring, T, ringx = F.s, F.ring, X.s, X.ring

                    def begin(c):
                        dve.wait_ge(s_x, c * 16 + 16)
                        F.ln_dve(dve, c, 1, x_in, x_n, "in_")
                        S["x_in_free"].by(dve.drain())

                    def linear_attention(c, j):
                        S["kg"].wait(dve, c, j + 1)
                        ps = two(ring.filled(dve, c, f"v{j}"))
                        for i in range(MPB):
                            m = j * MPB + i
                            ins = dve.scalar_tensor_tensor(kv[:, i, :], ps[:, i, :], va["v_bv"][:, m:m + 1], k_sb[:, j % 2, i, :],
                                                           op0=ALU.add, op1=ALU.mult)
                        ring.free(ins, f"v{j}")
                        dve.drain()
                        for i in range(MPB):
                            m = j * MPB + i
                            dve.tensor_tensor_scan(st[:, i, :], decay[:, m:m + 1].to_broadcast([P, CH]), kv[:, i, :],
                                                   carry[:, m:m + 1], ALU.mult, ALU.add)
                        ps = two(ring.filled(dve, c, f"q{j}"))
                        for i in range(MPB):
                            m = j * MPB + i
                            ins = dve.scalar_tensor_tensor(qg[:, i, :], ps[:, i, :], va["v_bq"][:, m:m + 1], g_sb[:, j % 2, i, :],
                                                           op0=ALU.add, op1=ALU.mult)
                        ring.free(ins, f"q{j}")
                        S["kvd"].by(dve.drain())
                        m = slice(j * MPB, (j + 1) * MPB)
                        dve.tensor_scalar(carry[:, m], st[:, :, CH - 1], keep[:, bass.ds(c, 1)], None, op0=ALU.mult)
                        S["oT"].by(dve.scalar_tensor_tensor(hT[:, m, :], st[:], 64 ** -0.5, qg[:], op0=ALU.mult, op1=ALU.mult))

                    def attention_out(c):
                        S["resid"].wait(dve, c, 1)
                        F.residual_ln(dve, c, "ao", x_bo, 1, x_n2)

                    def ffn_out(c):
                        S["resid"].wait(dve, c, 3)
                        F.residual_ln(dve, c, "fo", x_b2, 2, x_1)

                    def route(c):
                        ps = ringx.filled(dve, c, "lg")
                        ringx.free(dve.tensor_copy(lg[:], ps[:, 0:TT * NE].rearrange("p (t e) -> p t e", t=TT)), "lg")
                        dve.drain()
                        T["top"].by(dve.tensor_reduce(top1[:], lg[:], axis=AX, op=ALU.max))
                        dve.drain()
                        dve.tensor_tensor(eq[:], lg[:], top1[:].unsqueeze(2).to_broadcast([P, TT, NE]), ALU.is_equal)
                        dve.drain()
                        dve.tensor_tensor(eq[:], eq[:], first_key[:].unsqueeze(1).to_broadcast([P, TT, NE]), ALU.mult)
                        dve.drain()
                        dve.tensor_reduce(fk[:], eq[:], axis=AX, op=ALU.max)
                        dve.drain()
                        dve.tensor_tensor(eq[:], eq[:], fk[:].unsqueeze(2).to_broadcast([P, TT, NE]), ALU.is_equal)
                        dve.drain()
                        T["sig"].wait(dve, c, 1)
                        dve.tensor_tensor(lg[:], eq[:], sgm[:].unsqueeze(2).to_broadcast([P, TT, NE]), ALU.mult)
                        dve.drain()
                        dve.tensor_copy(r_hi[:, 0], lg[:])
                        dve.drain()
                        dve.tensor_copy(rw[:, :, 0:NE], r_hi[:, 0])
                        dve.tensor_tensor(eq[:], lg[:], r_hi[:, 0], ALU.subtract)
                        dve.drain()
                        dve.tensor_copy(r_hi[:, 1], eq[:])
                        dve.drain()
                        dve.tensor_copy(rw[:, :, 32:32 + NE], r_hi[:, 1])
                        T["route"].by(dve.tensor_tensor(rw[:, :, 64:64 + NE], eq[:], r_hi[:, 1], ALU.subtract))

                    def experts_in(c):
                        for e in range(NE):
                            T["rb"].wait(dve, c, e // 2 + 1)
                            if e >= XM:
                                T["xmu"].wait(dve, c, e - XM + 1)
                            T["xm"].by(dve.tensor_tensor(xm[:, e % XM], X.xT[:], rB[:, e, :].unsqueeze(1).to_broadcast([P, KD, CH]),
                                                         ALU.mult))

                    def experts_out(c):
                        dve.wait_ge(s_stored, c * 16 + 16)
                        X.residual_ln(dve, c, "ed", x_2, 2, x_3)

                    def experts_hidden(c):
                        T["silu"].wait(dve, c, 1)
                        ps = two(ringx.bank("gu"))
                        ringx.free(dve.tensor_tensor(hu[:], ps[:, 1, :], sg[:], ALU.mult), "gu")
                        dve.drain()
                        for e in range(NE):
                            T["he"].by(dve.scalar_tensor_tensor(he[:, e, :], rB[:, e, :], 0.0, hu[:], op0=ALU.is_gt, op1=ALU.mult))

                    begin(0)
                    for j in range(NP):
                        linear_attention(0, j)
                    attention_out(0)
                    begin(1)
                    ffn_out(0)
                    with dve.Fori(1, NCH) as it:
                        c = it - 1
                        linear_attention(it, 0)
                        linear_attention(it, 1)
                        X.centre_dve(dve, c, 0)
                        X.centre_dve(dve, c, 1)
                        X.sums_dve(dve, c, 0)
                        X.sums_dve(dve, c, 1)
                        linear_attention(it, 2)
                        linear_attention(it, 3)
                        X.residual_ln(dve, c, "ao", x_1, 1, x_2)
                        attention_out(it)
                        route(c)
                        experts_in(c)
                        begin(it + 1)
                        experts_hidden(c)
                        ffn_out(it)
                        experts_out(c)
                    c = NCH - 1
                    for i in range(TT):
                        X.centre_dve(dve, c, i)
                    for i in range(TT):
                        X.sums_dve(dve, c, i)
                    X.residual_ln(dve, c, "ao", x_1, 1, x_2)
                    route(c)
                    experts_in(c)
                    experts_hidden(c)
                    experts_out(c)

                @block.scalar
                def _(act):
                    kv0[2](act)
                    act.wait_ge(s_vec_a, n_vec_a)
                    act.activation(decay[:], va["v_decay"][:], ACT.Sigmoid).then_inc(s_decay, 1)
                    S, ring, T, ringx = F.s, F.ring, X.s, X.ring

                    def keys_gates(c, j):
                        if j >= 2:
                            S["kvd"].wait(act, c, j - 1)
                        for dst, name, func, bias in ((k_sb, "k", ACT.Identity, "v_bk"), (g_sb, "g", ACT.Sigmoid, "v_bg")):
                            ps = two(ring.filled(act, c, f"{name}{j}"))
                            for i in range(MPB):
                                m = j * MPB + i
                                ins = act.activation(dst[:, j % 2, i, :], ps[:, i, :], func, bias=va[bias][:, m:m + 1])
                            ring.free(ins, f"{name}{j}")
                        S["kg"].by(act.drain())

                    def ffn_hidden(c, js=range(NP)):
                        for j in js:
                            ps = two(ring.filled(act, c, f"f{j}"))
                            for i in range(MPB):
                                m = j * MPB + i
                                ins = act.activation(hT[:, m, :], ps[:, i, :], ACT.Gelu, bias=va["v_b1"][:, m:m + 1])
                            ring.free(ins, f"f{j}")
                        if js[-1] == NP - 1:
                            S["gelu"].by(act.drain())

                    def begin(c):
                        F.transpose_act(act, c, "xT1", va["v_ln1_g"], va["v_ln1_b"])

                    def gate_score(c):
                        T["top"].wait(act, c, 1)
                        T["sig"].by(act.activation(sgm[:], top1[:], ACT.Sigmoid))

                    def route_rows(c):
                        ps = ringx.filled(act, c, "rT")
                        ringx.free(act.activation(rT[:], ps[0:32 * PARTS, 0:CH], ACT.Copy), "rT")
                        T["rT"].by(act.drain())

                    def route_spread(c):
                        for j in range(NE // 2):
                            ps = two(ringx.filled(act, c, f"rb{j}"))
                            ringx.free(act.activation(rB[:, 2 * j:2 * j + 2, :], ps, ACT.Copy), f"rb{j}")
                            T["rb"].by(act.drain())

                    def experts_gate(c):
                        ps = two(ringx.filled(act, c, "gu"))
                        T["silu"].by(act.activation(sg[:], ps[:, 0, :], ACT.Silu))

                    begin(0)
                    for j in range(NP):
                        keys_gates(0, j)
                    F.transpose_act(act, 0, "xT2", va["v_ln2_g"], va["v_ln2_b"])
                    ffn_hidden(0)
                    begin(1)
                    with act.Fori(1, NCH) as it:
                        c = it - 1
                        keys_gates(it, 0)
                        X.transpose_act(act, c, "xTq")
                        keys_gates(it, 1)
                        X.query_act(act, c)
                        keys_gates(it, 2)
                        X.exp_act(act, c, 0)
                        X.exp_act(act, c, 1)
                        keys_gates(it, 3)
                        X.move_act(act, c, 0)
                        X.mixed_act(act, c, 0)
                        X.move_act(act, c, 1)
                        X.mixed_act(act, c, 1)
                        X.transpose_act(act, c, "xTe")
                        gate_score(c)
                        F.transpose_act(act, it, "xT2", va["v_ln2_g"], va["v_ln2_b"])
                        ffn_hidden(it, range(0, 2))
                        route_rows(c)
                        ffn_hidden(it, range(2, 4))
                        route_spread(c)
                        experts_gate(c)
                        begin(it + 1)
                    c = NCH - 1
                    X.transpose_act(act, c, "xTq")
                    X.query_act(act, c)
                    for i in range(TT):
                        X.exp_act(act, c, i)
                    for i in range(TT):
                        X.move_act(act, c, i)
                        X.mixed_act(act, c, i)
                    X.transpose_act(act, c, "xTe")
                    gate_score(c)
                    route_rows(c)
                    route_spread(c)
                    experts_gate(c)

                @block.tensor
                def _(pe):
                    pe.wait_ge(s_const, 1)
                    kv0[1](pe)
                    pe.wait_ge(s_setup, 1)
                    S, ring, T, ringx = F.s, F.ring, X.s, X.ring
                    ring.start(pe)
                    ringx.start(pe)

                    def begin(c):
                        S["in_xn"].wait(pe, c, 1)
                        F.transpose_pe(pe, c, "xT1", x_n)

                    def qkvg(c, j, fresh=False, which="kgvq"):
                        if j == 0:
                            S["xT"].wait(pe, c, 1)
                        for n in which:
                            if fresh and j == 0:
                                pe.wait_ge(s_w["a_W" + n], 16)
                            F.product(pe, c, f"{n}{j}", wa["a_W" + n], j, F.xT, KD)

                    def attention_out(c):
                        S["oT"].wait(pe, c, NP)
                        F.product_tok(pe, c, "ao", hT, wa["a_Wo"], KH)

                    def ffn_begin(c):
                        S["xn"].wait(pe, c, 1)
                        F.transpose_pe(pe, c, "xT2", x_n2)

                    def ffn_in(c, js=range(NP)):
                        S["xT"].wait(pe, c, 2)
                        for j in js:
                            F.product(pe, c, f"f{j}", wa["a_W1"], j, F.xT, KD)

                    def ffn_out(c):
                        S["gelu"].wait(pe, c, 1)
                        F.product_tok(pe, c, "fo", hT, wa["a_W2"], KH)

                    def cross_begin(c):
                        S["xn"].wait(pe, c, 2)
                        X.transpose_pe(pe, c, "xTq", x_1)

                    def query(c):
                        T["xT"].wait(pe, c, 1)
                        X.product(pe, c, "xq", wa["x0_Wq"], 0, X.xT, KD)

                    def cross_out(c):
                        T["oaT"].wait(pe, c, 1)
                        X.product_tok(pe, c, "ao", X.oaT, wa["x0_Wo"], KD)

                    def experts_begin(c):
                        T["xn"].wait(pe, c, 1)
                        X.transpose_pe(pe, c, "xTe", x_2)

                    def logits(c):
                        T["xT"].wait(pe, c, 2)
                        ps = ringx.acquire(pe, c, "lg")
                        for i in range(TT):
                            for k in range(KD):
                                last = pe.matmul(ps[:, i * NE:(i + 1) * NE], X.xT[:, k, i * P:(i + 1) * P], wa["e_gate"][:, k, :],
                                                 start=k == 0, stop=k == KD - 1)
                        ringx.full.by(last)

                    def route_rows(c):
                        T["route"].wait(pe, c, 1)
                        ps = ringx.acquire(pe, c, "rT")
                        for i in range(TT):
                            last = pe.transpose(ps[0:32 * PARTS, i * P:(i + 1) * P], rw[:, i, :], ident[:])
                        ringx.full.by(last)

                    def route_spread(c):
                        T["rT"].wait(pe, c, 1)
                        for j in range(NE // 2):
                            ps = two(ringx.acquire(pe, c, f"rb{j}"))
                            for i in range(2):
                                e = 2 * j + i
                                last = pe.matmul(ps[:, i, :], sel8[0:32 * PARTS, e:e + 1].to_broadcast([32 * PARTS, P]), rT[:],
                                                 start=True, stop=True)
                            ringx.full.by(last)

                    def experts_in(c, part):
                        ps = two(ringx.acquire(pe, c, "gu"))
                        for e in part:
                            T["xm"].wait(pe, c, e + 1)
                            for half, wt in ((0, wa["e_Wg"]), (1, wa["e_Wu"])):
                                for k in range(KD):
                                    last = pe.matmul(ps[:, half, :], wt[:, k, e * P:(e + 1) * P], xm[:, e % XM, k, :],
                                                     start=e == 0 and k == 0 and half == 0, stop=e == NE - 1 and k == KD - 1,
                                                     skip_group_check=True)
                            if e < NE - 1:
                                T["xmu"].by(last)
                            else:
                                ringx.full.by(last)

                    def experts_out(c):
                        T["he"].wait(pe, c, NE)
                        X.product_tok(pe, c, "ed", he, wa["e_Wd"], NE)

                    begin(0)
                    for j in range(NP):
                        qkvg(0, j, True)
                    for n in ORDER_A[6:]:
                        pe.wait_ge(s_w[n], 16)
                    attention_out(0)
                    ffn_begin(0)
                    ffn_in(0)
                    ffn_out(0)
                    begin(1)
                    with pe.Fori(1, NCH) as it:
                        c = it - 1
                        qkvg(it, 0)
                        cross_begin(c)
                        qkvg(it, 1)
                        query(c)
                        qkvg(it, 2, which="k")
                        pe.wait_ge(s_kv, c * 32 + 32)
                        T["qT"].wait(pe, c, 1)
                        X.scores_pe(pe, c, 0)
                        X.scores_pe(pe, c, 1)
                        qkvg(it, 2, which="gvq")
                        qkvg(it, 3, which="kg")
                        X.turn_pe(pe, c, 0)
                        qkvg(it, 3, which="v")
                        X.mix_pe(pe, c, 0)
                        X.turn_pe(pe, c, 1)
                        qkvg(it, 3, which="q")
                        X.mix_pe(pe, c, 1)
                        cross_out(c)
                        attention_out(it)
                        experts_begin(c)
                        logits(c)
                        ffn_begin(it)
                        ffn_in(it, range(0, 2))
                        route_rows(c)
                        ffn_in(it, range(2, 4))
                        route_spread(c)
                        experts_in(c, range(NE))
                        ffn_out(it)
                        begin(it + 1)
                        experts_out(c)
                    c = NCH - 1
                    cross_begin(c)
                    query(c)
                    T["qT"].wait(pe, c, 1)
                    pe.wait_ge(s_kv, c * 32 + 32)
                    for i in range(TT):
                        X.scores_pe(pe, c, i)
                    for i in range(TT):
                        X.turn_pe(pe, c, i)
                        X.mix_pe(pe, c, i)
                    cross_out(c)
                    experts_begin(c)
                    logits(c)
                    route_rows(c)
                    route_spread(c)
                    experts_in(c, range(NE))
                    experts_out(c)
            F.check(in_var=1, in_rstd=1, in_xn=1, xT=1, x_in_free=1, full=1, act=1)
            X.check()

        lb = ExitStack()
        with lb:
            WB = {"m_in": (KD, 2 * INNER), "m_xp": (KI, P), "m_out": (KI, D), "x1_Wqkv": (KD, 3 * D),
                  "x1_Wo": (KD, D), "f_w1": (KD, HID), "f_w2": (KD, HID), "f_h1": (KH, HID), "f_h2": (KH, HID),
                  "f_w3": (KH, D)}
            ORDER_B = ["x1_Wqkv", "m_in", "m_xp", "m_out", "x1_Wo", "f_w1", "f_w2", "f_h1", "f_h2", "f_w3"]
            VB = {"v_convw": KI * TAPS, "v_convb": KI, "v_dtb": KI, "v_alog": KI * NST, "v_D": KI, "v_bqkv": 3 * KD,
                  "v_s1": KH, "v_s2": KH, "v_s3": KH, "v_s4": KH}
            n_vec_b = 16 * (len(VB) + 3)
            s_vec_b, s_setup_b, s_exp_a = sem("b_vectors_loaded"), sem("b_setup_on_dve"), sem("exp_a_log")
            s_wb = {n: sem("loaded_" + n) for n in WB}
            wb = {n: alloc(lb, "sb_" + n, [P, *WB[n]]) for n in WB}
            vb = {n: alloc(lb, "sb_" + n, [P, k]) for n, k in VB.items()}
            dtw = alloc(lb, "dtw", [DTR, INNER])
            bout_row = alloc(lb, "bout_row", [P, D])
            s5_row = alloc(lb, "s5_row", [P, D])
            halo = alloc(lb, "halo", [P, KI, TAPS - 1])
            h_carry = alloc(lb, "h_carry", [P, KI, NST])
            x_in = alloc(lb, "xb_in", [P, TT, D])
            x_res = alloc(lb, "xb_res", [P, TT, D])
            x_1 = alloc(lb, "xb_1", [P, TT, D])
            x_2 = alloc(lb, "xb_2", [P, TT, D])
            x_3 = alloc(lb, "xb_3", [P, TT, D])
            xd_r = alloc(lb, "xd_r", [P, CH], BF16)
            with ExitStack() as stack:
                kv1 = kv_setup("kv1", stack, wb["x1_Wqkv"][:, :, D:2 * D], wb["x1_Wqkv"][:, :, 2 * D:3 * D],
                               vb["v_bqkv"][:, KD:2 * KD], (s_vec_b, s_wb["x1_Wqkv"]))
            xbuf = alloc(lb, "xbuf", [P, KI, TAPS - 1 + CH])
            u = alloc(lb, "u", [P, KI, CH])
            wdt = alloc(lb, "wdt", [P, KI, CH])
            dt = alloc(lb, "dt", [P, KI, CH])
            dA = alloc(lb, "dA", [P, 2, KI, CH])
            hb = alloc(lb, "hb", [P, 2, KI, CH])
            zs = alloc(lb, "zs", [P, KI, CH])
            y = xbuf[:, :, 0:CH]
            gate = alloc(lb, "gate", [P, 2, MPB, CH])
            xd_f, dtr = gate[:, 0, 0, :], gate[0:DTR, 0, 1, :]
            with ExitStack() as scratch:
                plan = [("xT2", "act", 1)]
                NP = KH // MPB
                for j in range(NP):
                    plan += [(f"a{j}", "act", 1), (f"b{j}", "dve", 1)]
                plan += [(f"c{j}", "act", 1) for j in range(NP)] + [(f"d{j}", "act", 1) for j in range(NP)] + [("fo", "dve", 1)]
                Y = Attention("xmlp", plan, 4, dict(var=2, rstd=2, xn=2, xT=2, resid=1, silu=NP, h0=NP, gelu=4), lb, scratch)
            h0 = alloc(lb, "h0", [P, KH, CH])
            h1 = alloc(lb, "h1", [P, KH, CH])
            plan = [("xT", "act", 1), ("x0", "act", 1), ("x1", "act", 1), ("z0", "act", 1), ("xd", "dve", 1), ("z1", "act", 1),
                    ("dt0", "act", 1), ("dt1", "act", 1)] + [(f"bc{n}", "dve", 1) for n in range(NST)] + [("mo", "dve", 1)]
            M = Stage("scan", plan, 0, dict(var=1, rstd=1, xn=1, xT=1, x_in_free=1, res=1, xb=1, conv=1, u=1, xd=1, soft=1,
                                            dt=1, y0=1, wdt=1, B=NST // 2, dtuB=NST // 2, dA=NST, scanned=NST, ch=NST, yn=NST, zs=1, yz=1), lb)
            s_x, s_kv, s_stored, s_turns = sem("B_x_in"), sem("B_kv_in"), sem("B_stored"), sem("B_sync_turns")

            PACE = [[range(6, 8), range(8, 10), range(10, 11), range(11, 13)],
                    [range(13, 15), range(15, 16), range(0), range(0)]]

            with nc.Block() as block:
                @block.sync
                def _(sp):
                    for n in VB:
                        load(sp, vb[n][:], t[n], s_vec_b)
                    load(sp, dtw[:], t["m_dtw"], s_vec_b)
                    for dst, n in ((bout_row, "r_bout"), (s5_row, "r_s5")):
                        load(sp, dst[:], t[n].unsqueeze(0).to_broadcast([P, D]), s_vec_b)
                    kv1[0](sp)
                    for n in ORDER_B:
                        load(sp, wb[n][:].rearrange("p k n -> p (k n)"), t[n], s_wb[n])
                    kv1[4](sp)
                    sync_loop(sp, M, Y, mid_v, x_in, x_3, out_v, 2, s_x, s_kv, s_stored, s_turns)

                @block.gpsimd
                def _(pool):
                    pool.wait_ge(s_vec_b, n_vec_b)
                    S, T = M.s, Y.s

                    def skip_term(c):
                        S["u"].wait(pool, c, 1)
                        S["y0"].by(pool.tensor_tensor(out=y, in0=u[:], in1=vb["v_D"][:].unsqueeze(2).to_broadcast([P, KI, CH]),
                                                      op=ALU.mult))

                    def add_states(c, ns):
                        for n in ns:
                            if n % 2 == 0:
                                if n == 0:
                                    S["wdt"].wait(pool, c, 1)
                                    S["y0"].wait(pool, c, 1)
                                S["B"].wait(pool, c, n // 2 + 1)
                                S["dtuB"].by(pool.tensor_tensor(out=hb[:, 1], in0=wdt[:],
                                                                in1=u[:, n // 2 % KI, :].unsqueeze(1).to_broadcast([P, KI, CH]),
                                                                op=ALU.mult))
                            S["ch"].wait(pool, c, n + 1)
                            S["yn"].by(pool.tensor_tensor(out=y, in0=y, in1=hb[:, n % 2], op=ALU.add))
                            S["yn"].wait(pool, c, n + 1)

                    def attn_residual(c):
                        T["xT"].wait(pool, c, 1)
                        T["resid"].by(pool.tensor_tensor(out=x_1[:], in0=x_1[:], in1=bout_row[:].unsqueeze(1).to_broadcast([P, TT, D]),
                                                         op=ALU.add))

                    skip_term(0)
                    add_states(0, range(NST))
                    M.ln_pool(pool, 0, 1)
                    with pool.Fori(1, NCH) as it:
                        c = it - 1
                        attn_residual(c)
                        skip_term(it)
                        Y.scale_pool(pool, c, 0)
                        Y.scale_pool(pool, c, 1)
                        add_states(it, range(2))
                        Y.ln_pool(pool, c, 1)
                        add_states(it, range(2, NST))
                        M.ln_pool(pool, it, 1)
                        Y.ln_pool(pool, c, 2)
                    c = NCH - 1
                    attn_residual(c)
                    Y.scale_pool(pool, c, 0)
                    Y.scale_pool(pool, c, 1)
                    Y.ln_pool(pool, c, 1)
                    Y.ln_pool(pool, c, 2)

                @block.vector
                def _(dve):
                    dve.wait_ge(s_vec_b, n_vec_b)
                    kv1[3](dve)
                    dve.memset(halo[:], 0.0)
                    dve.memset(h_carry[:], 0.0)
                    dve.memset(xd_r[:], 0.0)
                    dve.wait_ge(s_exp_a, 1)
                    dve.tensor_scalar(vb["v_alog"][:], vb["v_alog"][:], -1.0, None, op0=ALU.mult)
                    dve.drain().then_inc(s_setup_b, 1)
                    S, ring, T, ringy = M.s, M.ring, Y.s, Y.ring

                    def conv(c):
                        dve.tensor_copy(xbuf[:, :, 0:TAPS - 1], halo[:])
                        dve.drain()
                        S["xb"].wait(dve, c, 1)
                        for m in range(KI):
                            dve.tensor_scalar(wdt[:, m, :], xbuf[:, m, 0:CH], vb["v_convw"][:, m * TAPS:m * TAPS + 1],
                                              vb["v_convb"][:, m:m + 1], op0=ALU.mult, op1=ALU.add)
                        for tap in range(1, TAPS):
                            dve.drain()
                            for m in range(KI):
                                dve.scalar_tensor_tensor(wdt[:, m, :], xbuf[:, m, tap:tap + CH],
                                                         vb["v_convw"][:, m * TAPS + tap:m * TAPS + tap + 1], wdt[:, m, :],
                                                         op0=ALU.mult, op1=ALU.add)
                        dve.tensor_scalar(halo[:], xbuf[:, :, CH:CH + TAPS - 1], keep[:, bass.ds(c, 1)], None, op0=ALU.mult)
                        S["conv"].by(dve.drain())

                    def split_bc(c):
                        ps = ring.filled(dve, c, "xd")[:, 0:CH]
                        dve.tensor_copy(dtr, ps[0:DTR, :])
                        dve.tensor_copy(xd_r[32:64, :], ps[32:64, :])
                        dve.tensor_copy(xd_r[64:P, :], ps[64:P, :])
                        dve.drain()
                        ring.free(dve.tensor_tensor(xd_f[64:P, :], ps[64:P, :], xd_r[64:P, :], ALU.subtract), "xd")
                        dve.drain()
                        dve.tensor_copy(xd_r[64:P, :], xd_f[64:P, :])
                        dve.drain()
                        dve.tensor_tensor(xd_r[96:P, :], xd_f[96:P, :], xd_r[96:P, :], ALU.subtract)
                        S["xd"].by(dve.drain())

                    def step_sizes(c):
                        S["soft"].wait(dve, c, 1)
                        S["dt"].by(dve.scalar_tensor_tensor(dt[:], dt[:], 0.0, hb[:, 0], op0=ALU.max, op1=ALU.add))
                        dve.drain()
                        dve.tensor_tensor(wdt[:], dt[:], u[:], ALU.mult)
                        S["wdt"].by(dve.drain())

                    def states(c, ns):
                        for n in ns:
                            ps = two(ring.filled(dve, c, f"bc{n}"))
                            h = hb[:, n % 2]
                            if n % 2:
                                S["dtuB"].wait(dve, c, n // 2 + 1)
                            else:
                                if n:
                                    S["yn"].wait(dve, c, n - 1)
                                dve.tensor_tensor(h, wdt[:], ps[:, 0, :].unsqueeze(1).to_broadcast([P, KI, CH]), ALU.mult)
                                dve.drain()
                            S["dA"].wait(dve, c, n + 1)
                            for j in range(KI):
                                ins = dve.tensor_tensor_scan(h[:, j, :], dA[:, n % 2, j, :], h[:, j, :],
                                                             h_carry[:, j, n:n + 1], ALU.mult, ALU.add)
                            S["scanned"].by(ins)
                            dve.drain()
                            dve.tensor_scalar(h_carry[:, :, n], h[:, :, CH - 1], keep[:, bass.ds(c, 1)], None, op0=ALU.mult)
                            dve.drain()
                            ring.free(dve.tensor_tensor(h, h, ps[:, 1, :].unsqueeze(1).to_broadcast([P, KI, CH]), ALU.mult),
                                      f"bc{n}")
                            S["ch"].by(dve.drain())

                    def scan_out(c):
                        S["yn"].wait(dve, c, NST)
                        S["zs"].wait(dve, c, 1)
                        S["yz"].by(dve.tensor_tensor(wdt[:], y, zs[:], ALU.mult))
                        S["res"].wait(dve, c, 1)
                        M.residual_ln(dve, c, "mo", x_res, 1, x_1)

                    def cross_out(c):
                        T["resid"].wait(dve, c, 1)
                        Y.residual_ln(dve, c, "ao", x_1, 1, x_2)

                    def up(c, js):
                        for j in js:
                            T["silu"].wait(dve, c, j + 1)
                            ps = two(ringy.filled(dve, c, f"b{j}"))
                            for i in range(MPB):
                                m = j * MPB + i
                                ins = dve.scalar_tensor_tensor(h0[:, m, :], ps[:, i, :], vb["v_s2"][:, m:m + 1], gate[:, j % 2, i, :],
                                                               op0=ALU.mult, op1=ALU.mult)
                            ringy.free(ins, f"b{j}")
                            T["h0"].by(dve.drain())

                    def mlp_out(c):
                        ps = two(ringy.filled(dve, c, "fo"))
                        ringy.free(dve.tensor_tensor(Y.r[:], ps, s5_row[:].unsqueeze(1).to_broadcast([P, TT, D]), ALU.mult), "fo")
                        dve.drain()
                        dve.tensor_tensor(Y.r[:], Y.r[:], x_2[:], ALU.add)
                        dve.drain()
                        dve.wait_ge(s_stored, c * 16 + 16)
                        Y.ln_dve(dve, c, 2, Y.r, x_3)

                    conv(0)
                    split_bc(0)
                    step_sizes(0)
                    states(0, range(NST))
                    scan_out(0)
                    conv(1)
                    with dve.Fori(1, NCH) as it:
                        c = it - 1
                        split_bc(it)
                        Y.centre_dve(dve, c, 0)
                        Y.centre_dve(dve, c, 1)
                        Y.sums_dve(dve, c, 0)
                        Y.sums_dve(dve, c, 1)
                        step_sizes(it)
                        states(it, range(0, 2))
                        cross_out(c)
                        states(it, range(2, 3))
                        up(c, range(0, 2))
                        states(it, range(3, 4))
                        up(c, range(2, 4))
                        states(it, range(4, NST))
                        scan_out(it)
                        conv(it + 1)
                        mlp_out(c)
                    c = NCH - 1
                    Y.centre_dve(dve, c, 0)
                    Y.centre_dve(dve, c, 1)
                    Y.sums_dve(dve, c, 0)
                    Y.sums_dve(dve, c, 1)
                    cross_out(c)
                    up(c, range(NP))
                    mlp_out(c)

                @block.scalar
                def _(act):
                    act.wait_ge(s_vec_b, n_vec_b)
                    act.activation(vb["v_alog"][:], vb["v_alog"][:], ACT.Exp).then_inc(s_exp_a, 1)
                    kv1[2](act)
                    act.wait_ge(s_setup_b, 1)
                    S, ring, T, ringy = M.s, M.ring, Y.s, Y.ring

                    def keep_x(c, before=None):
                        act.wait_ge(s_x, c * 16 + 16)
                        if before is not None:
                            S["xn"].wait(act, before, 1)
                        S["res"].by(act.activation(x_res[:], x_in[:], ACT.Copy))
                        S["x_in_free"].by(act.drain())

                    def conv_in(c):
                        for j in range(KI // MPB):
                            ps = two(ring.filled(act, c, f"x{j}"))
                            ring.free(act.activation(xbuf[:, j * MPB:(j + 1) * MPB, TAPS - 1:], ps, ACT.Copy), f"x{j}")
                        S["xb"].by(act.drain())

                    def gates(c, js=range(KI // MPB)):
                        for j in js:
                            ps = two(ring.filled(act, c, f"z{j}"))
                            ring.free(act.activation(zs[:, j * MPB:(j + 1) * MPB, :], ps, ACT.Silu), f"z{j}")
                        if js[-1] == KI // MPB - 1:
                            S["zs"].by(act.drain())

                    def conv_out(c):
                        S["conv"].wait(act, c, 1)
                        S["u"].by(act.activation(u[:], wdt[:], ACT.Silu))

                    def steps_in(c):
                        for j in range(KI // MPB):
                            ps = two(ring.filled(act, c, f"dt{j}"))
                            for i in range(MPB):
                                m = j * MPB + i
                                ins = act.activation(dt[:, m, :], ps[:, i, :], ACT.Identity, bias=vb["v_dtb"][:, m:m + 1])
                            ring.free(ins, f"dt{j}")
                        act.drain()
                        act.activation(hb[:, 0], dt[:], ACT.Abs)
                        act.drain()
                        act.activation(hb[:, 0], hb[:, 0], ACT.Exp, scale=-1.0)

                    def steps_out(c):
                        act.drain()
                        S["soft"].by(act.activation(hb[:, 0], hb[:, 0], ACT.Ln, bias=1.0))
                        S["dt"].wait(act, c, 1)

                    def decays(c, ns):
                        for n in ns:
                            if n % 2:
                                if n == 1:
                                    S["wdt"].wait(act, c, 1)
                                    S["y0"].wait(act, c, 1)
                                if n // 2 >= KI:
                                    S["dtuB"].wait(act, c, n // 2 + 1 - KI)
                                ps = two(ring.filled(act, c, f"bc{n}"))
                                S["B"].by(act.activation(u[:, n // 2 % KI, :], ps[:, 0, :], ACT.Copy))
                            if n >= 2:
                                S["scanned"].wait(act, c, n - 1)
                            for j in range(KI):
                                ins = act.activation(dA[:, n % 2, j, :], dt[:, j, :], ACT.Exp,
                                                     scale=vb["v_alog"][:, j * NST + n:j * NST + n + 1])
                            S["dA"].by(ins)

                    def mlp_gate(c, js):
                        for j in js:
                            if j >= 2:
                                T["h0"].wait(act, c, j - 1)
                            ps = two(ringy.filled(act, c, f"a{j}"))
                            for i in range(MPB):
                                m = j * MPB + i
                                ins = act.activation(gate[:, j % 2, i, :], ps[:, i, :], ACT.Silu, scale=vb["v_s1"][:, m:m + 1])
                            ringy.free(ins, f"a{j}")
                            T["silu"].by(act.drain())

                    def scale_in(c, name, dst, scale, j):
                        ps = two(ringy.filled(act, c, f"{name}{j}"))
                        for i in range(MPB):
                            m = j * MPB + i
                            ins = act.activation(dst[:, m, :], ps[:, i, :], ACT.Copy, scale=vb[scale][:, m:m + 1])
                        ringy.free(ins, f"{name}{j}")

                    def gelus(c, name, h, scale):
                        act.drain()
                        T["gelu"].by(act.activation(h[:, 0:KH - MPB, :], h[:, 0:KH - MPB, :], ACT.Gelu))
                        j = NP - 1
                        ps = two(ringy.filled(act, c, f"{name}{j}"))
                        for i in range(MPB):
                            m = j * MPB + i
                            ins = act.activation(h[:, m, :], ps[:, i, :], ACT.Gelu, scale=vb[scale][:, m:m + 1])
                        ringy.free(ins, f"{name}{j}")
                        T["gelu"].by(act.drain())

                    M.transpose_act(act, 0, "xT")
                    keep_x(0)
                    conv_in(0)
                    conv_out(0)
                    gates(0, [0])
                    gates(0, [1])
                    steps_in(0)
                    steps_out(0)
                    decays(0, range(NST))
                    M.transpose_act(act, 1, "xT")
                    conv_in(1)
                    keep_x(1, 0)
                    with act.Fori(1, NCH) as it:
                        c = it - 1
                        conv_out(it)
                        Y.transpose_act(act, c, "xTq")
                        gates(it, [0])
                        Y.query_act(act, c, vb["v_bqkv"][:, 0:KD])
                        gates(it, [1])
                        Y.exp_act(act, c, 0)
                        steps_in(it)
                        Y.exp_act(act, c, 1)
                        steps_out(it)
                        Y.move_act(act, c, 0)
                        decays(it, range(0, 2))
                        Y.mixed_act(act, c, 0, vb["v_bqkv"][:, 2 * KD:3 * KD])
                        Y.move_act(act, c, 1)
                        Y.mixed_act(act, c, 1, vb["v_bqkv"][:, 2 * KD:3 * KD])
                        decays(it, range(2, 3))
                        Y.transpose_act(act, c, "xT2")
                        mlp_gate(c, range(0, 2))
                        decays(it, range(3, 4))
                        mlp_gate(c, range(2, 4))
                        decays(it, range(4, 6))
                        for j in range(NP - 1):
                            scale_in(c, "c", h1, "v_s3", j)
                            decays(it, PACE[0][j])
                        gelus(c, "c", h1, "v_s3")
                        decays(it, PACE[0][-1])
                        for j in range(NP - 1):
                            scale_in(c, "d", h0, "v_s4", j)
                            decays(it, PACE[1][j])
                        gelus(c, "d", h0, "v_s4")
                        M.transpose_act(act, it + 1, "xT")
                        conv_in(it + 1)
                        keep_x(it + 1, it)
                    c = NCH - 1
                    Y.transpose_act(act, c, "xTq")
                    Y.query_act(act, c, vb["v_bqkv"][:, 0:KD])
                    for i in range(TT):
                        Y.exp_act(act, c, i)
                    for i in range(TT):
                        Y.move_act(act, c, i)
                        Y.mixed_act(act, c, i, vb["v_bqkv"][:, 2 * KD:3 * KD])
                    Y.transpose_act(act, c, "xT2")
                    mlp_gate(c, range(NP))
                    for j in range(NP - 1):
                        scale_in(c, "c", h1, "v_s3", j)
                    gelus(c, "c", h1, "v_s3")
                    for j in range(NP - 1):
                        scale_in(c, "d", h0, "v_s4", j)
                    gelus(c, "d", h0, "v_s4")

                @block.tensor
                def _(pe):
                    kv1[1](pe)
                    pe.wait_ge(s_setup_b, 1)
                    for n in ORDER_B[1:4]:
                        pe.wait_ge(s_wb[n], 16)
                    S, ring, T, ringy = M.s, M.ring, Y.s, Y.ring
                    ring.start(pe)
                    ringy.start(pe)

                    def begin(c):
                        pe.wait_ge(s_x, c * 16 + 16)
                        M.transpose_pe(pe, c, "xT", x_in)

                    def inner(c, name, first_pair, js=range(KI // MPB)):
                        S["xT"].wait(pe, c, 1)
                        for j in js:
                            ps = ring.acquire(pe, c, f"{name}{j}")
                            for i in range(MPB):
                                m = (first_pair + j) * MPB + i
                                for k in range(KD):
                                    last = pe.matmul(ps[:, i * CH:(i + 1) * CH], wb["m_in"][:, k, m * P:(m + 1) * P], M.xT[:, k, :],
                                                     start=k == 0, stop=k == KD - 1)
                            ring.full.by(last)

                    def x_proj(c):
                        S["u"].wait(pe, c, 1)
                        ps = ring.acquire(pe, c, "xd")
                        for k in range(KI):
                            last = pe.matmul(ps[:, 0:CH], wb["m_xp"][:, k, :], u[:, k, :], start=k == 0, stop=k == KI - 1)
                        ring.full.by(last)

                    def dt_proj(c):
                        S["xd"].wait(pe, c, 1)
                        for j in range(KI // MPB):
                            ps = ring.acquire(pe, c, f"dt{j}")
                            for i in range(MPB):
                                m = j * MPB + i
                                last = pe.matmul(ps[:, i * CH:(i + 1) * CH], dtw[:, m * P:(m + 1) * P], dtr, start=True, stop=True)
                            ring.full.by(last)

                    def spread(c, ns):
                        for n in ns:
                            ps = ring.acquire(pe, c, f"bc{n}")
                            for i in range(2):
                                col = sel_bc[:, i * NST + n:i * NST + n + 1]
                                last = pe.matmul(ps[:, i * CH:(i + 1) * CH], col.to_broadcast([P, P]), xd_r[:], start=True, stop=True)
                            ring.full.by(last)

                    def scan_out(c):
                        S["yz"].wait(pe, c, 1)
                        M.product_tok(pe, c, "mo", wdt, wb["m_out"], KI)

                    def cross_begin(c):
                        S["xn"].wait(pe, c, 1)
                        Y.transpose_pe(pe, c, "xTq", x_1)

                    def query(c):
                        T["xT"].wait(pe, c, 1)
                        Y.product(pe, c, "xq", wb["x1_Wqkv"], 0, Y.xT, KD)

                    def keys_wait(c):
                        T["qT"].wait(pe, c, 1)
                        pe.wait_ge(s_kv, c * 32 + 32)

                    def cross_out(c):
                        T["oaT"].wait(pe, c, 1)
                        Y.product_tok(pe, c, "ao", Y.oaT, wb["x1_Wo"], KD)

                    def mlp_begin(c):
                        T["xn"].wait(pe, c, 1)
                        Y.transpose_pe(pe, c, "xT2", x_2)
                        T["xT"].wait(pe, c, 2)

                    def gate_up(c, js):
                        for j in js:
                            Y.product(pe, c, f"a{j}", wb["f_w1"], j, Y.xT, KD)
                            Y.product(pe, c, f"b{j}", wb["f_w2"], j, Y.xT, KD)

                    def hidden2(c, j):
                        ps = ringy.acquire(pe, c, f"d{j}")
                        if j == 0:
                            T["gelu"].wait(pe, c, 1)
                        for i in range(MPB):
                            m = j * MPB + i
                            for k in range(KH):
                                if m == 0 and k == KH - MPB:
                                    T["gelu"].wait(pe, c, 2)
                                last = pe.matmul(ps[:, i * CH:(i + 1) * CH], wb["f_h2"][:, k, m * P:(m + 1) * P], h1[:, k, :],
                                                 start=k == 0, stop=k == KH - 1)
                        ringy.full.by(last)

                    def mlp_out(c):
                        T["gelu"].wait(pe, c, 3)
                        Y.product_tok(pe, c, "fo", h0, wb["f_w3"], KH, (KH - MPB, lambda: T["gelu"].wait(pe, c, 4)))

                    begin(0)
                    inner(0, "x", 0)
                    inner(0, "z", KI // MPB, [0])
                    x_proj(0)
                    inner(0, "z", KI // MPB, [1])
                    dt_proj(0)
                    spread(0, range(NST))
                    scan_out(0)
                    begin(1)
                    inner(1, "x", 0)
                    for n in ORDER_B[4:]:
                        pe.wait_ge(s_wb[n], 16)
                    with pe.Fori(1, NCH) as it:
                        c = it - 1
                        cross_begin(c)
                        inner(it, "z", KI // MPB, [0])
                        query(c)
                        x_proj(it)
                        inner(it, "z", KI // MPB, [1])
                        keys_wait(c)
                        Y.scores_pe(pe, c, 0)
                        Y.scores_pe(pe, c, 1)
                        dt_proj(it)
                        spread(it, range(0, 2))
                        Y.turn_pe(pe, c, 0)
                        Y.mix_pe(pe, c, 0)
                        Y.turn_pe(pe, c, 1)
                        Y.mix_pe(pe, c, 1)
                        cross_out(c)
                        spread(it, range(2, 3))
                        mlp_begin(c)
                        gate_up(c, range(0, 2))
                        spread(it, range(3, 4))
                        gate_up(c, range(2, 4))
                        spread(it, range(4, 6))
                        T["h0"].wait(pe, c, NP)
                        for j in range(NP):
                            Y.product(pe, c, f"c{j}", wb["f_h1"], j, h0, KH)
                            spread(it, PACE[0][j])
                        for j in range(NP):
                            hidden2(c, j)
                            spread(it, PACE[1][j])
                        scan_out(it)
                        begin(it + 1)
                        inner(it + 1, "x", 0)
                        mlp_out(c)
                    c = NCH - 1
                    cross_begin(c)
                    query(c)
                    keys_wait(c)
                    for i in range(TT):
                        Y.scores_pe(pe, c, i)
                    for i in range(TT):
                        Y.turn_pe(pe, c, i)
                        Y.mix_pe(pe, c, i)
                    cross_out(c)
                    mlp_begin(c)
                    gate_up(c, range(NP))
                    T["h0"].wait(pe, c, NP)
                    for j in range(NP):
                        Y.product(pe, c, f"c{j}", wb["f_h1"], j, h0, KH)
                    for j in range(NP):
                        hidden2(c, j)
                    mlp_out(c)
            M.check(xT=1, full=3, act=3, xb=1, res=1, x_in_free=1, conv=1)
            Y.check()


def kernel(x, ctx_1024, L0_attn_ln1_g, L0_attn_ln1_b, L0_attn_Wq, L0_attn_bq, L0_attn_Wk, L0_attn_bk, L0_attn_Wv,
           L0_attn_bv, L0_attn_Wg, L0_attn_bg, L0_attn_decay_logit, L0_attn_Wo, L0_attn_bo, L0_attn_ln2_g,
           L0_attn_ln2_b, L0_attn_W1, L0_attn_b1, L0_attn_W2, L0_attn_b2, L0_xattn_Wq, L0_xattn_Wk, L0_xattn_Wv,
           L0_xattn_Wo, L0_ffn_gate_w, L0_ffn_w_gate, L0_ffn_w_up, L0_ffn_w_down, L1_attn_in_proj_w, L1_attn_conv_w,
           L1_attn_conv_b, L1_attn_x_proj_w, L1_attn_dt_proj_w, L1_attn_dt_proj_b, L1_attn_A_log, L1_attn_D_param,
           L1_attn_out_proj_w, L1_xattn_W_qkv, L1_xattn_b_qkv, L1_xattn_W_out, L1_xattn_b_out, L1_ffn_w1_w, L1_ffn_w1_s,
           L1_ffn_w2_w, L1_ffn_w2_s, L1_ffn_h1_w, L1_ffn_h1_s, L1_ffn_h2_w, L1_ffn_h2_s, L1_ffn_w3_w, L1_ffn_w3_s):
    import numpy as np
    from concourse import bacc
    from concourse.bass_utils import run_bass_kernel_spmd

    def rows(w):
        w = np.asarray(w)
        return np.ascontiguousarray(w.reshape(-1, P, w.shape[1]).transpose(1, 0, 2).reshape(P, -1))

    def vec(v):
        return np.ascontiguousarray(np.asarray(v).reshape(-1, P).T)

    def flat(w):
        w = np.asarray(w)
        return w.reshape(-1, w.shape[2])

    xp = np.asarray(L1_attn_x_proj_w)
    gap = np.zeros((32 - DTR, INNER), np.float32)
    bc = xp[DTR:]
    a = {
        "x": np.asarray(x),
        "ctxT": np.ascontiguousarray(np.asarray(ctx_1024).reshape(BATCH, KEYS, KD, P).transpose(3, 2, 0, 1).reshape(P, -1)),
        "a_Wq": rows(L0_attn_Wq), "a_Wk": rows(L0_attn_Wk), "a_Wv": rows(L0_attn_Wv), "a_Wg": rows(L0_attn_Wg),
        "a_Wo": rows(L0_attn_Wo), "a_W1": rows(L0_attn_W1), "a_W2": rows(L0_attn_W2),
        "x0_Wq": rows(np.asarray(L0_xattn_Wq).T), "x0_Wk": rows(np.asarray(L0_xattn_Wk).T),
        "x0_Wv": rows(np.asarray(L0_xattn_Wv).T), "x0_Wo": rows(np.asarray(L0_xattn_Wo).T),
        "e_gate": rows(np.asarray(L0_ffn_gate_w).T), "e_Wg": rows(flat(L0_ffn_w_gate).T),
        "e_Wu": rows(flat(L0_ffn_w_up).T), "e_Wd": rows(flat(np.asarray(L0_ffn_w_down).transpose(0, 2, 1))),
        "v_ln1_g": vec(L0_attn_ln1_g), "v_ln1_b": vec(L0_attn_ln1_b), "v_bq": vec(L0_attn_bq), "v_bk": vec(L0_attn_bk),
        "v_bv": vec(L0_attn_bv), "v_bg": vec(L0_attn_bg),
        "v_decay": vec(np.repeat(np.asarray(L0_attn_decay_logit), HID // HEADS)),
        "v_ln2_g": vec(L0_attn_ln2_g), "v_ln2_b": vec(L0_attn_ln2_b), "v_b1": vec(L0_attn_b1),
        "r_bo": np.asarray(L0_attn_bo), "r_b2": np.asarray(L0_attn_b2),
        "m_in": rows(np.asarray(L1_attn_in_proj_w).T), "m_xp": rows(np.concatenate([xp[:DTR], gap] + [bc] * PARTS).T),
        "m_dtw": np.ascontiguousarray(np.asarray(L1_attn_dt_proj_w).T), "m_out": rows(np.asarray(L1_attn_out_proj_w).T),
        "v_convw": rows(np.asarray(L1_attn_conv_w)[:, 0, :]), "v_convb": vec(L1_attn_conv_b), "v_dtb": vec(L1_attn_dt_proj_b),
        "v_alog": rows(L1_attn_A_log), "v_D": vec(L1_attn_D_param),
        "x1_Wqkv": rows(L1_xattn_W_qkv), "v_bqkv": vec(L1_xattn_b_qkv), "x1_Wo": rows(L1_xattn_W_out),
        "r_bout": np.asarray(L1_xattn_b_out),
        "f_w1": rows(np.asarray(L1_ffn_w1_w).T), "f_w2": rows(np.asarray(L1_ffn_w2_w).T), "f_h1": rows(np.asarray(L1_ffn_h1_w).T),
        "f_h2": rows(np.asarray(L1_ffn_h2_w).T), "f_w3": rows(np.asarray(L1_ffn_w3_w).T),
        "v_s1": vec(L1_ffn_w1_s), "v_s2": vec(L1_ffn_w2_s), "v_s3": vec(L1_ffn_h1_s), "v_s4": vec(L1_ffn_h2_s),
        "r_s5": np.asarray(L1_ffn_w3_s),
    }
    nc = bacc.Bacc("TRN2", target_bir_lowering=False, num_devices=1)
    t = {n: nc.dram_tensor("in_" + n, v.shape, F32, kind="ExternalInput").ap() for n, v in a.items()}
    mid = nc.dram_tensor("mid", (TOK, D), F32, kind="Internal").ap()
    kz_dram = nc.dram_tensor("kz_dram", (BATCH, P, KD * ROWS), F32, kind="Internal").ap()
    vz_dram = nc.dram_tensor("vz_dram", (BATCH, P, KD * 5 * P), F32, kind="Internal").ap()
    out = nc.dram_tensor("out", (BATCH, SEQ, D), F32, kind="ExternalOutput").ap()
    decoder(nc, t, mid, kz_dram, vz_dram, out)
    r = run_bass_kernel_spmd(nc, [{"in_" + n: v for n, v in a.items()}], core_ids=[0])
    return r.results[0]["out"]
```

```python
from contextlib import ExitStack

import concourse.bass as bass
from concourse import mybir

F32 = mybir.dt.float32
BF16 = mybir.dt.bfloat16
ACT = mybir.ActivationFunctionType
ALU = mybir.AluOpType
AX = mybir.AxisListType.X

P = 128
D = 256
KD = D // P
BATCH, SEQ = 2, 1024
TOK = BATCH * SEQ
CH = 256
NCH = TOK // CH
CPB = SEQ // CH
TT = CH // P
BANK = 512
MPB = BANK // CH
RING = 4
HID = 1024
KH = HID // P
NE = 8
KEYS = 77
HEADS, DH = 16, 16
HPT = P // DH
ROWS = HPT * KEYS
BLK = [P, P, P, P, ROWS - 4 * P]
HPB = 4
INNER, NST, DTR, TAPS = 512, 16, 16, 4
KI = INNER // P
BC = 2 * NST
PARTS = 3
EPS = 1e-5


class Signal:

    def __init__(self, sem, per):
        self.sem, self.per, self.seen = sem, per, 0

    def by(self, instruction):
        self.seen += 1
        instruction.then_inc(self.sem, 1)

    def wait(self, eng, c, k):
        assert k >= 1, (self.sem, k)
        eng.wait_ge(self.sem, c * self.per + k)


class Ring:

    def __init__(self, plan, psum, first, full, freed):
        self.psum, self.first, self.full, self.freed = psum, first, full, freed
        self.slots, self.where = [], {}
        for name, reader, n in plan:
            self.where[name] = len(self.slots)
            self.slots += [reader] * n
        self.given = {"act": 0, "dve": 0}
        full.per = sum(r is not None for r in self.slots)
        for r in freed:
            freed[r].per = self.slots.count(r)

    def bank(self, name, n=1):
        b = self.first + self.where[name] % RING
        return self.psum[:, b, :] if n == 1 else self.psum[:, b:b + n, :]

    def acquire(self, pe, c, name, n=1):
        own = range(self.where[name], self.where[name] + n)
        for r in ("act", "dve"):
            old = [s - RING for s in own if s >= RING and self.slots[s - RING] == r]
            last = [max(o for o in range(len(self.slots)) if o % RING == s % RING and self.slots[o]) for s in own if s < RING]
            last = [s for s in last if self.slots[s] == r]
            if old:
                self.freed[r].wait(pe, c, self.freed[r].per + self.slots[:old[-1] + 1].count(r))
            elif last:
                self.freed[r].wait(pe, c, self.slots[:max(last) + 1].count(r))
        return self.bank(name, n)

    def start(self, pe):
        for r in self.freed.values():
            pe.sem_inc(r.sem, r.per)

    def filled(self, eng, c, name, n=1):
        s = self.where[name] + n - 1
        self.full.wait(eng, c, sum(r is not None for r in self.slots[:s + 1]))
        return self.bank(name, n)

    def free(self, instruction, name, last=0):
        s = self.where[name] + last
        r = self.slots[s]
        assert self.slots[:s].count(r) == self.given[r] % self.freed[r].per, (name, self.given)
        self.given[r] += 1
        self.freed[r].by(instruction)


def two(ap):
    return ap.rearrange("p (k n) -> p k n", k=2)


def decoder(nc, t, mid, kz_dram, vz_dram, out):
    top = ExitStack()
    with top:
        def alloc(stack, name, shape, dt=F32):
            return stack.enter_context(nc.sbuf_tensor(name, shape, dt))

        def sem(name):
            return top.enter_context(nc.semaphore(name))

        ident = alloc(top, "ident", [P, P])
        head_mask = alloc(top, "head_mask", [P, HPT])
        row_mask = alloc(top, "row_mask", [P, 5, P])
        first_key = alloc(top, "first_key", [P, NE])
        half_neg = alloc(top, "half_neg", [P, TT])
        sel8 = alloc(top, "sel8", [P, NE], BF16)
        sel_bc = alloc(top, "sel_bc", [P, BC], BF16)
        keep = alloc(top, "keep", [P, NCH + 1])
        kz = alloc(top, "kz", [P, KD, HPT, KEYS])
        vz = alloc(top, "vz", [P, KD, 5, P])
        psum = top.enter_context(nc.psum_tensor("psum", [P, 8, BANK], F32))

        s_const = sem("constants_made")
        s_setup = sem("setup_on_dve")

        def load(eng, dst, src, s):
            eng.dma_start(dst, src).then_inc(s, 16)

        class Stage:

            def __init__(self, tag, plan, first_bank, per, stack):
                self.s = {n: Signal(sem(f"{tag}_{n}"), k) for n, k in per.items()}
                full = Signal(sem(f"{tag}_banks_full"), 0)
                freed = {"act": Signal(sem(f"{tag}_act_freed"), 0), "dve": Signal(sem(f"{tag}_dve_freed"), 0)}
                self.ring = Ring(plan, psum, first_bank, full, freed)
                self.r = alloc(stack, f"{tag}_r", [P, TT, D])
                self.xT = alloc(stack, f"{tag}_xT", [P, KD, CH])
                self.norm = {}
                for lane in ("", "in_")[:1 + ("in_var" in per)]:
                    self.norm[lane] = [alloc(stack, f"{tag}_{lane}{n}", [P, TT, *k])
                                       for n, k in (("stats", [6]), ("mv", [2]), ("ve", []), ("rstd", []))]

            def check(self, **ahead):
                bad = [(n, s.seen, s.per) for n, s in [*self.s.items(), ("full", self.ring.full), *self.ring.freed.items()]
                       if s.seen != 2 * s.per + ahead.get(n, 0)]
                assert not bad, bad

            def ln_dve(self, dve, c, k, src, dst, lane=""):
                stats, mv, ve, rstd = self.norm[lane]
                for i in range(TT):
                    dve.bn_stats(stats[:, i, :], src[:, i, :])
                dve.drain()
                for i in range(TT):
                    dve.bn_aggr(mv[:, i, :], stats[:, i, :])
                dve.drain()
                self.s[lane + "var"].by(dve.tensor_scalar(ve[:, :], mv[:, :, 1], EPS, None, op0=ALU.add))
                self.s[lane + "rstd"].wait(dve, c, k)
                for i in range(TT):
                    ins = dve.tensor_scalar(dst[:, i, :], src[:, i, :], mv[:, i, 0:1], rstd[:, i:i + 1],
                                            op0=ALU.subtract, op1=ALU.mult)
                self.s[lane + "xn"].by(ins)

            def ln_pool(self, pool, c, k, lane=""):
                _, _, ve, rstd = self.norm[lane]
                self.s[lane + "var"].wait(pool, c, k)
                self.s[lane + "rstd"].by(pool.tensor_tensor(out=rstd[:, :], in0=ve[:, :], in1=half_neg[:, :], op=ALU.pow))

            def residual_ln(self, dve, c, name, resid, k, dst):
                ps = self.ring.filled(dve, c, name)
                self.ring.free(dve.tensor_tensor(self.r[:], two(ps), resid[:], ALU.add), name)
                dve.drain()
                self.ln_dve(dve, c, k, self.r, dst)

            def transpose_pe(self, pe, c, name, src):
                ps = self.ring.acquire(pe, c, name)
                for kd in range(KD):
                    for i in range(TT):
                        last = pe.transpose(ps[:, kd * CH + i * P:kd * CH + (i + 1) * P], src[:, i, kd * P:(kd + 1) * P], ident[:])
                self.ring.full.by(last)

            def transpose_act(self, act, c, name, gain=None, bias=None):
                ps = self.ring.filled(act, c, name)
                if gain is None:
                    self.ring.free(act.activation(self.xT[:], two(ps), ACT.Copy), name)
                else:
                    for kd in range(KD):
                        ins = act.activation(self.xT[:, kd, :], two(ps)[:, kd, :], ACT.Identity, bias=bias[:, kd:kd + 1],
                                             scale=gain[:, kd:kd + 1])
                    self.ring.free(ins, name)
                self.s["xT"].by(act.drain())

            def product(self, pe, c, name, w, pair, rhs, kt, late=None):
                ps = self.ring.acquire(pe, c, name)
                for j in range(MPB):
                    m = pair * MPB + j
                    for k in range(kt):
                        if late and (j, k) == (0, late[0]):
                            late[1]()
                        last = pe.matmul(ps[:, j * CH:(j + 1) * CH], w[:, k, m * P:(m + 1) * P], rhs[:, k, :],
                                         start=k == 0, stop=k == kt - 1)
                self.ring.full.by(last)

            def product_tok(self, pe, c, name, actT, w, kt, late=None):
                ps = self.ring.acquire(pe, c, name)
                for i in range(TT):
                    for k in range(kt):
                        if late and (i, k) == (0, late[0]):
                            late[1]()
                        last = pe.matmul(ps[:, i * D:(i + 1) * D], actT[:, k, i * P:(i + 1) * P], w[:, k, :],
                                         start=k == 0, stop=k == kt - 1)
                self.ring.full.by(last)

        class Attention(Stage):

            SIGNALS = dict(qT=1, centred=2 * TT, exps=2 * TT, inv_sums=2 * TT, probs=2 * TT, probsT=TT, oaT=1)
            PLAN = [("xTq", "act", 1), ("xq", "act", 1)]
            PLAN += [(f"s{i}_{h}", "dve", 2) for i in range(TT) for h in range(2)]
            for i in range(TT):
                PLAN += [(f"pT{i}_0", "act", 1), (f"pT{i}_1", "act", 1), (f"pT{i}_2", "act", 1), (f"pv{i}", "act", 1)]
            PLAN += [("ao", "dve", 1)]

            def __init__(self, tag, plan, first_bank, per, stack, scratch):
                super().__init__(tag, self.PLAN + plan, first_bank, dict(self.SIGNALS, **per), stack)
                self.qT = alloc(stack, f"{tag}_qT", [P, KD, CH])
                self.oaT = alloc(stack, f"{tag}_oaT", [P, KD, CH])
                self.mx = alloc(stack, f"{tag}_mx", [P, 2, HEADS])
                self.rs = alloc(stack, f"{tag}_rs", [P, 2, HEADS])
                self.p = alloc(scratch, f"{tag}_p", [P, 2, HEADS * KEYS])
                self.pt = alloc(scratch, f"{tag}_pt", [P, 3, BANK])

            def scores_pe(self, pe, c, i):
                for h in range(2):
                    ps = self.ring.acquire(pe, c, f"s{i}_{h}", 2)
                    for b in range(2):
                        self.ring.full.by(pe.matmul(ps[:, b, 0:HPB * KEYS], self.qT[:, h, i * P:(i + 1) * P],
                                                    kz[:, h, b * HPB:(b + 1) * HPB, :].rearrange("p h k -> p (h k)"),
                                                    start=True, stop=True))

            def turn_pe(self, pe, c, i):
                for g in range(3):
                    if g < 2:
                        self.s["probs"].wait(pe, c, 2 * i + g + 1)
                    ps = self.ring.acquire(pe, c, f"pT{i}_{g}")
                    for pos in range(4 if g < 2 else 2):
                        kd, blk = (g, pos) if g < 2 else (pos, 4)
                        c0, n = kd * ROWS + blk * P, BLK[blk]
                        last = pe.transpose(ps[0:n, pos * P:(pos + 1) * P], self.p[:, i % 2, c0:c0 + n], ident[:])
                    self.ring.full.by(last)

            def mix_pe(self, pe, c, i):
                self.s["probsT"].wait(pe, c, i + 1)
                ps = self.ring.acquire(pe, c, f"pv{i}")
                for kd in range(KD):
                    for blk, n in enumerate(BLK):
                        g, pos = (kd, blk) if blk < 4 else (2, kd)
                        last = pe.matmul(ps[:, kd * P:(kd + 1) * P], vz[0:n, kd, blk, :],
                                         self.pt[0:n, g, pos * P:(pos + 1) * P], start=blk == 0, stop=blk == 4)
                self.ring.full.by(last)

            def query_act(self, act, c, bias=None):
                ps = self.ring.filled(act, c, "xq")
                for kd in range(KD):
                    b = 0.0 if bias is None else bias[:, kd:kd + 1]
                    ins = act.activation(self.qT[:, kd, :], two(ps)[:, kd, :], ACT.Identity, bias=b)
                self.ring.free(ins, "xq")
                self.s["qT"].by(act.drain())

            def half(self, i, h):
                return self.p[:, i % 2, h * ROWS:(h + 1) * ROWS]

            def exp_act(self, act, c, i, h):
                self.s["centred"].wait(act, c, 2 * i + h + 1)
                self.s["exps"].by(act.activation(self.half(i, h), self.half(i, h), ACT.Exp, scale=DH ** -0.5))

            def move_act(self, act, c, i):
                for g in range(3):
                    n, w = (P, BANK) if g < 2 else (BLK[4], 2 * P)
                    ps = self.ring.filled(act, c, f"pT{i}_{g}")
                    self.ring.free(act.activation(self.pt[0:n, g, 0:w], ps[0:n, 0:w], ACT.Copy), f"pT{i}_{g}")
                self.s["probsT"].by(act.drain())

            def mixed_act(self, act, c, i, bias=None):
                ps = self.ring.filled(act, c, f"pv{i}")
                for kd in range(KD):
                    b = 0.0 if bias is None else bias[:, kd:kd + 1]
                    ins = act.activation(self.oaT[:, kd, i * P:(i + 1) * P], ps[:, kd * P:(kd + 1) * P], ACT.Identity, bias=b)
                self.ring.free(ins, f"pv{i}")
                if i == TT - 1:
                    self.s["oaT"].by(act.drain())

            def centre_dve(self, dve, c, i, h):
                ps = self.ring.filled(dve, c, f"s{i}_{h}", 2)[:, :, 0:HPB * KEYS].rearrange("p b (h k) -> p b h k", h=HPB)
                m = self.mx[:, i % 2, h * HPT:(h + 1) * HPT].rearrange("p (b h) -> p b h", b=2)
                dve.tensor_reduce(m, ps, axis=AX, op=ALU.max)
                dve.drain()
                for b in range(2):
                    c0 = h * ROWS + b * HPB * KEYS
                    ins = dve.tensor_tensor(self.p[:, i % 2, c0:c0 + HPB * KEYS].rearrange("p (h k) -> p h k", h=HPB),
                                            ps[:, b], m[:, b, :].unsqueeze(2).to_broadcast([P, HPB, KEYS]), ALU.subtract)
                    self.ring.free(ins, f"s{i}_{h}", b)
                self.s["centred"].by(dve.drain())

            def sums_dve(self, dve, c, i, h):
                self.s["exps"].wait(dve, c, 2 * i + h + 1)
                r = self.rs[:, i % 2, h * HPT:(h + 1) * HPT]
                dve.tensor_reduce(r, self.half(i, h).rearrange("p (h k) -> p h k", h=HPT), axis=AX, op=ALU.add)
                dve.drain()
                self.s["inv_sums"].by(dve.reciprocal(r, r))

            def softmax_dve(self, dve, c):
                self.centre_dve(dve, c, 0, 0)
                self.centre_dve(dve, c, 0, 1)
                self.sums_dve(dve, c, 0, 0)
                self.sums_dve(dve, c, 0, 1)
                self.centre_dve(dve, c, 1, 0)
                self.centre_dve(dve, c, 1, 1)
                self.sums_dve(dve, c, 1, 0)
                self.sums_dve(dve, c, 1, 1)

            def scale_pool(self, pool, c, i):
                for h in range(2):
                    self.s["inv_sums"].wait(pool, c, 2 * i + h + 1)
                    v = self.half(i, h).rearrange("p (h k) -> p h k", h=HPT)
                    r = self.rs[:, i % 2, h * HPT:(h + 1) * HPT].unsqueeze(2).to_broadcast([P, HPT, KEYS])
                    self.s["probs"].by(pool.tensor_tensor(out=v, in0=v, in1=r, op=ALU.mult))

        class ContextSetup:

            def __init__(self, tag, stack, w_k, w_v, k_bias, loaded):
                self.w_k, self.w_v, self.k_bias, self.loaded = w_k, w_v, k_bias, loaded
                self.ctx = alloc(stack, f"{tag}_ctx_sb", [P, KD, BATCH, KEYS])
                self.rep = alloc(stack, f"{tag}_ctx_rep", [P, KD, BATCH, HPT, KEYS])
                self.k_sb = alloc(stack, f"{tag}_k_sb", [P, KD, BATCH, KEYS])
                self.s_ctx, self.s_rep, self.s_kp, self.s_ks = (sem(f"{tag}_{n}") for n in ("ctx", "ctx_rep", "k_psum", "k_sb"))
                self.s_vp, self.s_vf = sem(f"{tag}_v_psum"), sem(f"{tag}_v_freed")
                self.s_made, self.s_stored = sem(f"{tag}_kzvz_made"), sem(f"{tag}_kzvz_stored")

            def load_ctx(self, sp):
                load(sp, self.ctx[:].rearrange("p k b s -> p (k b s)"), t["ctxT"], self.s_ctx)

            def k_pe(self, pe):
                pe.wait_ge(self.s_ctx, 16)
                for s_loaded in self.loaded:
                    pe.wait_ge(s_loaded, 16)
                for m in range(KD):
                    for k in range(KD):
                        last = pe.matmul(psum[:, RING + m, 0:BATCH * KEYS], self.w_k[:, k, m * P:(m + 1) * P],
                                         self.ctx[:, k].rearrange("p b s -> p (b s)"), start=k == 0, stop=k == KD - 1)
                    last.then_inc(self.s_kp, 1)

            def v_pe(self, pe, b):
                pe.wait_ge(self.s_rep, 1)
                for blk in range(5):
                    n = (1 - b) * 5 + blk
                    if n >= 2:
                        pe.wait_ge(self.s_vf, n - 1)
                    for k in range(KD):
                        rows = self.rep[:, k, b].rearrange("p h s -> p (h s)")[:, blk * P:blk * P + BLK[blk]]
                        last = pe.matmul(psum[0:BLK[blk], RING + 2 + n % 2, 0:D], rows, self.w_v[:, k, 0:D],
                                         start=k == 0, stop=k == KD - 1)
                    last.then_inc(self.s_vp, 1)

            def done_pe(self, pe):
                pe.wait_ge(self.s_ks, KD)
                pe.wait_ge(self.s_vf, 10)

            def k_act(self, act):
                for m in range(KD):
                    act.wait_ge(self.s_kp, m + 1)
                    b = 0.0 if self.k_bias is None else self.k_bias[:, m:m + 1]
                    act.activation(self.k_sb[:, m].rearrange("p b s -> p (b s)"), psum[:, RING + m, 0:BATCH * KEYS],
                                   ACT.Identity, bias=b).then_inc(self.s_ks, 1)

            def repeat_dve(self, dve):
                dve.wait_ge(self.s_ctx, 16)
                for k in range(KD):
                    for b in range(BATCH):
                        dve.tensor_copy(self.rep[:, k, b], self.ctx[:, k, b].unsqueeze(1).to_broadcast([P, HPT, KEYS]))
                dve.memset(vz[:, :, 4, :], 0.0)
                dve.drain().then_inc(self.s_rep, 1)

            def make_dve(self, dve, b):
                dve.wait_ge(self.s_ks, KD)
                dve.wait_ge(s_const, 1)
                if b == 0:
                    dve.wait_ge(self.s_stored, 32)
                for m in range(KD):
                    dve.tensor_tensor(kz[:, m], self.k_sb[:, m, b].unsqueeze(1).to_broadcast([P, HPT, KEYS]),
                                      head_mask[:, :].unsqueeze(2).to_broadcast([P, HPT, KEYS]), ALU.mult)
                for blk in range(5):
                    n, r = (1 - b) * 5 + blk, BLK[blk]
                    dve.wait_ge(self.s_vp, n + 1)
                    dve.tensor_tensor(vz[0:r, :, blk, :], psum[0:r, RING + 2 + n % 2, 0:D].rearrange("p (k c) -> p k c", k=KD),
                                      row_mask[0:r, blk, :].unsqueeze(1).to_broadcast([r, KD, P]), ALU.mult).then_inc(self.s_vf, 1)
                dve.drain().then_inc(self.s_made, 1)

            def store(self, sp):
                for n, b in enumerate((1, 0)):
                    sp.wait_ge(self.s_made, n + 1)
                    sp.dma_start(kz_dram[b], kz[:].rearrange("p m h s -> p (m h s)")).then_inc(self.s_stored, 16)
                    sp.dma_start(vz_dram[b], vz[:].rearrange("p m k c -> p (m k c)")).then_inc(self.s_stored, 16)
                sp.wait_ge(self.s_stored, 64)

        def load_kv(sp, b, s):
            sp.dma_start(kz[:].rearrange("p m h s -> p (m h s)"), kz_dram[bass.ds(b, 1), :, :].rearrange("b p n -> p (b n)")).then_inc(s, 16)
            sp.dma_start(vz[:].rearrange("p m k c -> p (m k c)"), vz_dram[bass.ds(b, 1), :, :].rearrange("b p n -> p (b n)")).then_inc(s, 16)

        x_dram = t["x"].rearrange("b (t p) d -> (b t) p d", p=P)
        mid_v = mid.rearrange("(t p) d -> t p d", p=P)
        out_v = out.rearrange("b (t p) d -> (b t) p d", p=P)

        class Traffic:

            def __init__(self, tag, first, second, src, x_in, x_out, dst, n_ln):
                self.first, self.second, self.src, self.x_in, self.x_out, self.dst, self.n_ln = first, second, src, x_in, x_out, dst, n_ln
                self.s_x, self.s_kv, self.s_stored, self.s_turns = (sem(f"{tag}_{n}") for n in ("x_in", "kv_in", "stored", "sync_turns"))

            def first_chunk(self, sp):
                sp.dma_start(self.x_in[:], self.src[0:TT, :, :].rearrange("t p d -> p t d")).then_inc(self.s_x, 16)

            def chunk_in(self, sp, it, tile):
                self.first.s["x_in_free"].wait(sp, it, self.first.s["x_in_free"].per)
                sp.dma_start(self.x_in[:], self.src[bass.ds(tile, TT), :, :].rearrange("t p d -> p t d")).then_inc(self.s_x, 16)

            def chunk_out(self, sp, c, tile):
                self.second.s["xn"].wait(sp, c, self.n_ln)
                sp.dma_start(self.dst[bass.ds(tile, TT), :, :].rearrange("t p d -> p t d"), self.x_out[:]).then_inc(self.s_stored, 16)

            def start(self, sp, context):
                sp.sem_inc(self.s_stored, 16)
                self.chunk_in(sp, 0, TT)
                context.store(sp)
                load_kv(sp, 0, self.s_kv)

            def loop(self, sp):
                with sp.Fori(1, NCH) as it:
                    tile_next, tile_out, c = sp.snap((it + 1) % NCH * TT), sp.snap((it - 1) * TT), sp.snap(it - 1)
                    b = sp.snap(it // CPB)
                    self.chunk_in(sp, it, tile_next)
                    self.second.s["oaT"].wait(sp, c, 1)
                    load_kv(sp, b, self.s_kv)
                    self.chunk_out(sp, c, tile_out)
                    sp.sem_inc(self.s_turns, 1)

            def finish(self, sp):
                self.chunk_out(sp, NCH - 1, (NCH - 1) * TT)
                sp.wait_ge(self.s_stored, 16 * (NCH + 1))
                sp.wait_ge(self.s_x, 16 * (NCH + 1))

        WB = {"m_in": (KD, 2 * INNER), "m_xp": (KI, P), "m_out": (KI, D), "x1_Wqkv": (KD, 3 * D),
              "x1_Wo": (KD, D), "f_w1": (KD, HID), "f_w2": (KD, HID), "f_h1": (KH, HID), "f_h2": (KH, HID),
              "f_w3": (KH, D)}
        ORDER_B = ["m_in", "m_xp", "x1_Wqkv", "m_out", "x1_Wo", "f_w1", "f_w2", "f_h1", "f_h2", "f_w3"]
        VB = {"v_convw": KI * TAPS, "v_convb": KI, "v_dtb": KI, "v_alog": KI * NST, "v_D": KI, "v_bqkv": 3 * KD,
              "v_s1": KH, "v_s2": KH, "v_s3": KH, "v_s4": KH}
        n_vec_b = 16 * (len(VB) + 1)
        s_vec_b, s_rows_b, s_setup_b, s_exp_a = sem("b_vectors_loaded"), sem("b_rows_loaded"), sem("b_setup_on_dve"), sem("exp_a_log")
        s_wb = {n: sem("loaded_" + n) for n in WB}
        wb = {n: alloc(top, "sb_" + n, [P, *WB[n]]) for n in ORDER_B[:2]}
        vb = {n: alloc(top, "sb_" + n, [P, k]) for n, k in VB.items()}
        dtw = alloc(top, "dtw", [DTR, INNER])
        xb_in = alloc(top, "xb_in", [P, TT, D])

        la = ExitStack()
        with la:
            WA = {"a_Wq": (KD, HID), "a_Wk": (KD, HID), "a_Wv": (KD, HID), "a_Wg": (KD, HID), "a_Wo": (KH, D),
                  "a_W1": (KD, HID), "a_W2": (KH, D), "x0_Wq": (KD, D), "x0_Wk": (KD, D), "x0_Wv": (KD, D),
                  "x0_Wo": (KD, D), "e_gate": (KD, NE), "e_Wg": (KD, HID), "e_Wu": (KD, HID), "e_Wd": (NE, D)}
            ORDER_A = ["x0_Wk", "x0_Wv", "a_Wk", "a_Wg", "a_Wv", "a_Wq", "a_Wo", "a_W1", "a_W2", "x0_Wq", "x0_Wo",
                       "e_gate", "e_Wg", "e_Wu", "e_Wd"]
            VA = {"v_ln1_g": KD, "v_ln1_b": KD, "v_bq": KH, "v_bk": KH, "v_bv": KH, "v_bg": KH, "v_decay": KH,
                  "v_ln2_g": KD, "v_ln2_b": KD, "v_b1": KH}
            s_vec_a, s_decay = sem("a_vectors_loaded"), sem("decay_made")
            s_w = {n: sem("loaded_" + n) for n in WA}
            n_vec_a = 16 * (len(VA) + 2)
            wa = {n: alloc(la, "sb_" + n, [P, *WA[n]]) for n in WA if n[0] == "a"}
            va = {n: alloc(la, "sb_" + n, [P, k]) for n, k in VA.items()}
            bo_row = alloc(la, "bo_row", [P, D])
            b2_row = alloc(la, "b2_row", [P, D])
            decay = alloc(la, "decay", [P, KH])
            carry = alloc(la, "carry", [P, KH])
            x_in = alloc(la, "x_in", [P, TT, D])
            x_n = alloc(la, "x_n", [P, TT, D])
            x_bo = alloc(la, "x_bo", [P, TT, D])
            x_b2 = alloc(la, "x_b2", [P, TT, D])
            hT = alloc(la, "hT", [P, KH, CH])
            k_sb = alloc(la, "k_sb", [P, 2, MPB, CH])
            g_sb = alloc(la, "g_sb", [P, 2, MPB, CH])
            kv = alloc(la, "kv", [P, MPB, CH])
            st = alloc(la, "st", [P, MPB, CH])
            qg = alloc(la, "qg", [P, MPB, CH])
            NP = KH // MPB
            plan = [("xT1", "act", 1)]
            for j in range(NP):
                plan += [(f"k{j}", "act", 1), (f"g{j}", "act", 1), (f"v{j}", "dve", 1), (f"q{j}", "dve", 1)]
            plan += [("ao", "dve", 1), ("xT2", "act", 1)] + [(f"f{j}", "act", 1) for j in range(NP)] + [("fo", "dve", 1)]
            F = Stage("attnffn", plan, 0, dict(in_var=1, in_rstd=1, in_xn=1, var=2, rstd=2, xn=2, xT=2, x_in_free=2, kg=NP, kvd=NP, oT=NP, resid=3, gelu=1), la)
            wa.update((n, alloc(la, "sb_" + n, [P, *WA[n]])) for n in WA if n[0] != "a")
            x_1 = alloc(la, "x_1", [P, TT, D])
            x_2 = alloc(la, "x_2", [P, TT, D])
            x_3 = alloc(la, "x_3", [P, TT, D])
            rB = alloc(la, "rB", [P, NE, CH])
            he = alloc(la, "he", [P, NE, CH])
            XM = 3
            xm = alloc(la, "xm", [P, XM, KD, CH])
            sg = alloc(la, "sg", [P, CH])
            lg = alloc(la, "lg", [P, TT, NE])
            eq = alloc(la, "eq", [P, TT, NE])
            rw = alloc(la, "rw", [P, TT, 32 * PARTS])
            r_hi = alloc(la, "r_hi", [P, 2, TT, NE], BF16)
            top1 = alloc(la, "top1", [P, TT])
            sgm = alloc(la, "sgm", [P, TT])
            fk = alloc(la, "fk", [P, TT])
            rT = alloc(la, "rT", [32 * PARTS, CH], BF16)
            plan = [("xTe", "act", 1), ("lg", "dve", 1), ("rT", "act", 1)] + [(f"rb{j}", "act", 1) for j in range(NE // 2)]
            plan += [("gu", "dve", 1), ("ed", "dve", 1)]
            with ExitStack() as stack:
                kv0 = ContextSetup("kv0", stack, wa["x0_Wk"], wa["x0_Wv"], None, (s_w["x0_Wk"], s_w["x0_Wv"]))
            X = Attention("xmoe", plan, 4, dict(var=2, rstd=2, xn=2, xT=2, top=1, sig=1, route=1, rT=1, rb=NE // 2, xm=NE,
                                                xmu=NE - 1, silu=1, he=NE), la, la)
            traffic_a = Traffic("A", F, X, x_dram, x_in, x_3, mid_v, 2)
            s_x, s_kv, s_stored = traffic_a.s_x, traffic_a.s_kv, traffic_a.s_stored

        lb = ExitStack()
        with lb:
            wb.update((n, alloc(lb, "sb_" + n, [P, *WB[n]])) for n in ("x1_Wqkv", "m_out"))
            bout_row = alloc(lb, "bout_row", [P, D])
            s5_row = alloc(lb, "s5_row", [P, D])
            halo = alloc(lb, "halo", [P, KI, TAPS - 1])
            h_carry = alloc(lb, "h_carry", [P, KI, NST])
            x_res = alloc(lb, "xb_res", [P, TT, D])
            y_1 = alloc(lb, "xb_1", [P, TT, D])
            xd_r = alloc(lb, "xd_r", [P, CH], BF16)
            xbuf = alloc(lb, "xbuf", [P, KI, TAPS - 1 + CH])
            u = alloc(lb, "u", [P, KI, CH])
            wdt = alloc(lb, "wdt", [P, KI, CH])
            dt = alloc(lb, "dt", [P, KI, CH])
            dA = alloc(lb, "dA", [P, 2, KI, CH])
            hb = alloc(lb, "hb", [P, 2, KI, CH])
            zs = alloc(lb, "zs", [P, KI, CH])
            y = xbuf[:, :, 0:CH]
            gate = alloc(lb, "gate", [P, 2, MPB, CH])
            xd_f, dtr = gate[:, 0, 0, :], gate[0:DTR, 0, 1, :]
            plan = [("xT", "act", 1), ("x0", "act", 1), ("x1", "act", 1), ("xd", "dve", 1), ("dt0", "act", 1), ("dt1", "act", 1)]
            plan += [(f"bc{n}", "dve", 1) for n in range(2)] + [("z0", "act", 1), ("z1", "act", 1)]
            plan += [(f"bc{n}", "dve", 1) for n in range(2, NST)]
            plan += [("left out", None, 1), ("mo", "dve", 1)]
            M = Stage("scan", plan, 0, dict(var=1, rstd=1, xn=1, xT=1, x_in_free=1, res=1, xb=2, conv=2, u=2, xd=1, soft=1,
                                            dt=1, y0=1, wdt=1, B=NST // 2, dtuB=NST // 2, dA=NST, scanned=NST, ch=NST - 1, yn=NST - 1, zs=1, yz=1), lb)
            with ExitStack() as stack:
                kv1 = ContextSetup("kv1", stack, wb["x1_Wqkv"][:, :, D:2 * D], wb["x1_Wqkv"][:, :, 2 * D:3 * D],
                                   vb["v_bqkv"][:, KD:2 * KD], (s_wb["x1_Wqkv"],))
            wb.update((n, alloc(lb, "sb_" + n, [P, *WB[n]])) for n in ("f_w1", "f_w2"))
            wb.update((n, alloc(lb, "sb_" + n, [P, *WB[n]])) for n in ("x1_Wo", "f_h1", "f_h2", "f_w3"))
            y_2 = alloc(lb, "xb_2", [P, TT, D])
            y_3 = alloc(lb, "xb_3", [P, TT, D])
            with ExitStack() as scratch:
                plan = [("xT2", "act", 1)]
                NP = KH // MPB
                for j in range(NP):
                    plan += [(f"a{j}", "act", 1), (f"b{j}", "dve", 1)]
                plan += [(f"c{j}", "act", 1) for j in range(NP)] + [(f"d{j}", "act", 1) for j in range(NP)]
                plan += [("left out", None, 1), ("fo", "dve", 1)]
                Y = Attention("xmlp", plan, 4, dict(var=2, rstd=2, xn=2, xT=2, resid=1, silu=NP, h0=NP, gelu=4), lb, scratch)
            h0 = alloc(lb, "h0", [P, KH, CH])
            h1 = alloc(lb, "h1", [P, KH, CH])
            traffic_b = Traffic("B", M, Y, mid_v, xb_in, y_3, out_v, 2)
            s_xb, s_kv_b, s_stored_b = traffic_b.s_x, traffic_b.s_kv, traffic_b.s_stored

            PACE = [[range(6, 8), range(8, 10), range(10, 11), range(11, 13)],
                    [range(13, 15), range(15, 16), range(0), range(0)]]

        def first_stage_over(eng):
            F.s["xn"].wait(eng, NCH - 1, 2)
            F.s["xT"].wait(eng, NCH, 1)

        with nc.Block() as block:
            @block.sync
            def _(sp):
                traffic_a.first_chunk(sp)
                for n in VA:
                    load(sp, va[n][:], t[n], s_vec_a)
                for dst, n in ((bo_row, "r_bo"), (b2_row, "r_b2")):
                    load(sp, dst[:], t[n].unsqueeze(0).to_broadcast([P, D]), s_vec_a)
                for n in ORDER_A[:2]:
                    load(sp, wa[n][:].rearrange("p k n -> p (k n)"), t[n], s_w[n])
                kv0.load_ctx(sp)
                for n in ORDER_A[2:]:
                    load(sp, wa[n][:].rearrange("p k n -> p (k n)"), t[n], s_w[n])
                for n in ORDER_B[:2]:
                    load(sp, wb[n][:].rearrange("p k n -> p (k n)"), t[n], s_wb[n])
                for n in VB:
                    load(sp, vb[n][:], t[n], s_vec_b)
                load(sp, dtw[:], t["m_dtw"], s_vec_b)
                traffic_a.start(sp, kv0)
                traffic_a.loop(sp)
                sp.wait_ge(s_stored, 16 * 2)
                traffic_b.first_chunk(sp)
                first_stage_over(sp)
                for dst, n in ((bout_row, "r_bout"), (s5_row, "r_s5")):
                    load(sp, dst[:], t[n].unsqueeze(0).to_broadcast([P, D]), s_rows_b)
                for n in ORDER_B[2:4]:
                    load(sp, wb[n][:].rearrange("p k n -> p (k n)"), t[n], s_wb[n])
                kv1.load_ctx(sp)
                traffic_a.finish(sp)
                for n in ORDER_B[4:5]:
                    load(sp, wb[n][:].rearrange("p k n -> p (k n)"), t[n], s_wb[n])
                traffic_b.start(sp, kv1)
                for n in ORDER_B[5:]:
                    load(sp, wb[n][:].rearrange("p k n -> p (k n)"), t[n], s_wb[n])
                traffic_b.loop(sp)
                traffic_b.finish(sp)

            @block.gpsimd
            def _(pool):
                pool.memset(ident[:], 0.0)
                pool.memset(head_mask[:], 1.0)
                pool.memset(row_mask[:], 1.0)
                pool.memset(half_neg[:], -0.5)
                pool.memset(rw[:], 0.0)
                for e in range(NE):
                    pool.memset(first_key[:, e:e + 1], float(NE - e))
                for c in range(NCH + 1):
                    pool.memset(keep[:, c:c + 1], float(c % CPB != CPB - 1))
                pool.drain()
                pool.affine_select(out=ident[:], in_=ident[:], compare_op=ALU.not_equal, fill=1.0, base=0,
                                   pattern=[[-1, P]], channel_multiplier=1)
                pool.affine_select(out=head_mask[:], in_=head_mask[:], compare_op=ALU.is_ge, fill=0.0, base=0,
                                   pattern=[[-DH, HPT]], channel_multiplier=1)
                v = row_mask[:].rearrange("p k (h c) -> p k h c", c=DH)
                pool.affine_select(out=v, in_=v, compare_op=ALU.is_ge, fill=0.0, base=0,
                                   pattern=[[P, 5], [-KEYS, HPT], [0, DH]], channel_multiplier=1)
                pool.drain()
                pool.affine_select(out=head_mask[:], in_=head_mask[:], compare_op=ALU.is_ge, fill=0.0, base=DH - 1,
                                   pattern=[[DH, HPT]], channel_multiplier=-1)
                pool.affine_select(out=v, in_=v, compare_op=ALU.is_ge, fill=0.0, base=KEYS - 1,
                                   pattern=[[-P, 5], [KEYS, HPT], [0, DH]], channel_multiplier=-1)
                pool.drain().then_inc(s_const, 1)
                pool.wait_ge(s_vec_a, n_vec_a)

                def attn_residuals(c):
                    bc = bo_row[:].unsqueeze(1).to_broadcast([P, TT, D])
                    pool.wait_ge(s_x, c * 16 + 16)
                    S = F.s["resid"]
                    S.by(pool.tensor_tensor(out=x_bo[:], in0=x_in[:], in1=bc, op=ALU.add))
                    bc = b2_row[:].unsqueeze(1).to_broadcast([P, TT, D])
                    S.by(pool.tensor_tensor(out=x_b2[:], in0=x_in[:], in1=bc, op=ALU.add))
                    F.s["x_in_free"].by(pool.drain())

                def ffn_residual(c):
                    F.s["xn"].wait(pool, c, 1)
                    F.s["resid"].by(pool.tensor_tensor(out=x_b2[:], in0=x_b2[:], in1=F.r[:], op=ALU.add))

                F.ln_pool(pool, 0, 1, "in_")
                attn_residuals(0)
                F.ln_pool(pool, 0, 1)
                ffn_residual(0)
                F.ln_pool(pool, 1, 1, "in_")
                F.ln_pool(pool, 0, 2)
                with pool.Fori(1, NCH) as it:
                    c = it - 1
                    attn_residuals(it)
                    X.scale_pool(pool, c, 0)
                    X.scale_pool(pool, c, 1)
                    X.ln_pool(pool, c, 1)
                    F.ln_pool(pool, it, 1)
                    ffn_residual(it)
                    F.ln_pool(pool, it + 1, 1, "in_")
                    F.ln_pool(pool, it, 2)
                    X.ln_pool(pool, c, 2)

                pool.wait_ge(s_vec_b, n_vec_b)
                SM, SY = M.s, Y.s

                def skip_term(c):
                    SM["u"].wait(pool, c, 2)
                    SM["y0"].by(pool.tensor_tensor(out=y, in0=u[:], in1=vb["v_D"][:].unsqueeze(2).to_broadcast([P, KI, CH]),
                                                  op=ALU.mult))

                def add_states(c, ns):
                    for n in ns:
                        if n % 2 == 0:
                            if n == 0:
                                SM["wdt"].wait(pool, c, 1)
                                SM["y0"].wait(pool, c, 1)
                            SM["B"].wait(pool, c, n // 2 + 1)
                            SM["dtuB"].by(pool.tensor_tensor(out=hb[:, 1], in0=wdt[:],
                                                            in1=u[:, n // 2 % KI, :].unsqueeze(1).to_broadcast([P, KI, CH]),
                                                            op=ALU.mult))
                        if n == NST - 1:
                            continue
                        SM["ch"].wait(pool, c, n + 1)
                        SM["yn"].by(pool.tensor_tensor(out=y, in0=y, in1=hb[:, n % 2], op=ALU.add))
                        SM["yn"].wait(pool, c, n + 1)

                def attn_residual(c):
                    SY["xT"].wait(pool, c, 1)
                    SY["resid"].by(pool.tensor_tensor(out=y_1[:], in0=y_1[:], in1=bout_row[:].unsqueeze(1).to_broadcast([P, TT, D]),
                                                     op=ALU.add))

                c = NCH - 1
                X.scale_pool(pool, c, 0)
                X.scale_pool(pool, c, 1)
                skip_term(0)
                X.ln_pool(pool, c, 1)
                add_states(0, range(0, 7))
                X.ln_pool(pool, c, 2)
                add_states(0, range(7, NST))
                M.ln_pool(pool, 0, 1)
                pool.wait_ge(s_rows_b, 32)
                with pool.Fori(1, NCH) as it:
                    c = it - 1
                    attn_residual(c)
                    skip_term(it)
                    Y.scale_pool(pool, c, 0)
                    Y.scale_pool(pool, c, 1)
                    add_states(it, range(1))
                    Y.ln_pool(pool, c, 1)
                    add_states(it, range(1, NST))
                    M.ln_pool(pool, it, 1)
                    Y.ln_pool(pool, c, 2)
                c = NCH - 1
                attn_residual(c)
                Y.scale_pool(pool, c, 0)
                Y.scale_pool(pool, c, 1)
                Y.ln_pool(pool, c, 1)
                Y.ln_pool(pool, c, 2)

            @block.vector
            def _(dve):
                S, ring, T, ringx = F.s, F.ring, X.s, X.ring

                def begin(c):
                    dve.wait_ge(s_x, c * 16 + 16)
                    F.ln_dve(dve, c, 1, x_in, x_n, "in_")
                    S["x_in_free"].by(dve.drain())

                def linear_attention(c, j):
                    S["kg"].wait(dve, c, j + 1)
                    ps = two(ring.filled(dve, c, f"v{j}"))
                    for i in range(MPB):
                        m = j * MPB + i
                        ins = dve.scalar_tensor_tensor(kv[:, i, :], ps[:, i, :], va["v_bv"][:, m:m + 1], k_sb[:, j % 2, i, :],
                                                       op0=ALU.add, op1=ALU.mult)
                    ring.free(ins, f"v{j}")
                    dve.drain()
                    for i in range(MPB):
                        m = j * MPB + i
                        dve.tensor_tensor_scan(st[:, i, :], decay[:, m:m + 1].to_broadcast([P, CH]), kv[:, i, :],
                                               carry[:, m:m + 1], ALU.mult, ALU.add)
                    ps = two(ring.filled(dve, c, f"q{j}"))
                    for i in range(MPB):
                        m = j * MPB + i
                        ins = dve.scalar_tensor_tensor(qg[:, i, :], ps[:, i, :], va["v_bq"][:, m:m + 1], g_sb[:, j % 2, i, :],
                                                       op0=ALU.add, op1=ALU.mult)
                    ring.free(ins, f"q{j}")
                    S["kvd"].by(dve.drain())
                    m = slice(j * MPB, (j + 1) * MPB)
                    dve.tensor_scalar(carry[:, m], st[:, :, CH - 1], keep[:, bass.ds(c, 1)], None, op0=ALU.mult)
                    S["oT"].by(dve.scalar_tensor_tensor(hT[:, m, :], st[:], 64 ** -0.5, qg[:], op0=ALU.mult, op1=ALU.mult))

                def attention_out(c):
                    S["resid"].wait(dve, c, 1)
                    F.residual_ln(dve, c, "ao", x_bo, 1, x_bo)

                def ffn_out(c):
                    S["resid"].wait(dve, c, 3)
                    F.residual_ln(dve, c, "fo", x_b2, 2, x_1)

                def route(c):
                    ps = ringx.filled(dve, c, "lg")
                    ringx.free(dve.tensor_copy(lg[:], ps[:, 0:TT * NE].rearrange("p (t e) -> p t e", t=TT)), "lg")
                    dve.drain()
                    T["top"].by(dve.tensor_reduce(top1[:], lg[:], axis=AX, op=ALU.max))
                    dve.drain()
                    dve.tensor_tensor(eq[:], lg[:], top1[:].unsqueeze(2).to_broadcast([P, TT, NE]), ALU.is_equal)
                    dve.drain()
                    dve.tensor_tensor(eq[:], eq[:], first_key[:].unsqueeze(1).to_broadcast([P, TT, NE]), ALU.mult)
                    dve.drain()
                    dve.tensor_reduce(fk[:], eq[:], axis=AX, op=ALU.max)
                    dve.drain()
                    dve.tensor_tensor(eq[:], eq[:], fk[:].unsqueeze(2).to_broadcast([P, TT, NE]), ALU.is_equal)
                    dve.drain()
                    T["sig"].wait(dve, c, 1)
                    dve.tensor_tensor(lg[:], eq[:], sgm[:].unsqueeze(2).to_broadcast([P, TT, NE]), ALU.mult)
                    dve.drain()
                    dve.tensor_copy(r_hi[:, 0], lg[:])
                    dve.drain()
                    dve.tensor_copy(rw[:, :, 0:NE], r_hi[:, 0])
                    dve.tensor_tensor(eq[:], lg[:], r_hi[:, 0], ALU.subtract)
                    dve.drain()
                    dve.tensor_copy(r_hi[:, 1], eq[:])
                    dve.drain()
                    dve.tensor_copy(rw[:, :, 32:32 + NE], r_hi[:, 1])
                    T["route"].by(dve.tensor_tensor(rw[:, :, 64:64 + NE], eq[:], r_hi[:, 1], ALU.subtract))

                def experts_in(c, es=range(NE)):
                    for e in es:
                        T["rb"].wait(dve, c, e // 2 + 1)
                        if e >= XM:
                            T["xmu"].wait(dve, c, e - XM + 1)
                        T["xm"].by(dve.tensor_tensor(xm[:, e % XM], X.xT[:], rB[:, e, :].unsqueeze(1).to_broadcast([P, KD, CH]),
                                                     ALU.mult))

                def experts_out(c):
                    dve.wait_ge(s_stored, c * 16 + 16)
                    X.residual_ln(dve, c, "ed", x_2, 2, x_3)

                def experts_hidden(c):
                    T["silu"].wait(dve, c, 1)
                    ps = two(ringx.bank("gu"))
                    ringx.free(dve.tensor_tensor(sg[:], ps[:, 1, :], sg[:], ALU.mult), "gu")
                    dve.drain()
                    for e in range(NE):
                        T["he"].by(dve.scalar_tensor_tensor(he[:, e, :], rB[:, e, :], 0.0, sg[:], op0=ALU.is_gt, op1=ALU.mult))

                dve.wait_ge(s_const, 1)
                begin(0)
                kv0.repeat_dve(dve)
                dve.memset(carry[:], 0.0)
                for sel, n, at in ((sel8, NE, 0), (sel_bc, BC, 32)):
                    dve.tensor_tensor(sel[:], ident[:, at:at + n], ident[:, at + 32:at + 32 + n], ALU.add)
                    dve.drain()
                    dve.tensor_tensor(sel[:], sel[:], ident[:, at + 64:at + 64 + n], ALU.add)
                dve.drain().then_inc(s_setup, 1)
                kv0.make_dve(dve, 1)
                dve.wait_ge(s_vec_a, n_vec_a)
                dve.wait_ge(s_decay, 1)
                for j in range(NP):
                    linear_attention(0, j)
                attention_out(0)
                kv0.make_dve(dve, 0)
                begin(1)
                ffn_out(0)
                with dve.Fori(1, NCH) as it:
                    c = it - 1
                    linear_attention(it, 0)
                    linear_attention(it, 1)
                    X.softmax_dve(dve, c)
                    linear_attention(it, 2)
                    linear_attention(it, 3)
                    X.residual_ln(dve, c, "ao", x_1, 1, x_2)
                    attention_out(it)
                    route(c)
                    experts_in(c)
                    begin(it + 1)
                    experts_hidden(c)
                    ffn_out(it)
                    experts_out(c)

                SM, ringm, SY, ringy = M.s, M.ring, Y.s, Y.ring

                def conv(c):
                    dve.tensor_copy(xbuf[:, :, 0:TAPS - 1], halo[:])
                    dve.drain()
                    for j in range(KI // MPB):
                        SM["xb"].wait(dve, c, j + 1)
                        tiles = range(j * MPB, (j + 1) * MPB)
                        for m in tiles:
                            dve.tensor_scalar(wdt[:, m, :], xbuf[:, m, 0:CH], vb["v_convw"][:, m * TAPS:m * TAPS + 1],
                                              vb["v_convb"][:, m:m + 1], op0=ALU.mult, op1=ALU.add)
                        for tap in range(1, TAPS):
                            dve.drain()
                            for m in tiles:
                                dve.scalar_tensor_tensor(wdt[:, m, :], xbuf[:, m, tap:tap + CH],
                                                         vb["v_convw"][:, m * TAPS + tap:m * TAPS + tap + 1], wdt[:, m, :],
                                                         op0=ALU.mult, op1=ALU.add)
                        SM["conv"].by(dve.drain())
                    dve.tensor_scalar(halo[:], xbuf[:, :, CH:CH + TAPS - 1], keep[:, bass.ds(c, 1)], None, op0=ALU.mult)
                    dve.drain()

                def split_bc(c):
                    ps = ringm.filled(dve, c, "xd")[:, 0:CH]
                    dve.tensor_copy(dtr, ps[0:DTR, :])
                    dve.tensor_copy(xd_r[32:64, :], ps[32:64, :])
                    dve.tensor_copy(xd_r[64:P, :], ps[64:P, :])
                    dve.drain()
                    ringm.free(dve.tensor_tensor(xd_f[64:P, :], ps[64:P, :], xd_r[64:P, :], ALU.subtract), "xd")
                    dve.drain()
                    dve.tensor_copy(xd_r[64:P, :], xd_f[64:P, :])
                    dve.drain()
                    dve.tensor_tensor(xd_r[96:P, :], xd_f[96:P, :], xd_r[96:P, :], ALU.subtract)
                    SM["xd"].by(dve.drain())

                def step_sizes(c):
                    SM["soft"].wait(dve, c, 1)
                    SM["dt"].by(dve.scalar_tensor_tensor(dt[:], dt[:], 0.0, hb[:, 0], op0=ALU.max, op1=ALU.add))
                    dve.drain()
                    dve.tensor_tensor(wdt[:], dt[:], u[:], ALU.mult)
                    SM["wdt"].by(dve.drain())

                def states(c, ns):
                    for n in ns:
                        ps = two(ringm.filled(dve, c, f"bc{n}"))
                        h = hb[:, n % 2]
                        if n % 2:
                            SM["dtuB"].wait(dve, c, n // 2 + 1)
                        else:
                            if n:
                                SM["yn"].wait(dve, c, n - 1)
                            dve.tensor_tensor(h, wdt[:], ps[:, 0, :].unsqueeze(1).to_broadcast([P, KI, CH]), ALU.mult)
                            dve.drain()
                        SM["dA"].wait(dve, c, n + 1)
                        for j in range(KI):
                            ins = dve.tensor_tensor_scan(h[:, j, :], dA[:, n % 2, j, :], h[:, j, :],
                                                         h_carry[:, j, n:n + 1], ALU.mult, ALU.add)
                        SM["scanned"].by(ins)
                        dve.drain()
                        dve.tensor_scalar(h_carry[:, :, n], h[:, :, CH - 1], keep[:, bass.ds(c, 1)], None, op0=ALU.mult)
                        dve.drain()
                        ringm.free(dve.tensor_tensor(h, h, ps[:, 1, :].unsqueeze(1).to_broadcast([P, KI, CH]), ALU.mult),
                                  f"bc{n}")
                        drained = dve.drain()
                        if n < NST - 1:
                            SM["ch"].by(drained)

                def scan_out(c):
                    SM["yn"].wait(dve, c, NST - 1)
                    dve.tensor_tensor(y, y, hb[:, (NST - 1) % 2], ALU.add)
                    dve.drain()
                    SM["zs"].wait(dve, c, 1)
                    SM["yz"].by(dve.tensor_tensor(wdt[:], y, zs[:], ALU.mult))
                    SM["res"].wait(dve, c, 1)
                    M.residual_ln(dve, c, "mo", x_res, 1, y_1)

                def cross_out_1(c):
                    SY["resid"].wait(dve, c, 1)
                    Y.residual_ln(dve, c, "ao", y_1, 1, y_2)

                def up(c, js):
                    for j in js:
                        SY["silu"].wait(dve, c, j + 1)
                        ps = two(ringy.filled(dve, c, f"b{j}"))
                        for i in range(MPB):
                            m = j * MPB + i
                            ins = dve.scalar_tensor_tensor(h0[:, m, :], ps[:, i, :], vb["v_s2"][:, m:m + 1], gate[:, j % 2, i, :],
                                                           op0=ALU.mult, op1=ALU.mult)
                        ringy.free(ins, f"b{j}")
                        SY["h0"].by(dve.drain())

                def mlp_out(c):
                    ps = two(ringy.filled(dve, c, "fo"))
                    ringy.free(dve.tensor_tensor(Y.r[:], ps, s5_row[:].unsqueeze(1).to_broadcast([P, TT, D]), ALU.mult), "fo")
                    dve.drain()
                    dve.tensor_tensor(Y.r[:], Y.r[:], y_2[:], ALU.add)
                    dve.drain()
                    dve.wait_ge(s_stored_b, c * 16 + 16)
                    Y.ln_dve(dve, c, 2, Y.r, y_3)

                c = NCH - 1
                first_stage_over(dve)
                dve.memset(halo[:], 0.0)
                dve.memset(h_carry[:], 0.0)
                dve.memset(xd_r[:], 0.0)
                dve.wait_ge(s_vec_b, n_vec_b)
                dve.wait_ge(s_exp_a, 1)
                dve.tensor_scalar(vb["v_alog"][:], vb["v_alog"][:], -1.0, None, op0=ALU.mult)
                dve.drain().then_inc(s_setup_b, 1)
                X.softmax_dve(dve, c)
                conv(0)
                split_bc(0)
                X.residual_ln(dve, c, "ao", x_1, 1, x_2)
                step_sizes(0)
                states(0, range(0, 1))
                route(c)
                states(0, range(1, 2))
                experts_in(c, range(0, 3))
                states(0, range(2, 3))
                experts_in(c, range(3, 6))
                states(0, range(3, 4))
                experts_in(c, range(6, 8))
                states(0, range(4, 5))
                experts_hidden(c)
                states(0, range(5, 7))
                experts_out(c)
                kv1.repeat_dve(dve)
                states(0, range(7, 9))
                kv1.make_dve(dve, 1)
                states(0, range(9, 12))
                kv1.make_dve(dve, 0)
                states(0, range(12, NST))
                scan_out(0)
                conv(1)
                dve.wait_ge(s_rows_b, 32)
                with dve.Fori(1, NCH) as it:
                    c = it - 1
                    split_bc(it)
                    Y.softmax_dve(dve, c)
                    step_sizes(it)
                    states(it, range(0, 1))
                    cross_out_1(c)
                    states(it, range(1, 3))
                    up(c, range(0, 2))
                    states(it, range(3, 4))
                    up(c, range(2, 4))
                    states(it, range(4, NST))
                    scan_out(it)
                    conv(it + 1)
                    mlp_out(c)
                c = NCH - 1
                Y.softmax_dve(dve, c)
                cross_out_1(c)
                up(c, range(NP))
                mlp_out(c)

            @block.scalar
            def _(act):
                act.wait_ge(s_vec_a, n_vec_a)
                act.activation(decay[:], va["v_decay"][:], ACT.Sigmoid).then_inc(s_decay, 1)
                S, ring, T, ringx = F.s, F.ring, X.s, X.ring

                def keys_gates(c, j):
                    if j >= 2:
                        S["kvd"].wait(act, c, j - 1)
                    for dst, name, func, bias in ((k_sb, "k", ACT.Identity, "v_bk"), (g_sb, "g", ACT.Sigmoid, "v_bg")):
                        ps = two(ring.filled(act, c, f"{name}{j}"))
                        for i in range(MPB):
                            m = j * MPB + i
                            ins = act.activation(dst[:, j % 2, i, :], ps[:, i, :], func, bias=va[bias][:, m:m + 1])
                        ring.free(ins, f"{name}{j}")
                    S["kg"].by(act.drain())

                def ffn_hidden(c, js=range(NP)):
                    for j in js:
                        ps = two(ring.filled(act, c, f"f{j}"))
                        for i in range(MPB):
                            m = j * MPB + i
                            ins = act.activation(hT[:, m, :], ps[:, i, :], ACT.Gelu, bias=va["v_b1"][:, m:m + 1])
                        ring.free(ins, f"f{j}")
                    if js[-1] == NP - 1:
                        S["gelu"].by(act.drain())

                def begin(c):
                    F.transpose_act(act, c, "xT1", va["v_ln1_g"], va["v_ln1_b"])

                def gate_score(c):
                    T["top"].wait(act, c, 1)
                    T["sig"].by(act.activation(sgm[:], top1[:], ACT.Sigmoid))

                def route_rows(c):
                    ps = ringx.filled(act, c, "rT")
                    ringx.free(act.activation(rT[:], ps[0:32 * PARTS, 0:CH], ACT.Copy), "rT")
                    T["rT"].by(act.drain())

                def route_spread(c):
                    for j in range(NE // 2):
                        ps = two(ringx.filled(act, c, f"rb{j}"))
                        ringx.free(act.activation(rB[:, 2 * j:2 * j + 2, :], ps, ACT.Copy), f"rb{j}")
                        T["rb"].by(act.drain())

                def experts_gate(c):
                    ps = two(ringx.filled(act, c, "gu"))
                    T["silu"].by(act.activation(sg[:], ps[:, 0, :], ACT.Silu))

                begin(0)
                kv0.k_act(act)
                for j in range(NP):
                    keys_gates(0, j)
                F.transpose_act(act, 0, "xT2", va["v_ln2_g"], va["v_ln2_b"])
                ffn_hidden(0)
                begin(1)
                with act.Fori(1, NCH) as it:
                    c = it - 1
                    keys_gates(it, 0)
                    X.transpose_act(act, c, "xTq")
                    keys_gates(it, 1)
                    X.query_act(act, c)
                    keys_gates(it, 2)
                    X.exp_act(act, c, 0, 0)
                    X.exp_act(act, c, 0, 1)
                    X.exp_act(act, c, 1, 0)
                    X.exp_act(act, c, 1, 1)
                    keys_gates(it, 3)
                    X.move_act(act, c, 0)
                    X.mixed_act(act, c, 0)
                    X.move_act(act, c, 1)
                    X.mixed_act(act, c, 1)
                    X.transpose_act(act, c, "xTe")
                    gate_score(c)
                    F.transpose_act(act, it, "xT2", va["v_ln2_g"], va["v_ln2_b"])
                    ffn_hidden(it, range(0, 2))
                    route_rows(c)
                    ffn_hidden(it, range(2, 3))
                    route_spread(c)
                    ffn_hidden(it, range(3, 4))
                    experts_gate(c)
                    begin(it + 1)

                SM, ringm, SY, ringy = M.s, M.ring, Y.s, Y.ring

                def keep_x(c, before=None):
                    act.wait_ge(s_xb, c * 16 + 16)
                    if before is not None:
                        SM["xn"].wait(act, before, 1)
                    SM["res"].by(act.activation(x_res[:], xb_in[:], ACT.Copy))
                    SM["x_in_free"].by(act.drain())

                def conv_in(c):
                    for j in range(KI // MPB):
                        ps = two(ringm.filled(act, c, f"x{j}"))
                        ringm.free(act.activation(xbuf[:, j * MPB:(j + 1) * MPB, TAPS - 1:], ps, ACT.Copy), f"x{j}")
                        SM["xb"].by(act.drain())

                def gates(c):
                    for j in range(KI // MPB):
                        ps = two(ringm.filled(act, c, f"z{j}"))
                        ringm.free(act.activation(zs[:, j * MPB:(j + 1) * MPB, :], ps, ACT.Silu), f"z{j}")
                    SM["zs"].by(act.drain())

                def conv_out(c):
                    for j in range(KI // MPB):
                        SM["conv"].wait(act, c, j + 1)
                        m = slice(j * MPB, (j + 1) * MPB)
                        SM["u"].by(act.activation(u[:, m, :], wdt[:, m, :], ACT.Silu))

                def steps_in(c):
                    for j in range(KI // MPB):
                        ps = two(ringm.filled(act, c, f"dt{j}"))
                        for i in range(MPB):
                            m = j * MPB + i
                            ins = act.activation(dt[:, m, :], ps[:, i, :], ACT.Identity, bias=vb["v_dtb"][:, m:m + 1])
                        ringm.free(ins, f"dt{j}")
                    act.drain()
                    act.activation(hb[:, 0], dt[:], ACT.Abs)
                    act.drain()
                    act.activation(hb[:, 0], hb[:, 0], ACT.Exp, scale=-1.0)

                def steps_out(c):
                    act.drain()
                    SM["soft"].by(act.activation(hb[:, 0], hb[:, 0], ACT.Ln, bias=1.0))
                    SM["dt"].wait(act, c, 1)

                def decays(c, ns):
                    for n in ns:
                        if n % 2:
                            if n == 1:
                                SM["wdt"].wait(act, c, 1)
                                SM["y0"].wait(act, c, 1)
                            if n // 2 >= KI:
                                SM["dtuB"].wait(act, c, n // 2 + 1 - KI)
                            ps = two(ringm.filled(act, c, f"bc{n}"))
                            SM["B"].by(act.activation(u[:, n // 2 % KI, :], ps[:, 0, :], ACT.Copy))
                        if n >= 2:
                            SM["scanned"].wait(act, c, n - 1)
                        for j in range(KI):
                            ins = act.activation(dA[:, n % 2, j, :], dt[:, j, :], ACT.Exp,
                                                 scale=vb["v_alog"][:, j * NST + n:j * NST + n + 1])
                        SM["dA"].by(ins)

                def mlp_gate(c, js):
                    for j in js:
                        if j >= 2:
                            SY["h0"].wait(act, c, j - 1)
                        ps = two(ringy.filled(act, c, f"a{j}"))
                        for i in range(MPB):
                            m = j * MPB + i
                            ins = act.activation(gate[:, j % 2, i, :], ps[:, i, :], ACT.Silu, scale=vb["v_s1"][:, m:m + 1])
                        ringy.free(ins, f"a{j}")
                        SY["silu"].by(act.drain())

                def scale_in(c, name, dst, scale, j):
                    ps = two(ringy.filled(act, c, f"{name}{j}"))
                    for i in range(MPB):
                        m = j * MPB + i
                        ins = act.activation(dst[:, m, :], ps[:, i, :], ACT.Copy, scale=vb[scale][:, m:m + 1])
                    ringy.free(ins, f"{name}{j}")

                def gelus(c, name, h, scale):
                    act.drain()
                    SY["gelu"].by(act.activation(h[:, 0:KH - MPB, :], h[:, 0:KH - MPB, :], ACT.Gelu))
                    j = NP - 1
                    ps = two(ringy.filled(act, c, f"{name}{j}"))
                    for i in range(MPB):
                        m = j * MPB + i
                        ins = act.activation(h[:, m, :], ps[:, i, :], ACT.Gelu, scale=vb[scale][:, m:m + 1])
                    ringy.free(ins, f"{name}{j}")
                    SY["gelu"].by(act.drain())

                c = NCH - 1
                act.wait_ge(s_vec_b, n_vec_b)
                act.activation(vb["v_alog"][:], vb["v_alog"][:], ACT.Exp).then_inc(s_exp_a, 1)
                X.transpose_act(act, c, "xTq")
                first_stage_over(act)
                X.query_act(act, c)
                X.exp_act(act, c, 0, 0)
                M.transpose_act(act, 0, "xT")
                X.exp_act(act, c, 0, 1)
                keep_x(0)
                X.exp_act(act, c, 1, 0)
                conv_in(0)
                X.exp_act(act, c, 1, 1)
                X.move_act(act, c, 0)
                X.mixed_act(act, c, 0)
                X.move_act(act, c, 1)
                conv_out(0)
                X.mixed_act(act, c, 1)
                steps_in(0)
                steps_out(0)
                act.wait_ge(s_setup_b, 1)
                decays(0, range(0, 1))
                X.transpose_act(act, c, "xTe")
                gate_score(c)
                decays(0, range(1, 2))
                gates(0)
                route_rows(c)
                route_spread(c)
                decays(0, range(2, 4))
                experts_gate(c)
                decays(0, range(4, 8))
                kv1.k_act(act)
                decays(0, range(8, NST))
                M.transpose_act(act, 1, "xT")
                conv_in(1)
                keep_x(1, 0)
                with act.Fori(1, NCH) as it:
                    c = it - 1
                    conv_out(it)
                    Y.transpose_act(act, c, "xTq")
                    Y.query_act(act, c, vb["v_bqkv"][:, 0:KD])
                    Y.exp_act(act, c, 0, 0)
                    Y.exp_act(act, c, 0, 1)
                    steps_in(it)
                    Y.exp_act(act, c, 1, 0)
                    Y.exp_act(act, c, 1, 1)
                    Y.move_act(act, c, 0)
                    steps_out(it)
                    Y.mixed_act(act, c, 0, vb["v_bqkv"][:, 2 * KD:3 * KD])
                    Y.move_act(act, c, 1)
                    decays(it, range(0, 2))
                    Y.mixed_act(act, c, 1, vb["v_bqkv"][:, 2 * KD:3 * KD])
                    decays(it, range(2, 3))
                    Y.transpose_act(act, c, "xT2")
                    gates(it)
                    mlp_gate(c, range(0, 2))
                    decays(it, range(3, 4))
                    mlp_gate(c, range(2, 4))
                    decays(it, range(4, 6))
                    for j in range(NP - 1):
                        scale_in(c, "c", h1, "v_s3", j)
                        decays(it, PACE[0][j])
                    gelus(c, "c", h1, "v_s3")
                    decays(it, PACE[0][-1])
                    for j in range(NP - 1):
                        scale_in(c, "d", h0, "v_s4", j)
                        decays(it, PACE[1][j])
                    gelus(c, "d", h0, "v_s4")
                    M.transpose_act(act, it + 1, "xT")
                    conv_in(it + 1)
                    keep_x(it + 1, it)
                c = NCH - 1
                Y.transpose_act(act, c, "xTq")
                Y.query_act(act, c, vb["v_bqkv"][:, 0:KD])
                for i in range(TT):
                    Y.exp_act(act, c, i, 0)
                    Y.exp_act(act, c, i, 1)
                for i in range(TT):
                    Y.move_act(act, c, i)
                    Y.mixed_act(act, c, i, vb["v_bqkv"][:, 2 * KD:3 * KD])
                Y.transpose_act(act, c, "xT2")
                mlp_gate(c, range(NP))
                for j in range(NP - 1):
                    scale_in(c, "c", h1, "v_s3", j)
                gelus(c, "c", h1, "v_s3")
                for j in range(NP - 1):
                    scale_in(c, "d", h0, "v_s4", j)
                gelus(c, "d", h0, "v_s4")

            @block.tensor
            def _(pe):
                pe.wait_ge(s_const, 1)
                S, ring, T, ringx = F.s, F.ring, X.s, X.ring
                ring.start(pe)

                def begin(c):
                    S["in_xn"].wait(pe, c, 1)
                    F.transpose_pe(pe, c, "xT1", x_n)

                def qkvg(c, j, fresh=False, which="kgvq"):
                    if j == 0:
                        S["xT"].wait(pe, c, 1)
                    for n in which:
                        if fresh and j == 0:
                            pe.wait_ge(s_w["a_W" + n], 16)
                        F.product(pe, c, f"{n}{j}", wa["a_W" + n], j, F.xT, KD)

                def attention_out(c):
                    S["oT"].wait(pe, c, NP)
                    F.product_tok(pe, c, "ao", hT, wa["a_Wo"], KH)

                def ffn_begin(c):
                    S["xn"].wait(pe, c, 1)
                    F.transpose_pe(pe, c, "xT2", x_bo)

                def ffn_in(c, js=range(NP)):
                    S["xT"].wait(pe, c, 2)
                    for j in js:
                        F.product(pe, c, f"f{j}", wa["a_W1"], j, F.xT, KD)

                def ffn_out(c):
                    S["gelu"].wait(pe, c, 1)
                    F.product_tok(pe, c, "fo", hT, wa["a_W2"], KH)

                def cross_begin(c):
                    S["xn"].wait(pe, c, 2)
                    X.transpose_pe(pe, c, "xTq", x_1)

                def query(c):
                    T["xT"].wait(pe, c, 1)
                    X.product(pe, c, "xq", wa["x0_Wq"], 0, X.xT, KD)

                def cross_out(c):
                    T["oaT"].wait(pe, c, 1)
                    X.product_tok(pe, c, "ao", X.oaT, wa["x0_Wo"], KD)

                def experts_begin(c):
                    T["xn"].wait(pe, c, 1)
                    X.transpose_pe(pe, c, "xTe", x_2)

                def logits(c):
                    T["xT"].wait(pe, c, 2)
                    ps = ringx.acquire(pe, c, "lg")
                    for i in range(TT):
                        for k in range(KD):
                            last = pe.matmul(ps[:, i * NE:(i + 1) * NE], X.xT[:, k, i * P:(i + 1) * P], wa["e_gate"][:, k, :],
                                             start=k == 0, stop=k == KD - 1)
                    ringx.full.by(last)

                def route_rows(c):
                    T["route"].wait(pe, c, 1)
                    ps = ringx.acquire(pe, c, "rT")
                    for i in range(TT):
                        last = pe.transpose(ps[0:32 * PARTS, i * P:(i + 1) * P], rw[:, i, :], ident[:])
                    ringx.full.by(last)

                def route_spread(c):
                    T["rT"].wait(pe, c, 1)
                    for j in range(NE // 2):
                        ps = two(ringx.acquire(pe, c, f"rb{j}"))
                        for i in range(2):
                            e = 2 * j + i
                            last = pe.matmul(ps[:, i, :], sel8[0:32 * PARTS, e:e + 1].to_broadcast([32 * PARTS, P]), rT[:],
                                             start=True, stop=True)
                        ringx.full.by(last)

                def experts_in(c, part):
                    ps = two(ringx.acquire(pe, c, "gu"))
                    for e in part:
                        T["xm"].wait(pe, c, e + 1)
                        for half, wt in ((0, wa["e_Wg"]), (1, wa["e_Wu"])):
                            for k in range(KD):
                                last = pe.matmul(ps[:, half, :], wt[:, k, e * P:(e + 1) * P], xm[:, e % XM, k, :],
                                                 start=e == 0 and k == 0 and half == 0, stop=e == NE - 1 and k == KD - 1,
                                                 skip_group_check=True)
                        if e < NE - 1:
                            T["xmu"].by(last)
                        else:
                            ringx.full.by(last)

                def experts_out(c):
                    T["he"].wait(pe, c, NE)
                    X.product_tok(pe, c, "ed", he, wa["e_Wd"], NE)

                begin(0)
                kv0.k_pe(pe)
                kv0.v_pe(pe, 1)
                for j in range(NP):
                    qkvg(0, j, True)
                for n in ORDER_A[6:]:
                    pe.wait_ge(s_w[n], 16)
                attention_out(0)
                ffn_begin(0)
                ffn_in(0)
                kv0.v_pe(pe, 0)
                ffn_out(0)
                begin(1)
                pe.wait_ge(s_setup, 1)
                kv0.done_pe(pe)
                ringx.start(pe)
                with pe.Fori(1, NCH) as it:
                    c = it - 1
                    qkvg(it, 0)
                    cross_begin(c)
                    qkvg(it, 1)
                    query(c)
                    qkvg(it, 2, which="kg")
                    pe.wait_ge(s_kv, c * 32 + 32)
                    T["qT"].wait(pe, c, 1)
                    X.scores_pe(pe, c, 0)
                    X.scores_pe(pe, c, 1)
                    qkvg(it, 2, which="vq")
                    qkvg(it, 3, which="kg")
                    X.turn_pe(pe, c, 0)
                    qkvg(it, 3, which="v")
                    X.mix_pe(pe, c, 0)
                    X.turn_pe(pe, c, 1)
                    qkvg(it, 3, which="q")
                    X.mix_pe(pe, c, 1)
                    cross_out(c)
                    attention_out(it)
                    experts_begin(c)
                    logits(c)
                    ffn_begin(it)
                    ffn_in(it, range(0, 2))
                    route_rows(c)
                    ffn_in(it, range(2, 3))
                    route_spread(c)
                    ffn_in(it, range(3, 4))
                    experts_in(c, range(NE))
                    ffn_out(it)
                    begin(it + 1)
                    experts_out(c)

                SM, ringm, SY, ringy = M.s, M.ring, Y.s, Y.ring

                def scan_begin(c):
                    pe.wait_ge(s_xb, c * 16 + 16)
                    M.transpose_pe(pe, c, "xT", xb_in)

                def inner(c, name, first_pair, js=range(KI // MPB)):
                    SM["xT"].wait(pe, c, 1)
                    for j in js:
                        ps = ringm.acquire(pe, c, f"{name}{j}")
                        for i in range(MPB):
                            m = (first_pair + j) * MPB + i
                            for k in range(KD):
                                last = pe.matmul(ps[:, i * CH:(i + 1) * CH], wb["m_in"][:, k, m * P:(m + 1) * P], M.xT[:, k, :],
                                                 start=k == 0, stop=k == KD - 1)
                        ringm.full.by(last)

                def x_proj(c):
                    ps = ringm.acquire(pe, c, "xd")
                    for k in range(KI):
                        if k % MPB == 0:
                            SM["u"].wait(pe, c, k // MPB + 1)
                        last = pe.matmul(ps[:, 0:CH], wb["m_xp"][:, k, :], u[:, k, :], start=k == 0, stop=k == KI - 1)
                    ringm.full.by(last)

                def dt_proj(c):
                    SM["xd"].wait(pe, c, 1)
                    for j in range(KI // MPB):
                        ps = ringm.acquire(pe, c, f"dt{j}")
                        for i in range(MPB):
                            m = j * MPB + i
                            last = pe.matmul(ps[:, i * CH:(i + 1) * CH], dtw[:, m * P:(m + 1) * P], dtr, start=True, stop=True)
                        ringm.full.by(last)

                def spread(c, ns):
                    for n in ns:
                        ps = ringm.acquire(pe, c, f"bc{n}")
                        for i in range(2):
                            col = sel_bc[:, i * NST + n:i * NST + n + 1]
                            last = pe.matmul(ps[:, i * CH:(i + 1) * CH], col.to_broadcast([P, P]), xd_r[:], start=True, stop=True)
                        ringm.full.by(last)

                def scan_out(c):
                    SM["yz"].wait(pe, c, 1)
                    M.product_tok(pe, c, "mo", wdt, wb["m_out"], KI)

                def cross_begin_1(c):
                    SM["xn"].wait(pe, c, 1)
                    Y.transpose_pe(pe, c, "xTq", y_1)

                def query_1(c):
                    SY["xT"].wait(pe, c, 1)
                    Y.product(pe, c, "xq", wb["x1_Wqkv"], 0, Y.xT, KD)

                def keys_wait(c):
                    SY["qT"].wait(pe, c, 1)
                    pe.wait_ge(s_kv_b, c * 32 + 32)

                def cross_out_1(c):
                    SY["oaT"].wait(pe, c, 1)
                    pe.wait_ge(s_wb["x1_Wo"], 16)
                    Y.product_tok(pe, c, "ao", Y.oaT, wb["x1_Wo"], KD)

                def mlp_begin(c):
                    SY["xn"].wait(pe, c, 1)
                    Y.transpose_pe(pe, c, "xT2", y_2)
                    pe.wait_ge(s_wb["f_w1"], 16)
                    pe.wait_ge(s_wb["f_w2"], 16)
                    SY["xT"].wait(pe, c, 2)

                def gate_up(c, js):
                    for j in js:
                        Y.product(pe, c, f"a{j}", wb["f_w1"], j, Y.xT, KD)
                        Y.product(pe, c, f"b{j}", wb["f_w2"], j, Y.xT, KD)

                def hidden2(c, j):
                    ps = ringy.acquire(pe, c, f"d{j}")
                    if j == 0:
                        pe.wait_ge(s_wb["f_h2"], 16)
                        SY["gelu"].wait(pe, c, 1)
                    for i in range(MPB):
                        m = j * MPB + i
                        for k in range(KH):
                            if m == 0 and k == KH - MPB:
                                SY["gelu"].wait(pe, c, 2)
                            last = pe.matmul(ps[:, i * CH:(i + 1) * CH], wb["f_h2"][:, k, m * P:(m + 1) * P], h1[:, k, :],
                                             start=k == 0, stop=k == KH - 1)
                    ringy.full.by(last)

                def mlp_out(c):
                    pe.wait_ge(s_wb["f_w3"], 16)
                    SY["gelu"].wait(pe, c, 3)
                    Y.product_tok(pe, c, "fo", h0, wb["f_w3"], KH, (KH - MPB, lambda: SY["gelu"].wait(pe, c, 4)))

                c = NCH - 1
                cross_begin(c)
                query(c)
                first_stage_over(pe)
                ringm.start(pe)
                T["qT"].wait(pe, c, 1)
                pe.wait_ge(s_kv, c * 32 + 32)
                X.scores_pe(pe, c, 0)
                scan_begin(0)
                X.scores_pe(pe, c, 1)
                pe.wait_ge(s_wb["m_in"], 16)
                inner(0, "x", 0)
                for i in range(TT):
                    X.turn_pe(pe, c, i)
                    X.mix_pe(pe, c, i)
                pe.wait_ge(s_wb["m_xp"], 16)
                x_proj(0)
                cross_out(c)
                pe.wait_ge(s_vec_b, n_vec_b)
                dt_proj(0)
                spread(0, range(2))
                experts_begin(c)
                logits(c)
                inner(0, "z", KI // MPB)
                route_rows(c)
                route_spread(c)
                spread(0, range(2, 4))
                experts_in(c, range(NE))
                spread(0, range(4, 8))
                experts_out(c)
                spread(0, range(8, 9))
                T["xn"].wait(pe, c, 2)
                kv1.k_pe(pe)
                spread(0, range(9, 10))
                kv1.v_pe(pe, 1)
                spread(0, range(10, 13))
                kv1.v_pe(pe, 0)
                spread(0, range(13, NST))
                pe.wait_ge(s_wb["m_out"], 16)
                scan_out(0)
                scan_begin(1)
                inner(1, "x", 0)
                kv1.done_pe(pe)
                ringy.start(pe)
                with pe.Fori(1, NCH) as it:
                    c = it - 1
                    cross_begin_1(c)
                    x_proj(it)
                    query_1(c)
                    keys_wait(c)
                    Y.scores_pe(pe, c, 0)
                    dt_proj(it)
                    Y.scores_pe(pe, c, 1)
                    spread(it, range(0, 2))
                    Y.turn_pe(pe, c, 0)
                    inner(it, "z", KI // MPB, [0])
                    Y.mix_pe(pe, c, 0)
                    Y.turn_pe(pe, c, 1)
                    Y.mix_pe(pe, c, 1)
                    cross_out_1(c)
                    inner(it, "z", KI // MPB, [1])
                    spread(it, range(2, 3))
                    mlp_begin(c)
                    gate_up(c, range(0, 2))
                    spread(it, range(3, 4))
                    gate_up(c, range(2, 4))
                    spread(it, range(4, 6))
                    pe.wait_ge(s_wb["f_h1"], 16)
                    SY["h0"].wait(pe, c, NP - 1)
                    for j in range(NP):
                        Y.product(pe, c, f"c{j}", wb["f_h1"], j, h0, KH, (KH - MPB, lambda: SY["h0"].wait(pe, c, NP)) if j == 0 else None)
                        spread(it, PACE[0][j])
                    for j in range(NP):
                        hidden2(c, j)
                        spread(it, PACE[1][j])
                    scan_out(it)
                    scan_begin(it + 1)
                    inner(it + 1, "x", 0)
                    mlp_out(c)
                c = NCH - 1
                cross_begin_1(c)
                query_1(c)
                keys_wait(c)
                for i in range(TT):
                    Y.scores_pe(pe, c, i)
                for i in range(TT):
                    Y.turn_pe(pe, c, i)
                    Y.mix_pe(pe, c, i)
                cross_out_1(c)
                mlp_begin(c)
                gate_up(c, range(NP))
                SY["h0"].wait(pe, c, NP - 1)
                for j in range(NP):
                    Y.product(pe, c, f"c{j}", wb["f_h1"], j, h0, KH, (KH - MPB, lambda: SY["h0"].wait(pe, c, NP)) if j == 0 else None)
                for j in range(NP):
                    hidden2(c, j)
                mlp_out(c)
        F.check(in_var=1, in_rstd=1, in_xn=1, xT=1, x_in_free=1, full=1, act=1)
        X.check()
        M.check(xT=1, full=3, act=3, xb=2, res=1, x_in_free=1, conv=2)
        Y.check()


def kernel(x, ctx_1024, L0_attn_ln1_g, L0_attn_ln1_b, L0_attn_Wq, L0_attn_bq, L0_attn_Wk, L0_attn_bk, L0_attn_Wv,
           L0_attn_bv, L0_attn_Wg, L0_attn_bg, L0_attn_decay_logit, L0_attn_Wo, L0_attn_bo, L0_attn_ln2_g,
           L0_attn_ln2_b, L0_attn_W1, L0_attn_b1, L0_attn_W2, L0_attn_b2, L0_xattn_Wq, L0_xattn_Wk, L0_xattn_Wv,
           L0_xattn_Wo, L0_ffn_gate_w, L0_ffn_w_gate, L0_ffn_w_up, L0_ffn_w_down, L1_attn_in_proj_w, L1_attn_conv_w,
           L1_attn_conv_b, L1_attn_x_proj_w, L1_attn_dt_proj_w, L1_attn_dt_proj_b, L1_attn_A_log, L1_attn_D_param,
           L1_attn_out_proj_w, L1_xattn_W_qkv, L1_xattn_b_qkv, L1_xattn_W_out, L1_xattn_b_out, L1_ffn_w1_w, L1_ffn_w1_s,
           L1_ffn_w2_w, L1_ffn_w2_s, L1_ffn_h1_w, L1_ffn_h1_s, L1_ffn_h2_w, L1_ffn_h2_s, L1_ffn_w3_w, L1_ffn_w3_s):
    import numpy as np
    from concourse import bacc
    from concourse.bass_utils import run_bass_kernel_spmd

    def rows(w):
        w = np.asarray(w)
        return np.ascontiguousarray(w.reshape(-1, P, w.shape[1]).transpose(1, 0, 2).reshape(P, -1))

    def vec(v):
        return np.ascontiguousarray(np.asarray(v).reshape(-1, P).T)

    def flat(w):
        w = np.asarray(w)
        return w.reshape(-1, w.shape[2])

    xp = np.asarray(L1_attn_x_proj_w)
    gap = np.zeros((32 - DTR, INNER), np.float32)
    bc = xp[DTR:]
    a = {
        "x": np.asarray(x),
        "ctxT": np.ascontiguousarray(np.asarray(ctx_1024).reshape(BATCH, KEYS, KD, P).transpose(3, 2, 0, 1).reshape(P, -1)),
        "a_Wq": rows(L0_attn_Wq), "a_Wk": rows(L0_attn_Wk), "a_Wv": rows(L0_attn_Wv), "a_Wg": rows(L0_attn_Wg),
        "a_Wo": rows(L0_attn_Wo), "a_W1": rows(L0_attn_W1), "a_W2": rows(L0_attn_W2),
        "x0_Wq": rows(np.asarray(L0_xattn_Wq).T), "x0_Wk": rows(np.asarray(L0_xattn_Wk).T),
        "x0_Wv": rows(np.asarray(L0_xattn_Wv).T), "x0_Wo": rows(np.asarray(L0_xattn_Wo).T),
        "e_gate": rows(np.asarray(L0_ffn_gate_w).T), "e_Wg": rows(flat(L0_ffn_w_gate).T),
        "e_Wu": rows(flat(L0_ffn_w_up).T), "e_Wd": rows(flat(np.asarray(L0_ffn_w_down).transpose(0, 2, 1))),
        "v_ln1_g": vec(L0_attn_ln1_g), "v_ln1_b": vec(L0_attn_ln1_b), "v_bq": vec(L0_attn_bq), "v_bk": vec(L0_attn_bk),
        "v_bv": vec(L0_attn_bv), "v_bg": vec(L0_attn_bg),
        "v_decay": vec(np.repeat(np.asarray(L0_attn_decay_logit), HID // HEADS)),
        "v_ln2_g": vec(L0_attn_ln2_g), "v_ln2_b": vec(L0_attn_ln2_b), "v_b1": vec(L0_attn_b1),
        "r_bo": np.asarray(L0_attn_bo), "r_b2": np.asarray(L0_attn_b2),
        "m_in": rows(np.asarray(L1_attn_in_proj_w).T), "m_xp": rows(np.concatenate([xp[:DTR], gap] + [bc] * PARTS).T),
        "m_dtw": np.ascontiguousarray(np.asarray(L1_attn_dt_proj_w).T), "m_out": rows(np.asarray(L1_attn_out_proj_w).T),
        "v_convw": rows(np.asarray(L1_attn_conv_w)[:, 0, :]), "v_convb": vec(L1_attn_conv_b), "v_dtb": vec(L1_attn_dt_proj_b),
        "v_alog": rows(L1_attn_A_log), "v_D": vec(L1_attn_D_param),
        "x1_Wqkv": rows(L1_xattn_W_qkv), "v_bqkv": vec(L1_xattn_b_qkv), "x1_Wo": rows(L1_xattn_W_out),
        "r_bout": np.asarray(L1_xattn_b_out),
        "f_w1": rows(np.asarray(L1_ffn_w1_w).T), "f_w2": rows(np.asarray(L1_ffn_w2_w).T), "f_h1": rows(np.asarray(L1_ffn_h1_w).T),
        "f_h2": rows(np.asarray(L1_ffn_h2_w).T), "f_w3": rows(np.asarray(L1_ffn_w3_w).T),
        "v_s1": vec(L1_ffn_w1_s), "v_s2": vec(L1_ffn_w2_s), "v_s3": vec(L1_ffn_h1_s), "v_s4": vec(L1_ffn_h2_s),
        "r_s5": np.asarray(L1_ffn_w3_s),
    }
    nc = bacc.Bacc("TRN2", target_bir_lowering=False, num_devices=1)
    t = {n: nc.dram_tensor("in_" + n, v.shape, F32, kind="ExternalInput").ap() for n, v in a.items()}
    mid = nc.dram_tensor("mid", (TOK, D), F32, kind="Internal").ap()
    kz_dram = nc.dram_tensor("kz_dram", (BATCH, P, KD * ROWS), F32, kind="Internal").ap()
    vz_dram = nc.dram_tensor("vz_dram", (BATCH, P, KD * 5 * P), F32, kind="Internal").ap()
    out = nc.dram_tensor("out", (BATCH, SEQ, D), F32, kind="ExternalOutput").ap()
    decoder(nc, t, mid, kz_dram, vz_dram, out)
    r = run_bass_kernel_spmd(nc, [{"in_" + n: v for n, v in a.items()}], core_ids=[0])
    return r.results[0]["out"]
```
